# Optimizing a Trainium2 kernel written in Bass

```python
import numpy as np
import jax
import jax.numpy as jnp

def _softmax(x, axis=-1):
    return jax.nn.softmax(x, axis=axis)

def _gelu(x):
    return jax.nn.gelu(x, approximate=True)

def _silu(x):
    return jax.nn.silu(x)

def _sigmoid(x):
    return jax.nn.sigmoid(x)

def _layernorm(x, axis=-1, eps=1e-05):
    m = jnp.mean(x, axis=axis, keepdims=True)
    v = jnp.var(x, axis=axis, keepdims=True)
    return (x - m) / jnp.sqrt(v + eps)

def _scatter_add(tgt, idx, src, axis=0):
    return tgt.at[idx].add(src)

def _segment_sum(src, seg, n):
    return jax.ops.segment_sum(src, seg, n)
kernel_name = 'mk_xattn_ffn_d4_seqx_r8_a8e6a6'

def setup_inputs(seed: int=0):
    np.random.seed(seed)
    _w = jnp.asarray

    def _rec_inputs():
        import jax
        import jax.numpy as jnp
        _rk = jax.random.key(seed)
        x = 0.0002417 + 0.9998 * jax.random.normal(jax.random.fold_in(_rk, 1), (4, 512, 128), jnp.float32)
        _lenS = 512 - jax.random.randint(jax.random.fold_in(_rk, 7), (4,), 0, max(1, 512 // 4) + 1, jnp.int32)
        _lenS2 = 77 - jax.random.randint(jax.random.fold_in(_rk, 8), (4,), 0, max(1, 77 // 4) + 1, jnp.int32)
        _ctx_1024P = jax.random.normal(jax.random.fold_in(_rk, 11), (4, 16, 128), jnp.float32)
        _ctx_1024c = jax.random.dirichlet(jax.random.fold_in(_rk, 511), 0.3 * jnp.ones((16,), jnp.float32), (4, 77))
        _ctx_1024t = jnp.einsum('bsk,bkd->bsd', _ctx_1024c, _ctx_1024P)
        _ctx_1024t = _ctx_1024t * jax.lax.rsqrt(jnp.mean(jnp.square(_ctx_1024t)) + 1e-12) * 0.953939
        ctx_1024 = 7.22013e-05 + 1.00017 * (_ctx_1024t + 0.3 * jax.random.normal(jax.random.fold_in(_rk, 611), (4, 77, 128), jnp.float32))
        _validS = jnp.arange(512)[None, :] < _lenS[:, None]
        _validS2 = jnp.arange(77)[None, :] < _lenS2[:, None]
        _causal = jnp.tril(jnp.ones((512, 512), dtype=bool))
        mask_1xSxS2_ff0 = jnp.where(jnp.ones((1, 512, 77), dtype=bool), 0.0, -1000000000.0).astype(jnp.float32)
        mask_BxSxS2_bk0 = jnp.logical_not(jnp.broadcast_to(_validS2[:, None, :], (4, 512, 77)))
        return (x, ctx_1024, mask_1xSxS2_ff0, mask_BxSxS2_bk0)
    x, ctx_1024, mask_1xSxS2_ff0, mask_BxSxS2_bk0 = _rec_inputs()

    def _L0_xattn_setup():
        import jax, jax.numpy as jnp
        import numpy as np
        EMBED = 128
        HEADS = 16
        HEAD_DIM = EMBED // HEADS
        EXP_DIM = 2 * HEAD_DIM

        def _feature_map(x, fm_w, fm_b):
            z = jnp.einsum('nshd,ed->nshe', x, fm_w) + fm_b
            return jnp.concatenate([jnp.exp(z), jnp.exp(-z)], axis=-1)
        key = jax.random.key(seed)
        ks = jax.random.split(key, 7)
        N, S = (4, 256)
        values = jax.random.normal(ks[0], (N, S, EMBED), dtype=jnp.float32)
        keys_ = jax.random.normal(ks[1], (N, S, EMBED), dtype=jnp.float32)
        query = jax.random.normal(ks[2], (N, S, EMBED), dtype=jnp.float32)
        fm_w = jnp.eye(HEAD_DIM, dtype=jnp.float32) + 0.02 * jax.random.normal(ks[3], (HEAD_DIM, HEAD_DIM), dtype=jnp.float32)
        fm_b = 0.02 * jax.random.normal(ks[4], (HEAD_DIM,), dtype=jnp.float32)
        fc_w = jax.random.normal(ks[5], (EMBED, HEADS * EXP_DIM), dtype=jnp.float32) * (1.0 / np.sqrt(HEADS * EXP_DIM))
        fc_b = jnp.zeros((EMBED,), dtype=jnp.float32)
        return {'values': values, 'keys': keys_, 'query': query, 'fm_w': fm_w, 'fm_b': fm_b, 'fc_w': fc_w, 'fc_b': fc_b}
    _L0_xattn_all = _L0_xattn_setup()
    _L0_xattn_in = {k: v for k, v in _L0_xattn_all.items() if k in ('fm_w', 'fm_b', 'fc_w', 'fc_b')}
    del _L0_xattn_all

    def _L0_ffn_setup():
        import jax, jax.numpy as jnp
        import numpy as np
        D_MODEL, FF_DIM = (128, 256)
        N_SHARED, N_ROUTED, TOP_K = (1, 8, 2)
        BATCH, SEQ = (2, 256)
        key = jax.random.key(seed)
        ks = jax.random.split(key, 8)
        init = lambda k, shape: jax.random.normal(k, shape, jnp.float32) * 0.02
        x = jax.random.normal(ks[0], (BATCH, SEQ, D_MODEL), jnp.float32)
        Wg = init(ks[1], (D_MODEL, N_ROUTED))
        Ws1 = init(ks[2], (D_MODEL, FF_DIM))
        Ws3 = init(ks[3], (D_MODEL, FF_DIM))
        Ws2 = init(ks[4], (FF_DIM, D_MODEL))
        We1 = init(ks[5], (N_ROUTED, D_MODEL, FF_DIM))
        We3 = init(ks[6], (N_ROUTED, D_MODEL, FF_DIM))
        We2 = init(ks[7], (N_ROUTED, FF_DIM, D_MODEL))
        return {'x': x, 'Wg': Wg, 'Ws1': Ws1, 'Ws3': Ws3, 'Ws2': Ws2, 'We1': We1, 'We3': We3, 'We2': We2}
    _L0_ffn_all = _L0_ffn_setup()
    _L0_ffn_in = {k: v for k, v in _L0_ffn_all.items() if k in ('Wg', 'Ws1', 'Ws3', 'Ws2', 'We1', 'We3', 'We2')}
    del _L0_ffn_all

    def _L1_xattn_setup():
        import jax, jax.numpy as jnp
        import numpy as np
        HIDDEN = 128
        HEADS = 16
        D_K = HIDDEN // HEADS
        B, S = (2, 256)
        key = jax.random.key(seed)
        ks = jax.random.split(key, 11)
        sc = 1.0 / np.sqrt(HIDDEN)
        inp = {'q': jax.random.normal(ks[0], (B, S, HIDDEN), jnp.float32), 'k': jax.random.normal(ks[1], (B, S, HIDDEN), jnp.float32), 'v': jax.random.normal(ks[2], (B, S, HIDDEN), jnp.float32), 'Wq': jax.random.normal(ks[3], (HIDDEN, HIDDEN), jnp.float32) * sc, 'bq': jnp.zeros((HIDDEN,), jnp.float32), 'Wk': jax.random.normal(ks[4], (HIDDEN, HIDDEN), jnp.float32) * sc, 'bk': jnp.zeros((HIDDEN,), jnp.float32), 'Wv': jax.random.normal(ks[5], (HIDDEN, HIDDEN), jnp.float32) * sc, 'bv': jnp.zeros((HIDDEN,), jnp.float32), 'Wo': jax.random.normal(ks[6], (HIDDEN, HIDDEN), jnp.float32) * sc, 'bo': jnp.zeros((HIDDEN,), jnp.float32)}
        return inp
    _L1_xattn_all = _L1_xattn_setup()
    _L1_xattn_in = {k: v for k, v in _L1_xattn_all.items() if k in ('Wq', 'bq', 'Wk', 'bk', 'Wv', 'bv', 'Wo', 'bo')}
    del _L1_xattn_all

    def _L1_ffn_setup():
        import math
        import jax, jax.numpy as jnp
        import numpy as np
        B, L, D, F_FF, E = (4, 256, 128, 512, 8)
        TOP_K = 1
        CAPACITY_FACTOR = 1.25
        key = jax.random.key(seed)
        ks = jax.random.split(key, 4)
        h = jax.random.normal(ks[0], (B, L, D), dtype=jnp.float32)
        gate_w = jax.random.normal(ks[1], (E, D), dtype=jnp.float32) * 0.02
        gate_b = jnp.zeros((E,), dtype=jnp.float32)
        w1 = jax.random.normal(ks[2], (E, D, F_FF), dtype=jnp.float32) * 0.02
        b1 = jnp.zeros((E, F_FF), dtype=jnp.float32)
        w2 = jax.random.normal(ks[3], (E, F_FF, D), dtype=jnp.float32) * 0.02
        b2 = jnp.zeros((E, D), dtype=jnp.float32)
        return {'h': h, 'gate_w': gate_w, 'gate_b': gate_b, 'w1': w1, 'b1': b1, 'w2': w2, 'b2': b2}
    _L1_ffn_all = _L1_ffn_setup()
    _L1_ffn_in = {k: v for k, v in _L1_ffn_all.items() if k in ('gate_w', 'gate_b', 'w1', 'b1', 'w2', 'b2')}
    del _L1_ffn_all

    def _L2_xattn_setup():
        import jax, jax.numpy as jnp
        import numpy as np
        B, S, D_IN, D_MODEL = (4, 256, 128, 128)
        key = jax.random.key(seed)
        ks = jax.random.split(key, 8)
        glorot = np.sqrt(6.0 / (D_IN + D_MODEL))
        inp = {'q': jax.random.normal(ks[0], (B, S, D_IN), dtype=jnp.float32), 'k': jax.random.normal(ks[1], (B, S, D_IN), dtype=jnp.float32), 'v': jax.random.normal(ks[2], (B, S, D_IN), dtype=jnp.float32), 'mask': jnp.zeros((1, S, S), dtype=jnp.float32), 'kernel_q': jax.random.uniform(ks[3], (1, 1, D_IN, D_MODEL), jnp.float32, -glorot, glorot), 'kernel_k': jax.random.uniform(ks[4], (1, 1, D_IN, D_MODEL), jnp.float32, -glorot, glorot), 'kernel_v': jax.random.uniform(ks[5], (1, 1, D_IN, D_MODEL), jnp.float32, -glorot, glorot), 'bias_q': 0.05 * jax.random.normal(ks[6], (D_MODEL,), dtype=jnp.float32), 'bias_k': 0.05 * jax.random.normal(ks[7], (D_MODEL,), dtype=jnp.float32), 'bias_v': 0.05 * jax.random.normal(jax.random.fold_in(key, 7), (D_MODEL,), dtype=jnp.float32)}
        return inp
    _L2_xattn_all = _L2_xattn_setup()
    _L2_xattn_in = {k: v for k, v in _L2_xattn_all.items() if k in ('kernel_q', 'kernel_k', 'kernel_v', 'bias_q', 'bias_k', 'bias_v')}
    del _L2_xattn_all

    def _L2_ffn_setup():
        import jax, jax.numpy as jnp
        import numpy as np
        LORA_DIM = 16
        LORA_TOKEN_INDEX = 1
        B, S, D, H = (4, 256, 128, 512)
        key = jax.random.key(seed)
        ks = jax.random.split(key, 6)
        x = jax.random.normal(ks[0], (B, S, D), dtype=jnp.float32)
        W1 = jax.random.normal(ks[1], (H, D), dtype=jnp.float32) * 0.02
        b1 = jnp.zeros((H,), dtype=jnp.float32)
        W2 = jax.random.normal(ks[2], (D, H), dtype=jnp.float32) * 0.02
        b2 = jnp.zeros((D,), dtype=jnp.float32)
        scale = jnp.asarray(0.001, dtype=jnp.float32)
        return {'x': x, 'W1': W1, 'b1': b1, 'W2': W2, 'b2': b2, 'scale': scale}
    _L2_ffn_all = _L2_ffn_setup()
    _L2_ffn_in = {k: v for k, v in _L2_ffn_all.items() if k in ('W1', 'b1', 'W2', 'b2', 'scale')}
    del _L2_ffn_all

    def _L3_xattn_setup():
        import jax, jax.numpy as jnp
        import numpy as np
        NUM_HEADS = 16

        def softmax1(attn):
            padded = jnp.pad(attn, ((0, 0), (0, 0), (0, 0), (0, 1)))
            return jax.nn.softmax(padded, axis=-1)[..., :-1]
        key = jax.random.key(seed)
        ks = jax.random.split(key, 7)
        B, N, M, C = (2, 128, 512, 128)
        x = jax.random.normal(ks[0], (B, N, C), dtype=jnp.float32)
        context = jax.random.normal(ks[1], (B, M, C), dtype=jnp.float32)
        mask = jax.random.randint(ks[2], (B, N, M), 0, 2) > 0
        s = 1.0 / np.sqrt(C)
        Wq = jax.random.normal(ks[3], (C, C), dtype=jnp.float32) * s
        Wkv = jax.random.normal(ks[4], (C, 2 * C), dtype=jnp.float32) * s
        Wproj = jax.random.normal(ks[5], (C, C), dtype=jnp.float32) * s
        bproj = jnp.zeros((C,), dtype=jnp.float32)
        return {'x': x, 'context': context, 'mask': mask, 'Wq': Wq, 'Wkv': Wkv, 'Wproj': Wproj, 'bproj': bproj}
    _L3_xattn_all = _L3_xattn_setup()
    _L3_xattn_in = {k: v for k, v in _L3_xattn_all.items() if k in ('Wq', 'Wkv', 'Wproj', 'bproj')}
    del _L3_xattn_all

    def _L3_ffn_setup():
        import jax, jax.numpy as jnp
        import numpy as np
        B, S, H, NH, E, F = (4, 128, 128, 16, 8, 512)
        D = H // NH
        EPS = 1e-05

        def _layernorm(x, g, b):
            mu = jnp.mean(x, axis=-1, keepdims=True)
            var = jnp.var(x, axis=-1, keepdims=True)
            return (x - mu) * jax.lax.rsqrt(var + EPS) * g + b
        key = jax.random.key(seed)
        ks = jax.random.split(key, 16)
        s = 0.02
        return {'x': jax.random.normal(ks[0], (B, S, H), jnp.float32), 'ln1_g': jnp.ones((H,), jnp.float32), 'ln1_b': jnp.zeros((H,), jnp.float32), 'ln2_g': jnp.ones((H,), jnp.float32), 'ln2_b': jnp.zeros((H,), jnp.float32), 'wq': jax.random.normal(ks[1], (H, H), jnp.float32) * s, 'bq': jnp.zeros((H,), jnp.float32), 'wk': jax.random.normal(ks[2], (H, H), jnp.float32) * s, 'bk': jnp.zeros((H,), jnp.float32), 'wv': jax.random.normal(ks[3], (H, H), jnp.float32) * s, 'bv': jnp.zeros((H,), jnp.float32), 'wo': jax.random.normal(ks[4], (H, H), jnp.float32) * s, 'bo': jnp.zeros((H,), jnp.float32), 'gate_w': jax.random.normal(ks[5], (H, E), jnp.float32) * s, 'gate_b': jnp.zeros((E,), jnp.float32), 'w1': jax.random.normal(ks[6], (E, H, F), jnp.float32) * s, 'b1': jnp.zeros((E, F), jnp.float32), 'w2': jax.random.normal(ks[7], (E, F, H), jnp.float32) * s, 'b2': jnp.zeros((E, H), jnp.float32)}
    _L3_ffn_all = _L3_ffn_setup()
    _L3_ffn_in = {k: v for k, v in _L3_ffn_all.items() if k in ('ln1_g', 'ln1_b', 'ln2_g', 'ln2_b', 'wq', 'bq', 'wk', 'bk', 'wv', 'bv', 'wo', 'bo', 'gate_w', 'gate_b', 'w1', 'b1', 'w2', 'b2')}
    del _L3_ffn_all
    return {'x': x, 'ctx_1024': ctx_1024, 'mask_1xSxS2_ff0': mask_1xSxS2_ff0, 'mask_BxSxS2_bk0': mask_BxSxS2_bk0, 'L0_xattn_fm_w': _L0_xattn_in['fm_w'], 'L0_xattn_fm_b': _L0_xattn_in['fm_b'], 'L0_xattn_fc_w': _L0_xattn_in['fc_w'], 'L0_xattn_fc_b': _L0_xattn_in['fc_b'], 'L0_ffn_Wg': _L0_ffn_in['Wg'], 'L0_ffn_Ws1': _L0_ffn_in['Ws1'], 'L0_ffn_Ws3': _L0_ffn_in['Ws3'], 'L0_ffn_Ws2': _L0_ffn_in['Ws2'], 'L0_ffn_We1': _L0_ffn_in['We1'], 'L0_ffn_We3': _L0_ffn_in['We3'], 'L0_ffn_We2': _L0_ffn_in['We2'], 'L1_xattn_Wq': _L1_xattn_in['Wq'], 'L1_xattn_bq': _L1_xattn_in['bq'], 'L1_xattn_Wk': _L1_xattn_in['Wk'], 'L1_xattn_bk': _L1_xattn_in['bk'], 'L1_xattn_Wv': _L1_xattn_in['Wv'], 'L1_xattn_bv': _L1_xattn_in['bv'], 'L1_xattn_Wo': _L1_xattn_in['Wo'], 'L1_xattn_bo': _L1_xattn_in['bo'], 'L1_ffn_gate_w': _L1_ffn_in['gate_w'], 'L1_ffn_gate_b': _L1_ffn_in['gate_b'], 'L1_ffn_w1': _L1_ffn_in['w1'], 'L1_ffn_b1': _L1_ffn_in['b1'], 'L1_ffn_w2': _L1_ffn_in['w2'], 'L1_ffn_b2': _L1_ffn_in['b2'], 'L2_xattn_kernel_q': _L2_xattn_in['kernel_q'], 'L2_xattn_kernel_k': _L2_xattn_in['kernel_k'], 'L2_xattn_kernel_v': _L2_xattn_in['kernel_v'], 'L2_xattn_bias_q': _L2_xattn_in['bias_q'], 'L2_xattn_bias_k': _L2_xattn_in['bias_k'], 'L2_xattn_bias_v': _L2_xattn_in['bias_v'], 'L2_ffn_W1': _L2_ffn_in['W1'], 'L2_ffn_b1': _L2_ffn_in['b1'], 'L2_ffn_W2': _L2_ffn_in['W2'], 'L2_ffn_b2': _L2_ffn_in['b2'], 'L2_ffn_scale': _L2_ffn_in['scale'], 'L3_xattn_Wq': _L3_xattn_in['Wq'], 'L3_xattn_Wkv': _L3_xattn_in['Wkv'], 'L3_xattn_Wproj': _L3_xattn_in['Wproj'], 'L3_xattn_bproj': _L3_xattn_in['bproj'], 'L3_ffn_ln1_g': _L3_ffn_in['ln1_g'], 'L3_ffn_ln1_b': _L3_ffn_in['ln1_b'], 'L3_ffn_ln2_g': _L3_ffn_in['ln2_g'], 'L3_ffn_ln2_b': _L3_ffn_in['ln2_b'], 'L3_ffn_wq': _L3_ffn_in['wq'], 'L3_ffn_bq': _L3_ffn_in['bq'], 'L3_ffn_wk': _L3_ffn_in['wk'], 'L3_ffn_bk': _L3_ffn_in['bk'], 'L3_ffn_wv': _L3_ffn_in['wv'], 'L3_ffn_bv': _L3_ffn_in['bv'], 'L3_ffn_wo': _L3_ffn_in['wo'], 'L3_ffn_bo': _L3_ffn_in['bo'], 'L3_ffn_gate_w': _L3_ffn_in['gate_w'], 'L3_ffn_gate_b': _L3_ffn_in['gate_b'], 'L3_ffn_w1': _L3_ffn_in['w1'], 'L3_ffn_b1': _L3_ffn_in['b1'], 'L3_ffn_w2': _L3_ffn_in['w2'], 'L3_ffn_b2': _L3_ffn_in['b2']}

def reference(x, ctx_1024, mask_1xSxS2_ff0, mask_BxSxS2_bk0, L0_xattn_fm_w, L0_xattn_fm_b, L0_xattn_fc_w, L0_xattn_fc_b, L0_ffn_Wg, L0_ffn_Ws1, L0_ffn_Ws3, L0_ffn_Ws2, L0_ffn_We1, L0_ffn_We3, L0_ffn_We2, L1_xattn_Wq, L1_xattn_bq, L1_xattn_Wk, L1_xattn_bk, L1_xattn_Wv, L1_xattn_bv, L1_xattn_Wo, L1_xattn_bo, L1_ffn_gate_w, L1_ffn_gate_b, L1_ffn_w1, L1_ffn_b1, L1_ffn_w2, L1_ffn_b2, L2_xattn_kernel_q, L2_xattn_kernel_k, L2_xattn_kernel_v, L2_xattn_bias_q, L2_xattn_bias_k, L2_xattn_bias_v, L2_ffn_W1, L2_ffn_b1, L2_ffn_W2, L2_ffn_b2, L2_ffn_scale, L3_xattn_Wq, L3_xattn_Wkv, L3_xattn_Wproj, L3_xattn_bproj, L3_ffn_ln1_g, L3_ffn_ln1_b, L3_ffn_ln2_g, L3_ffn_ln2_b, L3_ffn_wq, L3_ffn_bq, L3_ffn_wk, L3_ffn_bk, L3_ffn_wv, L3_ffn_bv, L3_ffn_wo, L3_ffn_bo, L3_ffn_gate_w, L3_ffn_gate_b, L3_ffn_w1, L3_ffn_b1, L3_ffn_w2, L3_ffn_b2):
    import jax
    import jax.numpy as jnp

    def _L0_xattn_ref(values, keys, query, fm_w, fm_b, fc_w, fc_b):
        import jax, jax.numpy as jnp
        import numpy as np
        EMBED = 128
        HEADS = 16
        HEAD_DIM = EMBED // HEADS
        EXP_DIM = 2 * HEAD_DIM

        def _feature_map(x, fm_w, fm_b):
            z = jnp.einsum('nshd,ed->nshe', x, fm_w) + fm_b
            return jnp.concatenate([jnp.exp(z), jnp.exp(-z)], axis=-1)
        N, S, _ = query.shape
        v = values.reshape(N, -1, HEADS, HEAD_DIM)
        k = keys.reshape(N, -1, HEADS, HEAD_DIM)
        q = query.reshape(N, -1, HEADS, HEAD_DIM)
        v, k, q = (_feature_map(x, fm_w, fm_b) for x in (v, k, q))
        scores = jnp.einsum('nqhd,nkhd->nhqk', q, k) / jnp.sqrt(jnp.float32(EMBED))
        attn = jax.nn.softmax(scores, axis=-1)
        out = jnp.einsum('nhql,nlhd->nqhd', attn, v)
        out = out.reshape(N, S, HEADS * EXP_DIM)
        return out @ fc_w.T + fc_b

    def _L0_ffn_ref(x, Wg, Ws1, Ws3, Ws2, We1, We3, We2):
        import jax, jax.numpy as jnp
        import numpy as np
        D_MODEL, FF_DIM = (128, 256)
        N_SHARED, N_ROUTED, TOP_K = (1, 8, 2)
        BATCH, SEQ = (2, 256)
        B, S, d = x.shape
        E = Wg.shape[1]
        xf = x.reshape(-1, d)
        T = xf.shape[0]
        gates = jax.nn.sigmoid(xf @ Wg)
        vals, idx = jax.lax.top_k(gates, TOP_K)
        vals = vals / vals.sum(axis=-1, keepdims=True)
        w = jnp.zeros((T, E), x.dtype).at[jnp.arange(T)[:, None], idx].add(vals)
        shared = jax.nn.silu(xf @ Ws1) * (xf @ Ws3) @ Ws2
        h = jax.nn.silu(jnp.einsum('td,edf->tef', xf, We1)) * jnp.einsum('td,edf->tef', xf, We3)
        routed = jnp.einsum('tef,efd,te->td', h, We2, w)
        out = (shared + routed) / (N_SHARED + TOP_K)
        return out.reshape(B, S, d)

    def _L1_xattn_ref(q, k, v, Wq, bq, Wk, bk, Wv, bv, Wo, bo):
        import jax, jax.numpy as jnp
        import numpy as np
        HIDDEN = 128
        HEADS = 16
        D_K = HIDDEN // HEADS
        B, S = (2, 256)
        bs = q.shape[0]

        def proj(x, W, b):
            y = x @ W.T + b
            return y.reshape(bs, -1, HEADS, D_K).transpose(0, 2, 1, 3)
        qh, kh, vh = (proj(q, Wq, bq), proj(k, Wk, bk), proj(v, Wv, bv))
        scores = jnp.einsum('bhqd,bhkd->bhqk', qh, kh) / jnp.sqrt(jnp.float32(D_K))
        attn = jax.nn.softmax(scores, axis=-1)
        x = jnp.einsum('bhqk,bhkd->bhqd', attn, vh)
        x = x.transpose(0, 2, 1, 3).reshape(bs, -1, HEADS * D_K)
        return x @ Wo.T + bo

    def _L1_ffn_ref(h, gate_w, gate_b, w1, b1, w2, b2):
        import math
        import jax, jax.numpy as jnp
        import numpy as np
        B, L, D, F_FF, E = (4, 256, 128, 512, 8)
        TOP_K = 1
        CAPACITY_FACTOR = 1.25
        Bh, Lh, Dh = h.shape
        T = Bh * Lh
        capacity = max(1, math.ceil(CAPACITY_FACTOR * (T * TOP_K / E)))
        x = h.reshape(T, Dh)
        logits = x @ gate_w.T + gate_b
        probs = jax.nn.softmax(logits, axis=-1)
        idx = jnp.argmax(probs, axis=-1)
        top_prob = jnp.max(probs, axis=-1)
        one_hot = jax.nn.one_hot(idx, E, dtype=jnp.int32)
        pos = jnp.take_along_axis(jnp.cumsum(one_hot, axis=0), idx[:, None], axis=1)[:, 0] - 1
        keep = pos < capacity
        safe_pos = jnp.where(keep, pos, 0)
        buf = jnp.zeros((E, capacity, Dh), dtype=x.dtype)
        buf = buf.at[idx, safe_pos].add(x * keep[:, None].astype(x.dtype))
        hdn = jax.nn.relu(jnp.einsum('ecd,edf->ecf', buf, w1) + b1[:, None, :])
        eout = jnp.einsum('ecf,efd->ecd', hdn, w2) + b2[:, None, :]
        gathered = eout[idx, safe_pos]
        out = gathered * (top_prob * keep.astype(x.dtype))[:, None]
        return out.reshape(Bh, Lh, Dh)

    def _L2_xattn_ref(q, k, v, mask, kernel_q, kernel_k, kernel_v, bias_q, bias_k, bias_v):
        import jax, jax.numpy as jnp
        import numpy as np
        B, S, D_IN, D_MODEL = (4, 256, 128, 128)
        Wq, Wk, Wv = (kernel_q[0, 0], kernel_k[0, 0], kernel_v[0, 0])
        qp = jax.nn.relu(jnp.einsum('bsd,de->bse', q, Wq) + bias_q)
        kp = jax.nn.relu(jnp.einsum('bsd,de->bse', k, Wk) + bias_k)
        vp = jax.nn.relu(jnp.einsum('bsd,de->bse', v, Wv) + bias_v)
        scores = jax.nn.relu(jnp.einsum('bqe,bke->bqk', qp, kp))
        dk = jnp.asarray(kp.shape[-1], dtype=scores.dtype)
        logits = scores / jnp.sqrt(dk) + mask
        out = jax.nn.relu(jnp.einsum('bqk,bke->bqe', logits, vp))
        return out

    def _L2_ffn_ref(x, W1, b1, W2, b2, scale):
        import jax, jax.numpy as jnp
        import numpy as np
        LORA_DIM = 16
        LORA_TOKEN_INDEX = 1
        B, S, D, H = (4, 256, 128, 512)
        Bx, Sx, Dx = x.shape
        Hx = W1.shape[0]
        lt = jax.lax.dynamic_slice_in_dim(x, LORA_TOKEN_INDEX, LORA_DIM, axis=1)
        even = lt[:, ::2, :]
        odd = lt[:, 1::2, :]
        m1 = (even[:, :4, :, None] * odd[:, :4, None, :]).reshape(Bx, Hx, Dx)
        m2 = (even[:, 4:, :, None] * odd[:, 4:, None, :]).reshape(Bx, Dx, Hx)
        h = jnp.einsum('bsd,hd->bsh', x, W1) + scale * jnp.einsum('bsd,bhd->bsh', x, m1) + b1
        h = jax.nn.gelu(h, approximate=False)
        out = jnp.einsum('bsh,oh->bso', h, W2) + scale * jnp.einsum('bsh,boh->bso', h, m2) + b2
        return out

    def _L3_xattn_ref(x, context, mask, Wq, Wkv, Wproj, bproj):
        import jax, jax.numpy as jnp
        import numpy as np
        NUM_HEADS = 16

        def softmax1(attn):
            padded = jnp.pad(attn, ((0, 0), (0, 0), (0, 0), (0, 1)))
            return jax.nn.softmax(padded, axis=-1)[..., :-1]
        B, N, C = x.shape
        M = context.shape[1]
        H = NUM_HEADS
        d = C // H
        scale = d ** (-0.5)
        q = (x @ Wq).reshape(B, N, H, d).transpose(0, 2, 1, 3)
        kv = (context @ Wkv).reshape(B, M, 2, H, d)
        k = kv[:, :, 0].transpose(0, 2, 1, 3)
        v = kv[:, :, 1].transpose(0, 2, 1, 3)
        attn = jnp.einsum('bhnd,bhmd->bhnm', q, k) * scale
        neg = -jnp.finfo(attn.dtype).max
        attn = jnp.where(mask[:, None, :, :], neg, attn)
        attn = softmax1(attn)
        out = jnp.einsum('bhnm,bhmd->bhnd', attn, v)
        out = out.transpose(0, 2, 1, 3).reshape(B, N, C)
        return out @ Wproj + bproj

    def _L3_ffn_ref(x, ln1_g, ln1_b, ln2_g, ln2_b, wq, bq, wk, bk, wv, bv, wo, bo, gate_w, gate_b, w1, b1, w2, b2):
        import jax, jax.numpy as jnp
        import numpy as np
        B, S, H, NH, E, F = (4, 128, 128, 16, 8, 512)
        D = H // NH
        EPS = 1e-05

        def _layernorm(x, g, b):
            mu = jnp.mean(x, axis=-1, keepdims=True)
            var = jnp.var(x, axis=-1, keepdims=True)
            return (x - mu) * jax.lax.rsqrt(var + EPS) * g + b
        b, s, h = x.shape
        hn = _layernorm(x, ln1_g, ln1_b)
        q = (hn @ wq + bq).reshape(b, s, NH, D).transpose(0, 2, 1, 3)
        k = (hn @ wk + bk).reshape(b, s, NH, D).transpose(0, 2, 1, 3)
        v = (hn @ wv + bv).reshape(b, s, NH, D).transpose(0, 2, 1, 3)
        scores = jnp.einsum('bhqd,bhkd->bhqk', q, k) / jnp.sqrt(jnp.float32(D))
        attn = jax.nn.softmax(scores, axis=-1)
        o = jnp.einsum('bhqk,bhkd->bhqd', attn, v)
        o = o.transpose(0, 2, 1, 3).reshape(b, s, h)
        x = x + (o @ wo + bo)
        hn2 = _layernorm(x, ln2_g, ln2_b).reshape(-1, h)
        logits = hn2 @ gate_w + gate_b
        idx = jnp.argmax(logits, axis=-1)
        mid = jax.nn.relu(jnp.einsum('th,ehf->etf', hn2, w1) + b1[:, None, :])
        y = jnp.einsum('etf,efh->eth', mid, w2) + b2[:, None, :]
        moe = y[idx, jnp.arange(hn2.shape[0])]
        return x + moe.reshape(b, s, h)
    x = x + _L0_xattn_ref(ctx_1024, ctx_1024, _layernorm(x, axis=-1), L0_xattn_fm_w, L0_xattn_fm_b, L0_xattn_fc_w, L0_xattn_fc_b)
    x = x + _L0_ffn_ref(_layernorm(x, axis=-1), L0_ffn_Wg, L0_ffn_Ws1, L0_ffn_Ws3, L0_ffn_Ws2, L0_ffn_We1, L0_ffn_We3, L0_ffn_We2)
    x = x + _L1_xattn_ref(_layernorm(x, axis=-1), ctx_1024, ctx_1024, L1_xattn_Wq, L1_xattn_bq, L1_xattn_Wk, L1_xattn_bk, L1_xattn_Wv, L1_xattn_bv, L1_xattn_Wo, L1_xattn_bo)
    x = x + _L1_ffn_ref(_layernorm(x, axis=-1), L1_ffn_gate_w, L1_ffn_gate_b, L1_ffn_w1, L1_ffn_b1, L1_ffn_w2, L1_ffn_b2)
    x = x + _L2_xattn_ref(_layernorm(x, axis=-1), ctx_1024, ctx_1024, mask_1xSxS2_ff0, L2_xattn_kernel_q, L2_xattn_kernel_k, L2_xattn_kernel_v, L2_xattn_bias_q, L2_xattn_bias_k, L2_xattn_bias_v)
    x = x + _L2_ffn_ref(_layernorm(x, axis=-1), L2_ffn_W1, L2_ffn_b1, L2_ffn_W2, L2_ffn_b2, L2_ffn_scale)
    x = x + _L3_xattn_ref(_layernorm(x, axis=-1), ctx_1024, mask_BxSxS2_bk0, L3_xattn_Wq, L3_xattn_Wkv, L3_xattn_Wproj, L3_xattn_bproj)
    x = x + _L3_ffn_ref(_layernorm(x, axis=-1), L3_ffn_ln1_g, L3_ffn_ln1_b, L3_ffn_ln2_g, L3_ffn_ln2_b, L3_ffn_wq, L3_ffn_bq, L3_ffn_wk, L3_ffn_bk, L3_ffn_wv, L3_ffn_bv, L3_ffn_wo, L3_ffn_bo, L3_ffn_gate_w, L3_ffn_gate_b, L3_ffn_w1, L3_ffn_b1, L3_ffn_w2, L3_ffn_b2)
    return x

_drawn_inputs = setup_inputs


def setup_inputs(seed=0):
    import zlib

    import numpy as np

    out = dict(_drawn_inputs(seed))
    spreads = {'L0_xattn_fc_b': (0.0, 0.8),
     'L1_xattn_bq': (0.0, 0.8),
     'L1_xattn_bk': (0.0, 2.0),
     'L1_xattn_bv': (0.0, 0.8),
     'L1_xattn_bo': (0.0, 0.8),
     'L1_ffn_gate_b': (0.0, 0.8),
     'L1_ffn_b1': (0.0, 0.8),
     'L1_ffn_b2': (0.0, 2.0),
     'L2_ffn_b1': (0.0, 0.8),
     'L2_ffn_b2': (0.0, 0.8),
     'L3_xattn_bproj': (0.0, 2.0),
     'L3_ffn_ln1_g': (1.0, 0.6),
     'L3_ffn_ln1_b': (0.0, 0.8),
     'L3_ffn_ln2_g': (1.0, 0.6),
     'L3_ffn_ln2_b': (0.0, 0.8),
     'L3_ffn_bq': (0.0, 2.0),
     'L3_ffn_bk': (0.0, 2.0),
     'L3_ffn_bv': (0.0, 2.0),
     'L3_ffn_bo': (0.0, 2.0),
     'L3_ffn_gate_b': (0.0, 0.8),
     'L3_ffn_b1': (0.0, 2.0),
     'L3_ffn_b2': (0.0, 2.0)}
    factors = {'L0_xattn_fm_b': 4.172,
     'L0_ffn_Wg': 8.0,
     'L0_ffn_Ws1': 8.0,
     'L0_ffn_Ws3': 8.0,
     'L0_ffn_Ws2': 8.0,
     'L0_ffn_We1': 8.0,
     'L0_ffn_We3': 8.0,
     'L0_ffn_We2': 8.0,
     'L1_xattn_Wq': 8.0,
     'L1_xattn_Wk': 8.0,
     'L1_xattn_Wv': 3.092,
     'L1_ffn_gate_w': 8.0,
     'L1_ffn_w1': 8.0,
     'L1_ffn_w2': 8.0,
     'L2_xattn_bias_q': 8.0,
     'L2_xattn_bias_k': 8.0,
     'L2_ffn_W1': 8.0,
     'L2_ffn_W2': 8.0,
     'L3_xattn_Wq': 8.0,
     'L3_xattn_Wkv': 6.926,
     'L3_xattn_Wproj': 6.992,
     'L3_ffn_wq': 8.0,
     'L3_ffn_wk': 8.0,
     'L3_ffn_wv': 8.0,
     'L3_ffn_wo': 8.0,
     'L3_ffn_gate_w': 8.0,
     'L3_ffn_w1': 8.0,
     'L3_ffn_w2': 8.0}
    for name, (base, spread) in spreads.items():
        noise = np.random.default_rng([zlib.crc32(name.encode()), seed]).standard_normal(out[name].shape)
        drawn = base * np.exp(spread * noise) if base else spread * noise
        out[name] = jnp.asarray(drawn.astype(out[name].dtype))
    for name, factor in factors.items():
        out[name] = (out[name] * factor).astype(out[name].dtype)
    return out
```

```python
from contextlib import ExitStack

import numpy as np

import concourse.bass as bass
from concourse import mybir

F32 = mybir.dt.float32
F32R = mybir.dt.float32r
BF16 = mybir.dt.bfloat16
U8 = mybir.dt.uint8
ALU = mybir.AluOpType
ACT = mybir.ActivationFunctionType
AX = mybir.AxisListType.X

NB, S, D, NK, NH = 4, 512, 128, 77, 16
NKP = NK + 1
CK = NB * NKP
EPS = 1e-5
BIG = 1e30
CAP = 320
RM = 96
RK = 112


class Engine:

    def __init__(self, sem):
        self.sem, self.n, self.queue, self.past = sem, 0, [], {}

    def wait(self, *marks):
        for m in marks:
            if m is None:
                continue
            if isinstance(m, list):
                self.wait(*m)
                continue
            sem, value = m
            if self.past.get(sem.name, 0) < value:
                self.past[sem.name] = value
                self.queue.append(lambda e, s=sem, v=value: e.wait_ge(s, v))

    def do(self, make, *marks):
        self.wait(*marks)
        self.n += 1
        self.queue.append(lambda e, s=self.sem: make(e).then_inc(s, 1))
        return (self.sem, self.n)

    def quiet(self, make, *marks):
        self.wait(*marks)
        self.queue.append(make)

    def play(self, e):
        for make in self.queue:
            make(e)


class Loads:

    def __init__(self, sem):
        self.sem, self.n = sem, 0

    def start(self, engine, out, in_, *marks):
        engine.wait(*marks)
        self.n += 16
        engine.queue.append(lambda e, s=self.sem: e.dma_start(out, in_).then_inc(s, 16))

    def all(self):
        return (self.sem, self.n)


class Banks:

    def __init__(self, ps, count):
        self.ps, self.count, self.at, self.read = ps, count, 0, [[] for _ in range(8)]

    def take(self, n=1):
        if self.at + n > self.count:
            self.at = 0
        b = self.at
        self.at = (self.at + n) % self.count
        marks = []
        for i in range(b, b + n):
            assert self.read[i] is not None, "a bank whose reader is not queued yet"
            marks += self.read[i]
            self.read[i] = None
        return b, marks

    def free(self, b, *marks, n=1):
        for i in range(b, b + n):
            self.read[i] = list(marks)


class Slots:

    def __init__(self, aps):
        self.aps, self.at, self.read = aps, 0, [[] for _ in aps]

    def take(self):
        i = self.at
        self.at = (i + 1) % len(self.aps)
        assert self.read[i] is not None, "a slot whose reader is not queued yet"
        marks, self.read[i] = self.read[i], None
        return i, self.aps[i], marks

    def free(self, i, *marks):
        self.read[i] = list(marks)


def program(nc, A, out):
    with ExitStack() as ctx:
        def sb(name, cols, dt=F32):
            return ctx.enter_context(nc.sbuf_tensor(name, [128, cols], dt))

        def sem(name):
            return ctx.enter_context(nc.semaphore(name))

        PS = ctx.enter_context(nc.psum_tensor("PS", [128, 8, 512], F32))
        banks = Banks(PS, 6)
        acc_bank = Slots([6, 7])

        pe, act, dve, pool, sp = (Engine(sem(n)) for n in ("pe", "act", "dve", "pool", "sp"))
        loads = {}

        def load(name, dst, src, *marks, by=None):
            if name not in loads:
                loads[name] = Loads(sem("ld_" + name))
            loads[name].start(by or sp, dst, src, *marks)

        X = sb("X", NB * 512)
        Xb = [X[:, 512 * b:512 * b + 512] for b in range(NB)]
        RA = sb("RA", 8192)
        with nc.sbuf_tensor("Q0", [128, 8192], F32R) as Q0t:
            Q0 = [Q0t[:, 0:4096], Q0t[:, 4096:8192]]
        RB = sb("RB", 8192)
        S0 = sb("S0", 1280)
        S1 = sb("S1", 1024)
        S2 = sb("S2", 1408)
        QB = ctx.enter_context(nc.sbuf_tensor("QB", [128, 2 * 2048], F32R))
        KB = ctx.enter_context(nc.sbuf_tensor("KB", [128, 3 * 2048], F32R))
        STG = ctx.enter_context(nc.sbuf_tensor("STG", [128, 2 * 512], F32R))
        MX = ctx.enter_context(nc.sbuf_tensor("MX", [128, 2 * 4 * RK], F32R))
        MT = ctx.enter_context(nc.sbuf_tensor("MT", [128, 512], F32R))
        VB = sb("VB", 2048)
        Ht = sb("Ht", 2 * 512)
        HT = sb("HT", 2 * 512)
        PT = sb("PT", 8 * 512)
        OT = sb("OT", 2048)
        ON = sb("ON", 2 * 256)
        OC = sb("OC", 1024)
        CT = sb("CT", CK)
        ident = sb("ident", 128)
        tri = sb("tri", 128)
        ones = sb("ones", 128)
        msk = sb("msk", 2 * NH)
        rev = sb("rev", 32)
        bias = sb("bias", 12 * 128)
        b1t = sb("b1t", 64)
        b2t = sb("b2t", 256)
        cols = sb("cols", 40)
        st = sb("st", 2 * 24)
        mv = sb("mv", 2 * 8)
        ve = sb("ve", 2 * 8)
        nh = sb("nh", 4)
        rt = sb("rt", 2 * 512)
        den = sb("den", 2 * 64)
        negI = ctx.enter_context(nc.sbuf_tensor("negI", [128, 4 * NK + 4], BF16))
        mkb = ctx.enter_context(nc.sbuf_tensor("mkb", [128, 4 * 512], BF16))
        mk8 = ctx.enter_context(nc.sbuf_tensor("mk8", [128, 4 * 512], U8))
        mkf = sb("mkf", 512)
        gates = sb("gates", 24)
        prev = sb("prev", 8 * 17)
        L0Q = [None, None]

        pt = Slots([PT[:, 512 * i:512 * i + 512] for i in range(8)])
        stg = Slots([STG[:, 512 * i:512 * i + 512] for i in range(2)])

        load("c", ident[:, :], A["c_ident"])
        load("x0", X[:, 0:512].rearrange("p (t d) -> p t d", t=4), A["x"][0].rearrange("(t p) d -> p t d", p=128))
        load("c", msk[:, :], A["c_mask"])
        load("ctx", CT[:, :], A["ctxT"])
        load("l0", S0[:, 512:520], A["fm_w"])
        load("l0", S0[:, 768:1024], A["c_block"])
        load("l0", S0[:, 1024:1280].rearrange("p (c n) -> p c n", c=2), A["fc_w"].rearrange("(c p) n -> p c n", p=128))
        load("l0", cols[0:96, 0:1], A["fm_b"])
        load("l0", cols[0:96, 1:2], A["c_sign"])
        load("l0", bias[0:NK, 0:256], A["fm_br"])
        load("l0", bias[0:NK, 256:512], A["c_signr"])
        for b in range(1, NB):
            load(f"x{b}", Xb[b].rearrange("p (t d) -> p t d", t=4), A["x"][b].rearrange("(t p) d -> p t d", p=128))
        load("c2", tri[:, :], A["c_tri"])
        load("c2", rev[:, :], A["c_rev"])
        load("c2", gates[:, :].rearrange("p (l e) -> p l e", l=3), A["gates"].rearrange("l p e -> p l e"))
        load("rb", bias[:, 512:1536].rearrange("p (r d) -> p r d", r=8), A["rows"].rearrange("r p d -> p r d"))
        load("cb", cols[:, 2:40], A["colb"])
        load("rb", rt[:, 960:976], A["gateb"])

        W13 = RA[:, 0:9 * 512].rearrange("p (e n) -> p e n", e=9)
        W2m = RA[:, 9 * 512:9 * 512 + 9 * 256].rearrange("p (e c n) -> p e c n", e=9, c=2)
        load("l0f", W13, A["l0_w13"].rearrange("e p n -> p e n"))
        load("l0f", W2m, A["l0_w2"].rearrange("e (c p) n -> p e c n", p=128))
        load("l1", S1[:, :], A["l1_w"])
        load("l2", mkf[0:NK, :], A["mfT"])
        load("l2", mk8[0:NK, :], A["mbT"])
        load("l2", b1t[:, :], A["b1"])
        load("l2", b2t[0:8, :], A["b2"])

        ready_c = loads["c"].all()

        k = pool.do(lambda e: e.memset(nh[:, :], -0.5))
        k_nh = k
        k_ones = pool.do(lambda e: e.memset(ones[:, :], 1.0))
        k_mx = pool.do(lambda e: e.memset(MX[:, :].bitcast(F32), 0.0))
        k_stg = pool.do(lambda e: e.memset(STG[:, :].bitcast(F32), -1.0))
        k_prev = pool.do(lambda e: e.memset(prev[:, 0:8], 0.0))
        for i in range(2):
            stg.free(i, k_stg)

        xw = [[loads[f"x{b}"].all()] for b in range(NB)]
        yw = [[] for _ in range(NB)]
        hfree = [[], []]
        htfree = [[], []]
        qfree = [[], []]
        mxfree = [[k_mx], [k_mx]]
        rtfree = [[], []]
        mtfree = []
        kfree = []
        vfree = []
        mq = [Loads(sem("mq0")), Loads(sem("mq1"))]

        def mm(o, l, r, first=True, last=True):
            return lambda e: e.matmul(o, l, r, start=first, stop=last, skip_group_check=True)

        def layernorm(src, dst, par, src_marks, dst_marks):
            s6 = st[:, 24 * par:24 * par + 24]
            s2 = mv[:, 8 * par:8 * par + 8].rearrange("p (t c) -> p t c", t=4)
            v4 = ve[:, 8 * par:8 * par + 4]
            r4 = ve[:, 8 * par + 4:8 * par + 8]
            for t in range(4):
                m = dve.do(lambda e, t=t: e.bn_stats(s6[:, 6 * t:6 * t + 6], src[:, 128 * t:128 * t + 128]), src_marks)
            for t in range(4):
                m = dve.do(lambda e, t=t: e.bn_aggr(s2[:, t, :], s6[:, 6 * t:6 * t + 6]), m)
            m = dve.do(lambda e: e.tensor_scalar(v4, s2[:, :, 1], EPS, None, ALU.add), m)
            m = pool.do(lambda e: e.tensor_tensor(r4, v4, nh[:, :], ALU.pow), m, k_nh)
            for t in range(4):
                m2 = dve.do(lambda e, t=t: e.tensor_scalar(dst[:, 128 * t:128 * t + 128], src[:, 128 * t:128 * t + 128],
                                                           s2[:, t, 0:1], r4[:, t:t + 1], ALU.subtract, ALU.mult),
                            m, dst_marks)
            return m2

        def transposed(src, par, ready, scale=None, shift=None):
            b, marks = banks.take()
            for t in range(4):
                f = (lambda e, t=t: e.transpose(PS[:, b, 128 * t:128 * t + 128], src[:, 128 * t:128 * t + 128], ident[:, :]))
                if t < 3:
                    pe.quiet(f, ready, ready_c, marks)
                else:
                    turned = pe.do(f)
            dst = HT[:, 512 * par:512 * par + 512]
            if scale is None:
                m = act.do(lambda e: e.activation(dst, PS[:, b, :], ACT.Copy), turned, htfree[par])
            else:
                m = act.do(lambda e: e.activation(dst, PS[:, b, :], ACT.Identity, bias=shift, scale=scale),
                           turned, htfree[par], loads["cb"].all())
            htfree[par] = None
            banks.free(b, m)
            return m, turned

        def ln_front(b, par, scale=None, shift=None):
            H = Ht[:, 512 * par:512 * par + 512]
            h = layernorm(Xb[b], H, par, xw[b], hfree[par])
            hT, turned = transposed(H, par, h, scale, shift)
            hfree[par] = [turned]
            return h, hT

        def add_row(b, row, h):
            r = bias[:, 512 + 128 * row:640 + 128 * row].rearrange("p (o d) -> p o d", o=1).broadcast_to((128, 4, 128))
            x = Xb[b].rearrange("p (t d) -> p t d", t=4)
            m = pool.do(lambda e: e.tensor_tensor(x, x, r, ALU.add), h, xw[b], loads["rb"].all())
            xw[b] = [m]

        class Att:
            def __init__(self, n, hpg, vd, scale, wq, wk, bq, bk, wo, ready, row, expo=False, mask=False, bqm=None):
                self.n, self.hpg, self.vd, self.scale = n, hpg, vd, scale
                self.wq, self.wk, self.bq, self.bk, self.wo = wq, wk, bq, bk, wo
                self.ready, self.row, self.expo, self.mask = ready, row, expo, mask
                self.ng = NH // hpg

        def split(a, src_bank, n, out, part, bq, marks_ps, marks_out):
            P = PS[:, src_bank, 0:n]
            if a.expo:
                i, E, em = pt.take()
                m = act.do(lambda e: e.activation(E[0:96, 0:n], P[0:96, :], ACT.Exp, bias=bq, scale=1.0), marks_ps, em, a.ready)
                banks.free(src_bank, m)
                m1 = dve.do(lambda e: e.tensor_copy(out[0:96, :], E[0:96, 0:n]), m, marks_out)
                m2 = dve.do(lambda e: e.tensor_tensor(out[part:part + 32, :], E[part:part + 32, 0:n],
                                                      out[part:part + 32, :].bitcast(F32), ALU.subtract), m1)
                pt.free(i, m2)
                return m2
            if bq is None:
                m1 = act.do(lambda e: e.activation(out[0:96, :], P[0:96, :], ACT.Copy), marks_ps, marks_out)
                m2 = dve.do(lambda e: e.tensor_tensor(out[part:part + 32, :], P[part:part + 32, :],
                                                      out[part:part + 32, :].bitcast(F32), ALU.subtract), m1)
            else:
                m1 = act.do(lambda e: e.activation(out[0:96, :], P[0:96, :], ACT.Identity, bias=bq, scale=1.0),
                            marks_ps, marks_out, loads["cb"].all())
                m2 = dve.do(lambda e: e.scalar_tensor_tensor(out[part:part + 32, :], P[part:part + 32, :],
                                                             bq[part:part + 32, :],
                                                             out[part:part + 32, :].bitcast(F32),
                                                             ALU.add, ALU.subtract), m1)
            banks.free(src_bank, m2)
            return m2

        def keys(a, g, n, rhs, rhs_marks, kblk, k_marks):
            b, marks = banks.take()
            m = pe.do(mm(PS[0:96, b, 0:n], a.wk[:, g, :], rhs), marks, rhs_marks, a.ready)
            i, sg, sm = stg.take()
            m = split(a, b, n, sg[:, 0:n], 64, a.bk(g), [m], sm)
            mk = msk[0:RK, 0:16] if a.hpg == 4 else msk[0:RK, 16:32]
            for hh in range(a.hpg):
                h = g * a.hpg + hh
                m2 = pool.do(lambda e, hh=hh, h=h: e.tensor_scalar(kblk(hh)[0:RK, :], sg[0:RK, 0:n].bitcast(F32),
                                                                   mk[:, h:h + 1], None, ALU.mult), m, k_marks, ready_c)
            stg.free(i, m2)
            return m2

        def queries(a, g, par, hT, qs):
            b, marks = banks.take()
            m = pe.do(mm(PS[0:96, b, :], a.wq[:, g, :], HT[:, 512 * par:512 * par + 512]), marks, hT, a.ready)
            return split(a, b, 512, qs(g), 32, a.bq(g), [m], qfree[par]), m

        def row_maxima(par, reduced, qs, groups):
            nonlocal mtfree
            b, marks = banks.take()
            M = MX[:, 4 * RK * par:4 * RK * par + 4 * RK].rearrange("p (t c) -> p t c", t=4).bitcast(F32)
            for t in range(4):
                f = (lambda e, t=t: e.transpose(PS[0:RK, b, 128 * t:128 * t + 128], M[:, t, :], ident[:, :]))
                if t < 3:
                    pe.quiet(f, marks, reduced)
                else:
                    m = pe.do(f)
            m = dve.do(lambda e: e.tensor_copy(MT[RM:RK, :], PS[RM:RK, b, :]), m, mtfree)
            banks.free(b, m)
            for g in groups:
                mq[par].start(sp, qs(g)[RM:RK, :].bitcast(F32), MT[RM:RK, :].bitcast(F32), m, qfree[par])
            mtfree = [mq[par].all()]
            return mq[par].all()

        def out_front(a, b, par, po_marks):
            pass

        ot_free = [[], [], [], []]
        oc_free = []
        on = Slots([ON[:, 0:256], ON[:, 256:512]])

        def finish(a, par, ot_marks, dst, dst_marks, extra=None):
            nonlocal oc_free
            vd = a.vd
            nc2 = NH * vd // 128
            cb = []
            for c in range(nc2):
                cb.append(banks.take())
            oc_written = []
            for j in range(4):
                b, marks = banks.take()
                for hg in range(4):
                    f = (lambda e, hg=hg, b=b, j=j: e.transpose(PS[:, b, 128 * hg:128 * hg + 128],
                                                                OT[:, 512 * hg + 128 * j:512 * hg + 128 * j + 128], ident[:, :]))
                    if hg < 3:
                        pe.quiet(f, marks, ot_marks)
                    else:
                        m = pe.do(f)
                O = PS[:, b, :].rearrange("p (h c) -> p h c", c=32)
                R = den[:, 64 * par + 16 * j:64 * par + 16 * j + 16]
                if extra is None:
                    m = dve.do(lambda e, R=R, O=O: e.reciprocal(R, O[:, :, vd]), m)
                else:
                    m = dve.do(lambda e, R=R, O=O, j=j: e.tensor_tensor(R, O[:, :, vd], extra[0](j), ALU.add), m, extra[1])
                    m = dve.do(lambda e, R=R: e.reciprocal(R, R), m)
                i, N, nm = on.take()
                m = dve.do(lambda e, N=N, O=O, R=R: e.tensor_tensor(
                    N[:, 0:NH * vd].rearrange("p (h c) -> p h c", c=vd), O[:, :, 0:vd],
                    R.rearrange("p (h o) -> p h o", o=1).broadcast_to((128, NH, vd)), ALU.mult), m, nm)
                banks.free(b, m)
                for c in range(nc2):
                    m2 = pe.do(lambda e, c=c, j=j, N=N: e.transpose(PS[:, cb[c][0], 128 * j:128 * j + 128],
                                                                    N[:, 128 * c:128 * c + 128], ident[:, :]), m, cb[c][1])
                on.free(i, m2)
            for hg in range(4):
                ot_free[hg] = [m2]
            done = []
            for c in range(nc2):
                m = act.do(lambda e, c=c: e.activation(OC[:, 512 * c:512 * c + 512], PS[:, cb[c][0], :], ACT.Copy), m2, oc_free)
                banks.free(cb[c][0], m)
            b, marks = banks.take()
            for j in range(4):
                for c in range(nc2):
                    f = mm(PS[:, b, 128 * j:128 * j + 128], OC[:, 512 * c + 128 * j:512 * c + 128 * j + 128], a.wo[:, c, :],
                           c == 0, c == nc2 - 1)
                    if j < 3 or c < nc2 - 1:
                        pe.quiet(f, m, marks, a.ready)
                    else:
                        m2 = pe.do(f, m, marks)
            oc_free = [m2]
            m = dve.do(lambda e, b=b: e.tensor_tensor(dst, dst, PS[:, b, :], ALU.add), m2, dst_marks)
            banks.free(b, m)
            return m

        kall = KB[:, 0:NH * CK].rearrange("p (h k) -> p h k", h=NH)
        vall = VB[:, :].rearrange("p (b h c) -> p b h c", b=4, h=16)

        def prepare(a, wv, bvrow, bv_sign=None):
            nonlocal kfree, vfree
            a.kd = [keys(a, g, CK, CT[:, :], loads["ctx"].all(), lambda hh, g=g: kall[:, g * a.hpg + hh, :], kfree)
                    for g in range(a.ng)]
            vd = a.vd
            vz = VB[0:NK, :].rearrange("p (g c) -> p g c", c=32)
            m0 = pool.do(lambda e: e.memset(vz[:, :, vd + 1:32], 0.0), vfree)
            m0 = pool.do(lambda e: e.memset(vz[:, :, vd:vd + 1], 1.0), vfree)
            n = NH * vd
            a.vd_marks = [m0]
            for b in range(NB):
                k, marks = banks.take()
                m = pe.do(mm(PS[0:NK, k, 0:n], CT[:, NKP * b:NKP * b + NK], wv), marks, loads["ctx"].all(), a.ready)
                src = PS[0:NK, k, 0:n].rearrange("p (h c) -> p h c", c=vd)
                dst = vall[0:NK, b, :, 0:vd]
                if a.expo:
                    i, E, em = pt.take()
                    m = dve.do(lambda e, E=E, k=k: e.tensor_tensor(E[0:NK, 0:n], PS[0:NK, k, 0:n], bvrow, ALU.add), m, em)
                    banks.free(k, m)
                    m = act.do(lambda e, E=E, dst=dst: e.activation(dst, E[0:NK, 0:n].rearrange("p (h c) -> p h c", c=vd), ACT.Exp),
                               m, vfree)
                    pt.free(i, m)
                elif bvrow is None:
                    m = dve.do(lambda e, dst=dst, src=src: e.tensor_copy(dst, src), m, vfree)
                    banks.free(k, m)
                else:
                    m = dve.do(lambda e, dst=dst, src=src: e.tensor_tensor(dst, src, bvrow.rearrange("p (h c) -> p h c", c=vd), ALU.add),
                               m, vfree, loads["rb"].all())
                    banks.free(k, m)
                a.vd_marks.append(m)
            kfree, vfree = None, None

        def cross_front(a, b, par, qbuf):
            h, hT = ln_front(b, par)
            add_row(b, a.row, h)
            qs = lambda g: qbuf[par][:, 512 * g:512 * g + 512]
            qm = []
            for g in range(a.ng):
                m, read = queries(a, g, par, hT, qs)
                qm.append(m)
            htfree[par] = [read]
            M = MX[:, 4 * RK * par:4 * RK * par + 4 * RK].rearrange("p (t c) -> p t c", t=4)
            per = 1 if a.hpg == 4 else 3
            nr = a.hpg * NKP
            for t in range(4):
                for g0 in range(0, a.ng, per):
                    gs = range(g0, min(g0 + per, a.ng))
                    k, marks = banks.take()
                    for g in gs:
                        o = PS[:, k, nr * (g - g0):nr * (g - g0) + nr]
                        l = qs(g)[0:RM, 128 * t:128 * t + 128]
                        r = kall[0:RM, g * a.hpg:(g + 1) * a.hpg, NKP * b:NKP * b + NKP]
                        if a.mask:
                            pe.quiet(mm(o, l, r, True, False), marks, qm[g], a.kd[g])
                            m = pe.do(mm(o.rearrange("p (h k) -> p h k", k=NKP)[:, :, 0:NK], mkb[0:NK, 512 * b + 128 * t:512 * b + 128 * t + 128],
                                         negI[0:NK, 0:4 * NK], False, True), a.mask_ready)
                        else:
                            m = pe.do(mm(o, l, r), marks, qm[g], a.kd[g])
                    nh_ = len(gs) * a.hpg
                    src = PS[:, k, 0:nh_ * NKP].rearrange("p (h k) -> p h k", k=NKP)[:, :, 0:NK]
                    dst = M[:, t, RM + g0 * a.hpg:RM + g0 * a.hpg + nh_]
                    m = dve.do(lambda e, dst=dst, src=src: e.tensor_reduce(dst, src, AX, ALU.max), m, mxfree[par])
                    banks.free(k, m)
            extra = None
            if a.mask:
                m = dve.do(lambda e: e.tensor_scalar(M[:, :, RM:RK], M[:, :, RM:RK].bitcast(F32), 0.0, None, ALU.max), m)
                X1 = rt[:, 512 * par:512 * par + 64].rearrange("p (t h) -> p t h", t=4)
                me = act.do(lambda e: e.activation(X1, M[:, :, RM:RK].bitcast(F32), ACT.Exp, bias=0.0, scale=-a.scale), m, rtfree[par])
                rtfree[par] = None
                extra = (lambda j: X1[:, j, :], me)
            mt = row_maxima(par, m, qs, range(a.ng))
            mxfree[par] = [(pe.sem, pe.n)] + ([extra[1]] if extra else [])
            qfree[par] = None
            return qs, qm, mt, extra

        def back_groups(a, par, steps, evac):
            pass

        def cross_back(a, b, par, state):
            nonlocal kfree, vfree
            qs, qm, mt, extra = state
            ot = []
            wait_exp = []

            def scores(hg):
                res = []
                for i in range(4):
                    h = 4 * hg + i
                    g = h // a.hpg
                    k, marks = banks.take()
                    l = kall[0:RK, h, NKP * b:NKP * b + NK]
                    if a.mask:
                        pe.quiet(mm(PS[0:NK, k, :], l, qs(g)[0:RK, :], True, False), marks, mt, qm[g], a.kd[g])
                        m = pe.do(mm(PS[0:NK, k, :], negI[0:NK, 0:NK], mkb[0:NK, 512 * b:512 * b + 512], False, True), a.mask_ready)
                    else:
                        m = pe.do(mm(PS[0:NK, k, :], l, qs(g)[0:RK, :]), marks, mt, qm[g], a.kd[g])
                    s, P, pm = pt.take()
                    m = act.do(lambda e, P=P, k=k: e.activation(P[0:NK, :], PS[0:NK, k, :], ACT.Exp, bias=0.0, scale=a.scale), m, pm)
                    banks.free(k, m)
                    res.append((h, s, P, m))
                return res

            def values(hg, res):
                i6, o, om = acc_bank.take()
                for i, (h, s, P, m) in enumerate(res):
                    f = mm(PS[32 * i:32 * i + 32, o, :], vall[0:NK, b, h, :], P[0:NK, :])
                    if i < 3:
                        pe.quiet(f, [r[3] for r in res], om, a.vd_marks)
                    else:
                        m = pe.do(f)
                for (h, s, P, _) in res:
                    pt.free(s, m)
                m = dve.do(lambda e, o=o: e.tensor_copy(OT[:, 512 * hg:512 * hg + 512], PS[:, o, :]), m, ot_free[hg])
                acc_bank.free(i6, m)
                ot.append(m)

            last = scores(0)
            for hg in range(4):
                nxt = scores(hg + 1) if hg < 3 else None
                values(hg, last)
                last = nxt
            qfree[par] = [(pe.sem, pe.n)]
            kfree = [(pe.sem, pe.n)]
            vfree = [(pe.sem, pe.n)]
            m = finish(a, par, ot, Xb[b], xw[b], extra)
            if extra:
                rtfree[par] = [m]
            xw[b] = [m]

        def route_common(L, par, k0, lm):
            R = rt[:, 512 * par + k0:512 * par + k0 + 128]
            v = R[:, 0:4]
            r = R[:, 8:40].rearrange("p (t e) -> p t e", t=4)
            mx = R[:, 4:8]
            oh = R[:, 40:72].rearrange("p (t e) -> p t e", t=4)
            m = dve.do(lambda e: e.tensor_reduce(v, L, AX, ALU.max), lm)
            vb = v.rearrange("p (t o) -> p t o", o=1).broadcast_to((128, 4, 8))
            m = dve.do(lambda e: e.tensor_tensor(r, L, vb, ALU.is_equal), m)
            m = dve.do(lambda e: e.tensor_tensor(r, r, rev[:, :].rearrange("p (t e) -> p t e", t=4), ALU.mult), m, loads["c2"].all())
            m = dve.do(lambda e: e.tensor_reduce(mx, r, AX, ALU.max), m)
            m = dve.do(lambda e: e.tensor_tensor(oh, r, mx.rearrange("p (t o) -> p t o", o=1).broadcast_to((128, 4, 8)), ALU.is_equal), m)
            return v, oh, m

        def moe_front(kind, b, par, li, scale=None, shift=None, src=None):
            if src is None:
                h, hT = ln_front(b, par)
            else:
                h, hT = src
            G = gates[:, 8 * li:8 * li + 8]
            hv = HT[:, 512 * par:512 * par + 512]
            k, marks = banks.take()
            for t in range(4):
                f = mm(PS[:, k, 8 * t:8 * t + 8], hv[:, 128 * t:128 * t + 128], G)
                if t < 3:
                    pe.quiet(f, marks, hT, loads["c2"].all())
                else:
                    m = pe.do(f)
            Rt = rt[:, 512 * par:512 * par + 448]
            L = Rt[:, 0:32].rearrange("p (t e) -> p t e", t=4)
            W = Rt[:, 32:68].rearrange("p (t e) -> p t e", t=4)
            psl = PS[:, k, 0:32].rearrange("p (t e) -> p t e", t=4)
            if kind == 0:
                m = dve.do(lambda e: e.tensor_copy(L, psl), m, rtfree[par])
            else:
                gb = rt[:, 960 + 8 * (kind - 1):968 + 8 * (kind - 1)].rearrange("p (o e) -> p o e", o=1).broadcast_to((128, 4, 8))
                m = dve.do(lambda e: e.tensor_tensor(L, psl, gb, ALU.add), m, rtfree[par], loads["rb"].all())
            banks.free(k, m)
            v1, oh1, m = route_common(L, par, 80, m)
            W8 = W[:, :, 0:8]
            bc = lambda ap: ap.rearrange("p (t o) -> p t o", o=1).broadcast_to((128, 4, 8))
            wT = None
            if kind == 0:
                L2 = Rt[:, 352:384].rearrange("p (t e) -> p t e", t=4)
                m = dve.do(lambda e: e.scalar_tensor_tensor(L2, oh1, -BIG, L, ALU.mult, ALU.add), m)
                v2, oh2, m = route_common(L2, par, 208, m)
                gv = Rt[:, 384:392]
                T = Rt[:, 392:404]
                m = dve.do(lambda e: e.tensor_copy(gv[:, 0:4], v1), m)
                m = dve.do(lambda e: e.tensor_copy(gv[:, 4:8], v2), m)
                m = act.do(lambda e: e.activation(gv, gv, ACT.Exp, bias=0.0, scale=-1.0), m)
                m = dve.do(lambda e: e.tensor_scalar(gv, gv, 1.0, None, ALU.add), m)
                m = dve.do(lambda e: e.reciprocal(gv, gv), m)
                m = dve.do(lambda e: e.tensor_tensor(T[:, 0:4], gv[:, 0:4], gv[:, 4:8], ALU.add), m)
                m = dve.do(lambda e: e.tensor_scalar(T[:, 0:4], T[:, 0:4], 3.0, None, ALU.mult), m)
                m = dve.do(lambda e: e.reciprocal(T[:, 4:8], T[:, 0:4]), m)
                m = dve.do(lambda e: e.tensor_tensor(gv.rearrange("p (a t) -> p a t", a=2), gv.rearrange("p (a t) -> p a t", a=2),
                                                     T[:, 4:8].rearrange("p (o t) -> p o t", o=1).broadcast_to((128, 2, 4)), ALU.mult), m)
                m = dve.do(lambda e: e.tensor_tensor(W8, oh1, bc(gv[:, 0:4]), ALU.mult), m)
                m = dve.do(lambda e: e.tensor_tensor(L2, oh2, bc(gv[:, 4:8]), ALU.mult), m)
                m = dve.do(lambda e: e.tensor_tensor(W8, W8, L2, ALU.add), m)
                m = dve.do(lambda e: e.memset(W[:, :, 8:9], 1.0 / 3.0), m)
            elif kind == 1:
                E = Rt[:, 352:384].rearrange("p (t e) -> p t e", t=4)
                P1 = Rt[:, 384:392]
                me = dve.do(lambda e: e.tensor_tensor(E, L, bc(v1), ALU.subtract), m)
                me = act.do(lambda e: e.activation(E, E, ACT.Exp), me)
                me = dve.do(lambda e: e.tensor_reduce(P1[:, 0:4], E, AX, ALU.add), me)
                me = dve.do(lambda e: e.reciprocal(P1[:, 4:8], P1[:, 0:4]), me)
                pv = prev[:, 32 * b:32 * b + 40]
                mp = m
                for t in range(4):
                    mp = dve.do(lambda e, t=t: e.tensor_tensor(pv[:, 8 * t + 8:8 * t + 16], pv[:, 8 * t:8 * t + 8], oh1[:, t, :], ALU.add), mp, k_prev)
                k, marks = banks.take()
                ohf = Rt[:, 120:152]
                pe.quiet(mm(PS[:, k, 0:32], tri[:, :], ohf, True, False), marks, m, loads["c2"].all())
                m = pe.do(mm(PS[:, k, 0:32], ones[:, :], pv[:, 0:32], False, True), mp, k_ones)
                psl2 = PS[:, k, 0:32].rearrange("p (t e) -> p t e", t=4)
                m = dve.do(lambda e: e.scalar_tensor_tensor(W8, psl2, CAP + 0.5, oh1, ALU.is_le, ALU.mult), m)
                banks.free(k, m)
                m = dve.do(lambda e: e.tensor_tensor(W8, W8, bc(P1[:, 4:8]), ALU.mult), m, me)
            else:
                m = dve.do(lambda e: e.tensor_copy(W8, oh1), m)
            if kind:
                k, marks = banks.take()
                for t in range(4):
                    f = (lambda e, t=t, k=k: e.transpose(PS[0:8, k, 128 * t:128 * t + 128], W8[:, t, :], ident[:, :]))
                    if t < 3:
                        pe.quiet(f, marks, m)
                    else:
                        mw = pe.do(f)
                wT = Ht[0:8, 512 * par:512 * par + 512]
                mw = act.do(lambda e, k=k: e.activation(wT, PS[0:8, k, :], ACT.Copy), mw, hfree[par])
                banks.free(k, mw)
                hfree[par] = None
                rtfree[par] = None
                return hT, W, m, wT, mw
            rtfree[par] = None
            return hT, W, m, None, None

        def combine(b, W, wm, e_, k, m):
            ms = []
            for t in range(4):
                x = Xb[b][:, 128 * t:128 * t + 128]
                ms.append(dve.do(lambda e, t=t, x=x: e.scalar_tensor_tensor(x, PS[:, k, 128 * t:128 * t + 128], W[:, t, e_:e_ + 1],
                                                                            x, ALU.mult, ALU.add), m, wm, xw[b]))
            banks.free(k, ms[-1])
            xw[b] = [ms[-1]]

        def gated_back(b, par, state):
            hT, W, wm, _, _ = state
            hv = HT[:, 512 * par:512 * par + 512]
            rdy = loads["l0f"].all()

            def up(x):
                res = []
                for c in range(2):
                    kg, m1 = banks.take()
                    mg = pe.do(mm(PS[:, kg, :], W13[:, x, 128 * c:128 * c + 128], hv), m1, hT, rdy)
                    ku, m1 = banks.take()
                    mu = pe.do(mm(PS[:, ku, :], W13[:, x, 256 + 128 * c:384 + 128 * c], hv), m1)
                    s, P, pm = pt.take()
                    m = act.do(lambda e, P=P, kg=kg: e.activation(P, PS[:, kg, :], ACT.Silu), mg, pm)
                    banks.free(kg, m)
                    m = dve.do(lambda e, P=P, ku=ku: e.tensor_tensor(P, P, PS[:, ku, :], ALU.mult), m, mu)
                    banks.free(ku, m)
                    res.append((s, P, m))
                return res

            def down(x, res):
                k, m1 = banks.take()
                for t in range(4):
                    for c in range(2):
                        f = mm(PS[:, k, 128 * t:128 * t + 128], res[c][1][:, 128 * t:128 * t + 128], W2m[:, x, c, :], c == 0, c == 1)
                        if t == 3 and c == 1:
                            m = pe.do(f)
                        else:
                            pe.quiet(f, m1, [r[2] for r in res])
                for r in res:
                    pt.free(r[0], m)
                combine(b, W, wm, x, k, m)

            last = up(0)
            for x in range(9):
                nxt = up(x + 1) if x < 8 else None
                down(x, last)
                last = nxt
            htfree[par] = [(pe.sem, pe.n)]
            rtfree[par] = list(xw[b])

        def relu_back(b, par, state, w1, w2, b1, b2, rdy):
            hT, W, wm, wT, mw = state
            hv = HT[:, 512 * par:512 * par + 512]

            def up(x):
                res = []
                for c in range(4):
                    k, m1 = banks.take()
                    m = pe.do(mm(PS[:, k, :], w1[:, x, 128 * c:128 * c + 128], hv), m1, hT, rdy)
                    s, P, pm = pt.take()
                    bb = b1[:, 4 * x + c:4 * x + c + 1]
                    if c == 3:
                        m = dve.do(lambda e, P=P, k=k, bb=bb: e.tensor_scalar(P, PS[:, k, :], bb, 0.0, ALU.add, ALU.max), m, pm, loads["l2"].all())
                    else:
                        m = act.do(lambda e, P=P, k=k, bb=bb: e.activation(P, PS[:, k, :], ACT.Relu, bias=bb, scale=1.0), m, pm, loads["l2"].all())
                    banks.free(k, m)
                    res.append((s, P, m))
                return res

            def down(x, res):
                k, m1 = banks.take()
                for t in range(4):
                    for c in range(4):
                        f = mm(PS[:, k, 128 * t:128 * t + 128], res[c][1][:, 128 * t:128 * t + 128], w2[:, x, c, :], c == 0, c == 3)
                        if t == 3 and c == 3:
                            m = pe.do(f)
                        else:
                            pe.quiet(f, m1, [r[2] for r in res])
                for r in res:
                    pt.free(r[0], m)
                combine(b, W, wm, x, k, m)

            last = up(0)
            for x in range(8):
                nxt = up(x + 1) if x < 7 else None
                down(x, last)
                last = nxt
            htfree[par] = [(pe.sem, pe.n)]
            k, m1 = banks.take()
            for t in range(4):
                f = mm(PS[:, k, 128 * t:128 * t + 128], wT[:, 128 * t:128 * t + 128], b2)
                if t < 3:
                    pe.quiet(f, m1, mw, loads["l2"].all())
                else:
                    m = pe.do(f)
            hfree[par] = [m]
            m = dve.do(lambda e: e.tensor_tensor(Xb[b], Xb[b], PS[:, k, :], ALU.add), m, xw[b])
            banks.free(k, m)
            xw[b] = [m]
            rtfree[par] = [m]

        W0 = S0[:, 0:512]
        WR0 = S2[:, 0:768]
        wr0 = WR0.rearrange("p (g q c) -> p g q c", g=8, q=3)
        wv0 = S0[:, 768:1024]
        l0r = loads["l0"].all()
        F8 = S0[:, 512:520].rearrange("p (o e) -> p o e", o=1).broadcast_to((128, 32, 8))
        blk = S0[:, 768:1024].rearrange("p (a e) -> p a e", e=8)
        m = dve.do(lambda e: e.tensor_tensor(blk, blk, F8, ALU.mult), l0r)
        for q in range(3):
            mw0 = dve.do(lambda e, q=q: e.tensor_copy(wr0[:, :, q, :], wv0.rearrange("p (g c) -> p g c", g=8)), m)
        m = dve.do(lambda e: e.tensor_tensor(cols[0:96, 0:1], cols[0:96, 0:1], cols[0:96, 1:2], ALU.mult), l0r)
        bv0 = bias[0:NK, 0:256]
        mw0 = dve.do(lambda e: e.tensor_tensor(bv0, bv0, bias[0:NK, 256:512], ALU.mult), l0r)

        wrap = WR0.rearrange("p (g c) -> p g c", g=8)
        a0 = Att(0, 2, 16, 1.0 / float(np.sqrt(np.float32(128))), wrap, wrap, lambda g: cols[0:96, 0:1], lambda g: cols[0:96, 0:1],
                 S0[:, 1024:1280].rearrange("p (c n) -> p c n", c=2), [l0r, mw0], 0, expo=True)
        prepare(a0, wv0, bv0)

        units = []
        for b in range(NB):
            units.append((lambda par, b=b: cross_front(a0, b, par, Q0), lambda par, s, b=b: cross_back(a0, b, par, s), f"l0x{b}"))

        for b in range(NB):
            units.append((lambda par, b=b: moe_front(0, b, par, 0), lambda par, s, b=b: gated_back(b, par, s), f"l0f{b}"))

        w1v = S1[:, :]
        a1 = Att(1, 4, 8, 1.0 / float(np.sqrt(np.float32(8))),
                 w1v[:, 0:384].rearrange("p (g c) -> p g c", g=4), w1v[:, 384:768].rearrange("p (g c) -> p g c", g=4),
                 lambda g: cols[0:96, 2 + g:3 + g], lambda g: cols[0:96, 6 + g:7 + g],
                 w1v[:, 896:1024].rearrange("p (c n) -> p c n", c=1), [loads["l1"].all(), loads["cb"].all()], 1)
        QQ = [QB[:, 0:2048], QB[:, 2048:4096]]
        for b in range(NB):
            units.append((lambda par, b=b: cross_front(a1, b, par, QQ), lambda par, s, b=b: cross_back(a1, b, par, s), f"l1x{b}"))
        w1e = RB[:, 0:4096].rearrange("p (e n) -> p e n", e=8)
        w2e = RB[:, 4096:8192].rearrange("p (e c n) -> p e c n", e=8, c=4)
        for b in range(NB):
            units.append((lambda par, b=b: moe_front(1, b, par, 1),
                          lambda par, s, b=b: relu_back(b, par, s, w1e, w2e, b1t[:, 0:32], b2t[0:8, 0:128], loads["l1f"].all()), f"l1f{b}"))

        KP = RB[:, 0:CK]
        VP = RB[:, 512:1024]
        QP = RB[:, 1024:2048]
        S2v = S2[:, :]
        l2 = {}

        def l2_prepare():
            end1 = [(pe.sem, pe.n)]
            l2["free"] = end1
            for i in range(2):
                ltfree[i], w12free[i] = end1, end1
            k, marks = banks.take()
            m = pe.do(mm(PS[:, k, 0:CK], S2v[:, 128:256], CT[:, :]), marks, loads["l2w"].all())
            m = act.do(lambda e, k=k: e.activation(KP, PS[:, k, 0:CK], ACT.Relu, bias=cols[:, 11:12], scale=1.0), m, end1)
            banks.free(k, m)
            l2["k"] = m
            k, marks = banks.take()
            for b in range(NB):
                f = mm(PS[0:NK, k, 128 * b:128 * b + 128], CT[:, NKP * b:NKP * b + NK], S2v[:, 256:384])
                if b < 3:
                    pe.quiet(f, marks)
                else:
                    m = pe.do(f)
            vb = bias[0:NK, 512 + 128 * 6:512 + 128 * 7].rearrange("p (o d) -> p o d", o=1).broadcast_to((NK, 4, 128))
            vv = VP[0:NK, 0:512].rearrange("p (b d) -> p b d", b=4)
            m = dve.do(lambda e: e.tensor_tensor(vv, PS[0:NK, k, :].rearrange("p (b d) -> p b d", b=4), vb, ALU.add), m, end1)
            banks.free(k, m)
            l2["v"] = dve.do(lambda e: e.tensor_scalar(VP[0:NK, 0:512], VP[0:NK, 0:512], 0.0, None, ALU.max), m)

        qpfree = [None, None]

        def l2x_front(b, par):
            h, hT = ln_front(b, par)
            k, marks = banks.take()
            m = pe.do(mm(PS[:, k, :], S2v[:, 0:128], HT[:, 512 * par:512 * par + 512]), marks, hT, loads["l2w"].all())
            htfree[par] = [m]
            qp = QP[:, 512 * par:512 * par + 512]
            qpfree[par] = qpfree[par] or l2["free"]
            m = act.do(lambda e: e.activation(qp, PS[:, k, :], ACT.Relu, bias=cols[:, 10:11], scale=1.0), m, qpfree[par])
            banks.free(k, m)
            return qp, m

        def l2x_back(b, par, state):
            qp, m = state
            k, marks = banks.take()
            m = pe.do(mm(PS[0:NK, k, :], KP[:, NKP * b:NKP * b + NK], qp), m, marks, l2["k"])
            qpfree[par] = [m]
            s, P, pm = pt.take()
            m = act.do(lambda e: e.activation(P[0:NK, :], PS[0:NK, k, :], ACT.Relu, bias=0.0, scale=1.0 / float(np.sqrt(np.float32(128)))), m, pm)
            banks.free(k, m)
            m = dve.do(lambda e: e.tensor_tensor(P[0:NK, :], P[0:NK, :], mkf[0:NK, :], ALU.add), m)
            k2, marks = banks.take()
            for t in range(4):
                f = mm(PS[:, k2, 128 * t:128 * t + 128], P[0:NK, 128 * t:128 * t + 128], VP[0:NK, 128 * b:128 * b + 128])
                if t < 3:
                    pe.quiet(f, m, marks, l2["v"])
                else:
                    m = pe.do(f)
            pt.free(s, m)
            m = dve.do(lambda e: e.scalar_tensor_tensor(Xb[b], PS[:, k2, :], 0.0, Xb[b], ALU.max, ALU.add), m, xw[b])
            banks.free(k2, m)
            xw[b] = [m]

        for b in range(NB):
            units.append((lambda par, b=b: l2x_front(b, par), lambda par, s, b=b: l2x_back(b, par, s), f"l2x{b}"))

        LT = RB[:, 2048:6144]
        W1x = RB[:, 6144:7168]
        W2x = RB[:, 7168:8192]
        lq = [Loads(sem("lq0")), Loads(sem("lq1"))]
        ltfree = [[], []]
        w12free = [[], []]

        def l2f_front(b, par):
            H = Ht[:, 512 * par:512 * par + 512]
            h, hT = ln_front(b, par)
            add_row(b, 2, h)
            lt = LT[0:1, 2048 * par:2048 * par + 2048]
            lq[par].start(sp, lt.rearrange("o (t d) -> o t d", t=16), H[1:17, 0:128], h, ltfree[par])
            lm = lq[par].all()
            hfree[par] = hfree[par] + [lm]
            row = lambda t: lt[:, 128 * t:128 * t + 128]
            w1 = W1x[:, 512 * par:512 * par + 512]
            w2 = W2x[:, 512 * par:512 * par + 512]
            k, marks = banks.take()
            for i in range(4):
                f = mm(PS[:, k, 128 * i:128 * i + 128], row(2 * i + 1), row(2 * i))
                if i < 3:
                    pe.quiet(f, marks, lm)
                else:
                    m = pe.do(f)
            m1 = dve.do(lambda e, k=k: e.scalar_tensor_tensor(w1, PS[:, k, :], cols[:, 12:13], S2v[:, 384:896], ALU.mult, ALU.add),
                        m, w12free[par], loads["cb"].all(), loads["l2w"].all())
            banks.free(k, m1)
            k, marks = banks.take()
            o = PS[:, k, :].rearrange("p (r o) -> p r o", r=4)
            for i in range(4):
                f = mm(o[:, :, 32 * i:32 * i + 32], row(2 * (4 + i) + 1),
                       row(2 * (4 + i)).rearrange("p (o r) -> p r o", r=4))
                if i < 3:
                    pe.quiet(f, marks)
                else:
                    m = pe.do(f)
            ltfree[par] = [m]
            m2 = dve.do(lambda e, k=k: e.scalar_tensor_tensor(w2, PS[:, k, :], cols[:, 12:13], S2v[:, 896:1408], ALU.mult, ALU.add), m)
            banks.free(k, m2)
            return hT, w1, w2, m1, m2

        def l2f_back(b, par, state):
            hT, w1, w2, m1, m2 = state
            res = []
            for c in range(4):
                k, marks = banks.take()
                m = pe.do(mm(PS[:, k, :], w1[:, 128 * c:128 * c + 128], HT[:, 512 * par:512 * par + 512]), marks, hT, m1)
                s, P, pm = pt.take()
                m = act.do(lambda e, P=P, k=k, c=c: e.activation(P, PS[:, k, :], ACT.Gelu, bias=cols[:, 13 + c:14 + c], scale=1.0), m, pm)
                banks.free(k, m)
                res.append((s, P, m))
            htfree[par] = [(pe.sem, pe.n)]
            k, marks = banks.take()
            for t in range(4):
                for c in range(4):
                    f = mm(PS[:, k, 128 * t:128 * t + 128], res[c][1][:, 128 * t:128 * t + 128], w2[:, 128 * c:128 * c + 128], c == 0, c == 3)
                    if t == 3 and c == 3:
                        m = pe.do(f)
                    else:
                        pe.quiet(f, marks, m2, [r[2] for r in res])
            for r in res:
                pt.free(r[0], m)
            w12free[par] = [m]
            m = dve.do(lambda e: e.tensor_tensor(Xb[b], Xb[b], PS[:, k, :], ALU.add), m, xw[b])
            banks.free(k, m)
            xw[b] = [m]

        for b in range(NB):
            units.append((lambda par, b=b: l2f_front(b, par), lambda par, s, b=b: l2f_back(b, par, s), f"l2f{b}"))

        w3 = S0[:, 0:1024]
        a3 = Att(3, 4, 8, float(8 ** -0.5),
                 w3[:, 0:384].rearrange("p (g c) -> p g c", g=4), w3[:, 384:768].rearrange("p (g c) -> p g c", g=4),
                 lambda g: None, lambda g: None,
                 w3[:, 896:1024].rearrange("p (c n) -> p c n", c=1), None, 3, mask=True)

        def l3x_masks():
            m = dve.do(lambda e: e.tensor_copy(mkb[0:NK, :], mk8[0:NK, :]), loads["l2"].all())
            i3 = ident[0:NK, 0:NK].rearrange("p (o k) -> p o k", o=1).broadcast_to((NK, 4, NK))
            a3.mask_ready = dve.do(lambda e: e.tensor_scalar(negI[0:NK, 0:4 * NK].rearrange("p (h k) -> p h k", h=4), i3, -BIG, None, ALU.mult), ready_c)

        for b in range(NB):
            units.append((lambda par, b=b: cross_front(a3, b, par, QQ), lambda par, s, b=b: cross_back(a3, b, par, s), f"l3x{b}"))

        w4 = S1[:, :]
        a4 = Att(4, 4, 8, 1.0 / float(np.sqrt(np.float32(8))),
                 w4[:, 0:384].rearrange("p (g c) -> p g c", g=4), w4[:, 384:768].rearrange("p (g c) -> p g c", g=4),
                 lambda g: cols[0:96, 17 + g:18 + g], lambda g: cols[0:96, 21 + g:22 + g],
                 w4[:, 896:1024].rearrange("p (c n) -> p c n", c=1), None, 4)
        Y = RB[:, 0:2048]
        Yb = [Y[:, 512 * b:512 * b + 512] for b in range(NB)]
        V4 = [RB[:, 2048:4096], RB[:, 4096:6144]]
        v4free = [[], []]
        kslots = Slots([KB[:, 2048 * i:2048 * i + 2048] for i in range(3)])
        k4 = {}

        def l3_self_open(marks):
            for i in range(2):
                vz = V4[i].rearrange("p (g c) -> p g c", c=32)
                m = pool.do(lambda e, vz=vz: e.memset(vz[:, :, 9:32], 0.0), marks)
                m = pool.do(lambda e, vz=vz: e.memset(vz[:, :, 8:9], 1.0), marks)
                v4free[i] = [m]

        def self_norms(b, par):
            h0 = layernorm(Xb[b], Yb[b], par, xw[b], k4["rb_free"])
            H = Ht[:, 512 * par:512 * par + 512]
            h = layernorm(Yb[b], H, par, h0, hfree[par])
            hT, turned = transposed(H, par, h, cols[:, 25:26], cols[:, 26:27])
            hfree[par] = [turned]
            r = bias[:, 512 + 128 * 4:640 + 128 * 4].rearrange("p (o d) -> p o d", o=1).broadcast_to((128, 4, 128))
            y = Yb[b].rearrange("p (t d) -> p t d", t=4)
            yw[b] = [pool.do(lambda e: e.tensor_tensor(y, y, r, ALU.add), h)]
            k, marks = banks.take()
            hv = HT[:, 512 * par:512 * par + 512]
            for c in range(4):
                f = mm(PS[:, k, 128 * c:128 * c + 128], hv[:, 128 * c:128 * c + 128], w4[:, 768:896])
                if c < 3:
                    pe.quiet(f, marks, hT, a4.ready)
                else:
                    m = pe.do(f)
            bv = bias[:, 512 + 128 * 7:640 + 128 * 7].rearrange("p (h c) -> p h c", c=8)
            vv = V4[par].rearrange("p (c h k) -> p c h k", c=4, h=16)
            for c in range(4):
                src = PS[:, k, 128 * c:128 * c + 128].rearrange("p (h c) -> p h c", c=8)
                mv_ = dve.do(lambda e, c=c, src=src: e.tensor_tensor(vv[:, c, :, 0:8], src, bv, ALU.add), m, v4free[par])
            banks.free(k, mv_)
            v4free[par] = None
            return hT, vv, mv_

        def self_front(b, g, par, st):
            hT, vv, vm = st
            qs = lambda g: QQ[par][:, 512 * g:512 * g + 512]
            qm, read = queries(a4, g, par, hT, qs)
            s, K, km = kslots.take()
            kv = K.rearrange("p (h k) -> p h k", h=4)
            kd = keys(a4, g, 512, HT[:, 512 * par:512 * par + 512], hT, lambda hh: kv[:, hh, :], km)
            M = MX[:, 4 * RK * par:4 * RK * par + 4 * RK].rearrange("p (t c) -> p t c", t=4)
            for t in range(4):
                for p2 in range(2):
                    k, marks = banks.take(2)
                    for i in range(2):
                        f = mm(PS[:, k + i, :], qs(g)[0:RM, 128 * t:128 * t + 128], kv[0:RM, 2 * p2 + i, :])
                        if i:
                            m = pe.do(f)
                        else:
                            pe.quiet(f, marks, qm, kd)
                    dst = M[:, t, RM + 4 * g + 2 * p2:RM + 4 * g + 2 * p2 + 2]
                    m = dve.do(lambda e, dst=dst, k=k: e.tensor_reduce(dst, PS[:, k:k + 2, :], AX, ALU.max), m, mxfree[par])
                    banks.free(k, m, n=2)
            mt = row_maxima(par, m, qs, [g])
            mxfree[par] = [(pe.sem, pe.n)]
            return s, kv, kd, qm, mt

        def self_back(b, g, par, st, fr):
            hT, vv, vm = st
            s, kv, kd, qm, mt = fr
            qs = QQ[par][:, 512 * g:512 * g + 512]
            i6, o, om = acc_bank.take()

            def scores(c):
                res = []
                for i in range(4):
                    k, marks = banks.take()
                    m = pe.do(mm(PS[:, k, :], kv[0:RK, i, 128 * c:128 * c + 128], qs[0:RK, :]), marks, mt, qm, kd)
                    sl, P, pm = pt.take()
                    m = act.do(lambda e, P=P, k=k: e.activation(P, PS[:, k, :], ACT.Exp, bias=0.0, scale=a4.scale), m, pm)
                    banks.free(k, m)
                    res.append((sl, P, m))
                return res

            def values(c, res):
                for i, (sl, P, m) in enumerate(res):
                    f = mm(PS[32 * i:32 * i + 32, o, :], vv[:, c, 4 * g + i, :], P, c == 0, c == 3)
                    if i < 3:
                        pe.quiet(f, [r[2] for r in res], om, vm)
                    else:
                        m = pe.do(f)
                for r in res:
                    pt.free(r[0], m)
                return m

            last = scores(0)
            for c in range(4):
                nxt = scores(c + 1) if c < 3 else None
                m = values(c, last)
                last = nxt
            kslots.free(s, m)
            m = dve.do(lambda e: e.tensor_copy(OT[:, 512 * g:512 * g + 512], PS[:, o, :]), m, ot_free[g])
            acc_bank.free(i6, m)
            return m

        def self_attention():
            pend = None
            st = None
            ots = []

            def flush(p):
                b, g, par, s, fr = p
                ots.append(self_back(b, g, par, s, fr))
                if g == 3:
                    qfree[par] = [(pe.sem, pe.n)]
                    v4free[par] = [(pe.sem, pe.n)]
                    m = finish(a4, par, list(ots), Yb[b], yw[b])
                    yw[b] = [m]
                    ots.clear()
                    xx = pool.do(lambda e: e.tensor_tensor(Xb[b], Xb[b], Yb[b], ALU.add), m, xw[b])
                    xw[b] = [xx]

            for b in range(NB):
                par = b % 2
                for g in range(4):
                    if g == 0:
                        st = self_norms(b, par)
                    fr = self_front(b, g, par, st)
                    if g == 3:
                        htfree[par] = [(pe.sem, pe.n)]
                        qfree[par] = None
                    if pend:
                        flush(pend)
                    pend = (b, g, par, st, fr)
            flush(pend)

        def l3m_front(b, par):
            H = Ht[:, 512 * par:512 * par + 512]
            h = layernorm(Yb[b], H, par, yw[b], hfree[par])
            hT, turned = transposed(H, par, h, cols[:, 27:28], cols[:, 28:29])
            hfree[par] = [turned]
            return moe_front(2, b, par, 2, src=(h, hT))

        w1g = RA[:, 0:4096].rearrange("p (e n) -> p e n", e=8)
        w2g = RA[:, 4096:8192].rearrange("p (e c n) -> p e c n", e=8, c=4)

        def play_units(us, between, alone):
            pend = None
            for i, (front, back, name) in enumerate(us):
                par = i % 2
                if name in alone:
                    pend()
                    pend = None
                    alone[name]()
                state = front(par)
                if pend:
                    pend()
                if name in between:
                    between[name]()
                pend = (lambda back=back, par=par, state=state: back(par, state))
            pend()

        def after_l0x():
            m = (pe.sem, pe.n)
            load("l1f", w1e, A["l1_w1"].rearrange("e p n -> p e n"), m)
            load("l1f", w2e, A["l1_w2"].rearrange("e (c p) n -> p e c n", p=128), m)
            load("l3x", w3, A["l3x_w"], m)
            load("l2w", S2[:, :], A["l2_w"], m)

        def mid_l0f():
            prepare(a1, w1v[:, 768:896], bias[0:NK, 512 + 128 * 5:512 + 128 * 6])

        def after_l0f():
            m = (pe.sem, pe.n)
            load("l3f", w1g, A["l3_w1"].rearrange("e p n -> p e n"), m)
            load("l3f", w2g, A["l3_w2"].rearrange("e (c p) n -> p e c n", p=128), m)

        def after_l1x():
            load("l3s", w4, A["l3s_w"], (pe.sem, pe.n))

        def before_l3x():
            l3x_masks()
            a3.ready = [loads["l3x"].all()]
            prepare(a3, w3[:, 768:896], None)

        play_units(units, {"l0f0": after_l0x, "l0f2": mid_l0f, "l1x0": after_l0f, "l1f0": after_l1x,
                           "l2f2": before_l3x}, {"l2x0": l2_prepare})
        a4.ready = [loads["l3s"].all()]
        end3 = [(pe.sem, pe.n)]
        k4["rb_free"] = end3
        for i in range(3):
            kslots.free(i, end3)
        l3_self_open(end3)
        self_attention()
        um = [(lambda par, b=b: l3m_front(b, par),
               lambda par, s, b=b: relu_back(b, par, s, w1g, w2g, b1t[:, 32:64], b2t[0:8, 128:256], loads["l3f"].all()), f"l3m{b}")
              for b in range(NB)]
        fin = Loads(sem("fin"))

        def emit_out(b):
            fin.start(sp, out[b].rearrange("(t p) d -> p t d", p=128), Xb[b].rearrange("p (t d) -> p t d", t=4), xw[b])

        um = [(f, (lambda par, s, bk=bk, b=b: (bk(par, s), emit_out(b))), n) for b, (f, bk, n) in enumerate(um)]
        play_units(um, {}, {})
        sp.wait(fin.all())

        block = ctx.enter_context(nc.Block())
        block.sync(sp.play)
        block.gpsimd(pool.play)
        block.scalar(act.play)
        block.vector(dve.play)
        block.tensor(pe.play)


def kernel(**inputs):
    import numpy as _np
    import concourse.bacc as _bacc
    from concourse import mybir as _mybir
    from concourse.bass_utils import run_bass_kernel_spmd as _run

    I = {k: _np.asarray(v) for k, v in inputs.items()}

    def rep(w):
        return _np.tile(w.reshape(128, 4, 1, 32), (1, 1, 3, 1)).reshape(128, 384)

    def repb(b):
        return _np.tile(b.reshape(4, 32).T, (4, 1))

    rows = lambda v: _np.broadcast_to(v.reshape(1, -1), (128, v.size))
    r = _np.arange(RK)[:, None]
    h = _np.arange(NH)[None, :]

    def mask(hd, hpg):
        return _np.where(r < RM, (r % 32) // hd == h % hpg, r - RM == h).astype(_np.float32)

    msk = _np.zeros((128, 32), _np.float32)
    msk[:RK, 0:16], msk[:RK, 16:32] = mask(8, 4), mask(16, 2)
    block = _np.zeros((16, 8, 16, 2, 8), _np.float32)
    for i in range(16):
        block[i, :, i, 0, :], block[i, :, i, 1, :] = 1.0, -1.0
    sign = _np.repeat(_np.tile(_np.array([1.0, -1.0], _np.float32), 128), 8)
    C = {
        "x": I["x"], "ctxT": _np.pad(I["ctx_1024"].transpose(2, 0, 1), ((0, 0), (0, 0), (0, 1))).reshape(128, CK),
        "c_ident": _np.eye(128, dtype=_np.float32), "c_mask": msk,
        "c_block": block.reshape(128, 256), "c_sign": sign[:96].reshape(96, 1), "c_signr": _np.tile(sign[:256], (NK, 1)),
        "c_tri": _np.triu(_np.ones((128, 128), _np.float32)),
        "c_rev": _np.tile(_np.arange(8, 0, -1).astype(_np.float32), (128, 4)),
        "fm_w": _np.tile(I["L0_xattn_fm_w"].T, (16, 1)), "fm_b": _np.tile(I["L0_xattn_fm_b"], 12).reshape(96, 1),
        "fm_br": _np.tile(I["L0_xattn_fm_b"], (NK, 32)), "fc_w": I["L0_xattn_fc_w"].T,
        "gates": _np.stack([I["L0_ffn_Wg"], I["L1_ffn_gate_w"].T, I["L3_ffn_gate_w"]]),
        "gateb": _np.concatenate([rows(I["L1_ffn_gate_b"]), rows(I["L3_ffn_gate_b"])], 1),
        "rows": _np.stack([rows(I[n]) for n in ("L0_xattn_fc_b", "L1_xattn_bo", "L2_ffn_b2", "L3_xattn_bproj", "L3_ffn_bo",
                                                "L1_xattn_bv", "L2_xattn_bias_v", "L3_ffn_bv")]),
        "colb": _np.concatenate([
            repb(I["L1_xattn_bq"]), repb(I["L1_xattn_bk"]), I["L2_xattn_bias_q"][:, None], I["L2_xattn_bias_k"][:, None],
            rows(I["L2_ffn_scale"].reshape(1)), I["L2_ffn_b1"].reshape(4, 128).T, repb(I["L3_ffn_bq"]), repb(I["L3_ffn_bk"]),
            I["L3_ffn_ln1_g"][:, None], I["L3_ffn_ln1_b"][:, None], I["L3_ffn_ln2_g"][:, None], I["L3_ffn_ln2_b"][:, None],
            _np.zeros((128, 11), _np.float32)], 1),
        "l0_w13": _np.concatenate([_np.concatenate([I["L0_ffn_We1"], I["L0_ffn_Ws1"][None]]),
                                   _np.concatenate([I["L0_ffn_We3"], I["L0_ffn_Ws3"][None]])], 2),
        "l0_w2": _np.concatenate([I["L0_ffn_We2"], I["L0_ffn_Ws2"][None]]),
        "l1_w": _np.concatenate([rep(I["L1_xattn_Wq"].T), rep(I["L1_xattn_Wk"].T), I["L1_xattn_Wv"].T, I["L1_xattn_Wo"].T], 1),
        "l1_w1": I["L1_ffn_w1"], "l1_w2": I["L1_ffn_w2"],
        "b1": _np.concatenate([I["L1_ffn_b1"].reshape(32, 128).T, I["L3_ffn_b1"].reshape(32, 128).T], 1),
        "b2": _np.concatenate([I["L1_ffn_b2"], I["L3_ffn_b2"]], 1),
        "l2_w": _np.concatenate([I["L2_xattn_kernel_q"][0, 0], I["L2_xattn_kernel_k"][0, 0], I["L2_xattn_kernel_v"][0, 0],
                                 I["L2_ffn_W1"].T, I["L2_ffn_W2"].T.reshape(4, 128, 128).transpose(1, 0, 2).reshape(128, 512)], 1),
        "mfT": I["mask_1xSxS2_ff0"][0].T, "mbT": I["mask_BxSxS2_bk0"].transpose(2, 0, 1).reshape(NK, 2048),
        "l3x_w": _np.concatenate([rep(I["L3_xattn_Wq"]), rep(I["L3_xattn_Wkv"][:, 0:128]), I["L3_xattn_Wkv"][:, 128:256],
                                  I["L3_xattn_Wproj"]], 1),
        "l3s_w": _np.concatenate([rep(I["L3_ffn_wq"]), rep(I["L3_ffn_wk"]), I["L3_ffn_wv"], I["L3_ffn_wo"]], 1),
        "l3_w1": I["L3_ffn_w1"], "l3_w2": I["L3_ffn_w2"],
    }
    nc = _bacc.Bacc("TRN2", target_bir_lowering=False, num_devices=1)
    arrays, aps = {}, {}
    for name, a in C.items():
        a = _np.ascontiguousarray(a)
        arrays["in_" + name] = a
        aps[name] = nc.dram_tensor("in_" + name, a.shape, _mybir.dt.from_np(a.dtype), kind="ExternalInput").ap()
    o = nc.dram_tensor("out_0", (4, 512, 128), _mybir.dt.float32, kind="ExternalOutput").ap()
    program(nc, aps, o)
    res = _run(nc, [arrays], core_ids=[0])
    return res.results[0]["out_0"]
```

```python
from contextlib import ExitStack

import numpy as np

import concourse.bass as bass
from concourse import mybir

F32 = mybir.dt.float32
F32R = mybir.dt.float32r
BF16 = mybir.dt.bfloat16
U8 = mybir.dt.uint8
I32 = mybir.dt.int32
ALU = mybir.AluOpType
ACT = mybir.ActivationFunctionType
AX = mybir.AxisListType.X

NB, S, D, NK, NH = 4, 512, 128, 77, 16
NKP = NK + 1
CK = NB * NKP
EPS = 1e-5
BIG = 1e30
CAP = 320
RM = 96
RK = 112


class Engine:

    def __init__(self, sem):
        self.sem, self.n, self.queue, self.past = sem, 0, [], {}

    def wait(self, *marks):
        for m in marks:
            if m is None:
                continue
            if isinstance(m, list):
                self.wait(*m)
                continue
            sem, value = m
            if self.past.get(sem.name, 0) < value:
                self.past[sem.name] = value
                self.queue.append(lambda e, s=sem, v=value: e.wait_ge(s, v))

    def do(self, make, *marks):
        self.wait(*marks)
        self.n += 1
        self.queue.append(lambda e, s=self.sem: make(e).then_inc(s, 1))
        return (self.sem, self.n)

    def quiet(self, make, *marks):
        self.wait(*marks)
        self.queue.append(make)

    def play(self, e):
        for make in self.queue:
            make(e)


class Loads:

    def __init__(self, sem):
        self.sem, self.n = sem, 0

    def start(self, engine, out, in_, *marks):
        engine.wait(*marks)
        self.n += 16
        engine.queue.append(lambda e, s=self.sem: e.dma_start(out, in_).then_inc(s, 16))

    def scatter(self, pool, out, idx, in_, limit, *marks):
        pool.wait(*marks)
        self.n += 16
        pool.queue.append(lambda e, s=self.sem: e.indirect_dma_start(
            out, bass.IndirectOffsetOnAxis(ap=idx, axis=0), in_, None, bounds_check=limit, oob_is_err=False).then_inc(s, 16))

    def gather(self, pool, out, in_, idx, limit, *marks):
        pool.wait(*marks)
        self.n += 16
        pool.queue.append(lambda e, s=self.sem: e.indirect_dma_start(
            out, None, in_, bass.IndirectOffsetOnAxis(ap=idx, axis=0), bounds_check=limit, oob_is_err=False).then_inc(s, 16))

    def all(self):
        return (self.sem, self.n)


class Turns:

    def __init__(self, places):
        self.places, self.read, self.order = places, [[] for _ in places], list(range(len(places)))

    def take(self):
        i = next(i for i in self.order if self.read[i] is not None)
        self.order.remove(i)
        self.order.append(i)
        marks, self.read[i] = self.read[i], None
        return i, marks

    def take_pair(self):
        i = next(i for i in self.order if i % 2 == 0 and self.read[i] is not None and self.read[i + 1] is not None)
        marks = self.read[i] + self.read[i + 1]
        for k in (i, i + 1):
            self.order.remove(k)
            self.order.append(k)
            self.read[k] = None
        return i, marks

    def free(self, i, *marks):
        self.order.remove(i)
        self.order.append(i)
        self.read[i] = list(marks)


class Slots(Turns):
    def take(self):
        i, marks = super().take()
        return i, self.places[i], marks


def together(*streams):
    out, at, live = [None] * len(streams), [0] * len(streams), set(range(len(streams)))
    while live:
        k = min(live, key=lambda i: (at[i] / streams[i][1], i))
        try:
            next(streams[k][0])
            at[k] += 1
        except StopIteration as stop:
            out[k] = stop.value
            live.remove(k)
    return out


def alone_(stream):
    return together((stream, 1))[0]


def program(nc, A, out):
    with ExitStack() as ctx:
        def sb(name, cols, dt=F32):
            return ctx.enter_context(nc.sbuf_tensor(name, [128, cols], dt))

        def sem(name):
            return ctx.enter_context(nc.semaphore(name))

        PS = ctx.enter_context(nc.psum_tensor("PS", [128, 8, 512], F32))
        banks = Turns(list(range(6)))
        acc_bank = Slots([6, 7])

        pe, act, dve, pool, sp = (Engine(sem(n)) for n in ("pe", "act", "dve", "pool", "sp"))
        loads = {}

        def load(name, dst, src, *marks, by=None):
            if name not in loads:
                loads[name] = Loads(sem("ld_" + name))
            loads[name].start(by or sp, dst, src, *marks)

        X = sb("X", NB * 512)
        Xb = [X[:, 512 * b:512 * b + 512] for b in range(NB)]
        RA = sb("RA", 8192)
        with nc.sbuf_tensor("Q0", [128, 8192], F32R) as Q0t:
            Q0 = [Q0t[:, 0:4096], Q0t[:, 4096:8192]]
        RB = sb("RB", 8192)
        S0 = sb("S0", 1280)
        S1 = sb("S1", 1024)
        S2 = sb("S2", 1408)
        QB = ctx.enter_context(nc.sbuf_tensor("QB", [128, 2 * 2048], F32R))
        KB = ctx.enter_context(nc.sbuf_tensor("KB", [128, 3 * 2048], F32R))
        STG = ctx.enter_context(nc.sbuf_tensor("STG", [128, 2 * 512], F32R))
        MX = ctx.enter_context(nc.sbuf_tensor("MX", [128, 2 * 4 * RK], F32R))
        MT = ctx.enter_context(nc.sbuf_tensor("MT", [128, 512], F32R))
        VB = sb("VB", 2048)
        Ht = sb("Ht", 2 * 512)
        HT = sb("HT", 2 * 512)
        PT = sb("PT", 10 * 512)
        OT = sb("OT", 2048)
        ON = sb("ON", 2 * 256)
        OC = sb("OC", 1024)
        CT = sb("CT", CK)
        ident = sb("ident", 128)
        tri = sb("tri", 128)
        ones = sb("ones", 128)
        msk = sb("msk", 2 * NH)
        rev = sb("rev", 32)
        bias = sb("bias", 8 * 128)
        b1t = sb("b1t", 64)
        b2t = sb("b2t", 256)
        cols = sb("cols", 40)
        st = sb("st", 2 * 24)
        mv = sb("mv", 2 * 8)
        ve = sb("ve", 2 * 8)
        nh = sb("nh", 4)
        rt = sb("rt", 2 * 512)
        den = sb("den", 2 * 64)
        negI = ctx.enter_context(nc.sbuf_tensor("negI", [128, 4 * NK + 4], BF16))
        mkb = ctx.enter_context(nc.sbuf_tensor("mkb", [128, 4 * 512], BF16))
        mk8 = ctx.enter_context(nc.sbuf_tensor("mk8", [128, 4 * 512], U8))
        mkf = RB[:, 4096:4608]
        gates = sb("gates", 24)
        prev = sb("prev", 8 * 17)
        off1 = sb("off1", 32)
        ints = ctx.enter_context(nc.sbuf_tensor("ints", [128, 64], I32))
        keep = sb("keep", 64)
        dbuf = nc.dram_tensor("dbuf", (8 * CAP, 128), F32, kind="Internal").ap()
        dout = nc.dram_tensor("dout", (8 * CAP, 128), F32, kind="Internal").ap()
        b2r = VB[:, 0:1024]

        pt = Slots([PT[:, 512 * i:512 * i + 512] for i in range(10)])
        stg = Slots([STG[:, 512 * i:512 * i + 512] for i in range(2)])

        load("c", ident[:, :], A["c_ident"])
        load("x0", X[:, 0:512].rearrange("p (t d) -> p t d", t=4), A["x"][0].rearrange("(t p) d -> p t d", p=128))
        load("c", msk[:, :], A["c_mask"])
        load("ctx", CT[:, :], A["ctxT"])
        load("l0", S0[:, 512:520], A["fm_w"])
        load("l0", S0[:, 768:1024], A["c_block"])
        load("l0", S0[:, 1024:1280].rearrange("p (c n) -> p c n", c=2), A["fc_w"].rearrange("(c p) n -> p c n", p=128))
        load("l0", cols[0:96, 0:1], A["fm_b"])
        load("l0", cols[0:96, 1:2], A["c_sign"])
        load("l0", OC[0:NK, 0:256], A["fm_br"])
        load("l0", OC[0:NK, 256:512], A["c_signr"])
        for b in range(1, NB):
            load(f"x{b}", Xb[b].rearrange("p (t d) -> p t d", t=4), A["x"][b].rearrange("(t p) d -> p t d", p=128))
        load("c2", tri[:, :], A["c_tri"])
        load("c2", rev[:, :], A["c_rev"])
        load("c2", gates[:, :].rearrange("p (l e) -> p l e", l=3), A["gates"].rearrange("l p e -> p l e"))
        load("rb", bias[:, 0:1024].rearrange("p (r d) -> p r d", r=8), A["rows"].rearrange("r p d -> p r d"))
        load("cb", cols[:, 2:40], A["colb"])
        load("rb", rt[:, 960:976], A["gateb"])

        W13 = RA[:, 0:9 * 512].rearrange("p (e n) -> p e n", e=9)
        W2m = RA[:, 9 * 512:9 * 512 + 9 * 256].rearrange("p (e c n) -> p e c n", e=9, c=2)
        load("l0f", W13, A["l0_w13"].rearrange("e p n -> p e n"))
        load("l0f", W2m, A["l0_w2"].rearrange("e (c p) n -> p e c n", p=128))
        load("l1", S1[:, :], A["l1_w"])
        load("l2", mk8[0:NK, :], A["mbT"])
        load("l2", b1t[:, :], A["b1"])
        load("l2", b2t[0:8, :], A["b2"])
        load("c2", off1[:, :], A["c_off"])

        ready_c = loads["c"].all()
        k_zero = dve.do(lambda e: e.memset(OT[:, :], 0.0))
        for i in range(2):
            load("zero", dbuf[1280 * i:1280 * i + 1280, :].rearrange("(p t) d -> p (t d)", p=128), OT[:, 0:1280], k_zero)

        k = pool.do(lambda e: e.memset(nh[:, :], -0.5))
        k_nh = k
        k_ones = pool.do(lambda e: e.memset(ones[:, :], 1.0))
        k_mx = dve.do(lambda e: e.memset(MX[:, :].bitcast(F32), 0.0))
        k_stg = dve.do(lambda e: e.memset(STG[:, :].bitcast(F32), -1.0))
        k_prev = pool.do(lambda e: e.memset(prev[:, 0:8], 0.0))
        for i in range(2):
            stg.free(i, k_stg)

        xw = [[loads[f"x{b}"].all()] for b in range(NB)]
        yw = [[] for _ in range(NB)]
        hfree = [[], []]
        htfree = [[], []]
        qfree = [[], []]
        mxfree = [[k_mx], [k_mx]]
        rtfree = [[], []]
        mtfree = []
        kfree = []
        vfree = []
        mq = [Loads(sem("mq0")), Loads(sem("mq1"))]

        def mm(o, l, r, first=True, last=True):
            return lambda e: e.matmul(o, l, r, start=first, stop=last, skip_group_check=True)

        def layernorm(src, dst, par, src_marks, dst_marks):
            s6 = st[:, 24 * par:24 * par + 24]
            s2 = mv[:, 8 * par:8 * par + 8].rearrange("p (t c) -> p t c", t=4)
            v4 = ve[:, 8 * par:8 * par + 4]
            r4 = ve[:, 8 * par + 4:8 * par + 8]
            for t in range(4):
                m = dve.do(lambda e, t=t: e.bn_stats(s6[:, 6 * t:6 * t + 6], src[:, 128 * t:128 * t + 128]), src_marks)
            yield
            for t in range(4):
                m = dve.do(lambda e, t=t: e.bn_aggr(s2[:, t, :], s6[:, 6 * t:6 * t + 6]), m)
            m = dve.do(lambda e: e.tensor_scalar(v4, s2[:, :, 1], EPS, None, ALU.add), m)
            m = pool.do(lambda e: e.tensor_tensor(r4, v4, nh[:, :], ALU.pow), m, k_nh)
            yield
            yield
            for t in range(4):
                m2 = dve.do(lambda e, t=t: e.tensor_scalar(dst[:, 128 * t:128 * t + 128], src[:, 128 * t:128 * t + 128],
                                                           s2[:, t, 0:1], r4[:, t:t + 1], ALU.subtract, ALU.mult),
                            m, dst_marks)
            yield
            return m2

        def transposed(src, par, ready, scale=None, shift=None):
            b, marks = banks.take()
            for t in range(4):
                f = (lambda e, t=t: e.transpose(PS[:, b, 128 * t:128 * t + 128], src[:, 128 * t:128 * t + 128], ident[:, :]))
                if t < 3:
                    pe.quiet(f, ready, ready_c, marks)
                else:
                    turned = pe.do(f)
            yield
            dst = HT[:, 512 * par:512 * par + 512]
            if scale is None:
                m = act.do(lambda e: e.activation(dst, PS[:, b, :], ACT.Copy), turned, htfree[par])
            else:
                m = act.do(lambda e: e.activation(dst, PS[:, b, :], ACT.Identity, bias=shift, scale=scale),
                           turned, htfree[par], loads["cb"].all())
            htfree[par] = None
            banks.free(b, m)
            yield
            return m, turned

        def ln_front(b, par, scale=None, shift=None):
            H = Ht[:, 512 * par:512 * par + 512]
            h = yield from layernorm(Xb[b], H, par, xw[b], hfree[par])
            hT, turned = yield from transposed(H, par, h, scale, shift)
            hfree[par] = [turned]
            return h, hT

        def add_row(b, row, h):
            r = bias[:, 128 * row:128 + 128 * row].rearrange("p (o d) -> p o d", o=1).broadcast_to((128, 4, 128))
            x = Xb[b].rearrange("p (t d) -> p t d", t=4)
            m = pool.do(lambda e: e.tensor_tensor(x, x, r, ALU.add), h, xw[b], loads["rb"].all())
            xw[b] = [m]

        class Att:
            def __init__(self, n, hpg, vd, scale, wq, wk, bq, bk, wo, ready, row, expo=False, mask=False, bqm=None):
                self.n, self.hpg, self.vd, self.scale = n, hpg, vd, scale
                self.wq, self.wk, self.bq, self.bk, self.wo = wq, wk, bq, bk, wo
                self.ready, self.row, self.expo, self.mask = ready, row, expo, mask
                self.ng = NH // hpg

        def split(a, src_bank, n, out, part, bq, marks_ps, marks_out):
            P = PS[:, src_bank, 0:n]
            if a.expo:
                i, E, em = pt.take()
                m = act.do(lambda e: e.activation(E[0:96, 0:n], P[0:96, :], ACT.Exp, bias=bq, scale=1.0), marks_ps, em, a.ready)
                banks.free(src_bank, m)
                yield
                m1 = dve.do(lambda e: e.tensor_copy(out[0:96, :], E[0:96, 0:n]), m, marks_out)
                m2 = dve.do(lambda e: e.tensor_tensor(out[part:part + 32, :], E[part:part + 32, 0:n],
                                                      out[part:part + 32, :].bitcast(F32), ALU.subtract), m1)
                pt.free(i, m2)
                yield
                return m2
            if bq is None:
                m1 = act.do(lambda e: e.activation(out[0:96, :], P[0:96, :], ACT.Copy), marks_ps, marks_out)
                yield
                m2 = dve.do(lambda e: e.tensor_tensor(out[part:part + 32, :], P[part:part + 32, :],
                                                      out[part:part + 32, :].bitcast(F32), ALU.subtract), m1)
            else:
                m1 = act.do(lambda e: e.activation(out[0:96, :], P[0:96, :], ACT.Identity, bias=bq, scale=1.0),
                            marks_ps, marks_out, loads["cb"].all())
                yield
                m2 = dve.do(lambda e: e.scalar_tensor_tensor(out[part:part + 32, :], P[part:part + 32, :],
                                                             bq[part:part + 32, :],
                                                             out[part:part + 32, :].bitcast(F32),
                                                             ALU.add, ALU.subtract), m1)
            banks.free(src_bank, m2)
            yield
            return m2

        def keys(a, g, n, rhs, rhs_marks, kblk, k_marks):
            b, marks = banks.take()
            m = pe.do(mm(PS[0:96, b, 0:n], a.wk[:, g, :], rhs), marks, rhs_marks, a.ready)
            yield
            i, sg, sm = stg.take()
            m = yield from split(a, b, n, sg[:, 0:n], 64, a.bk(g), [m], sm)
            mk = msk[0:RK, 0:16] if a.hpg == 4 else msk[0:RK, 16:32]
            for hh in range(a.hpg):
                h = g * a.hpg + hh
                if hh % 2:
                    ma = act.do(lambda e, hh=hh, h=h: e.activation(kblk(hh)[0:RK, :], sg[0:RK, 0:n].bitcast(F32), ACT.Copy,
                                                                   scale=mk[:, h:h + 1]), m, k_marks, ready_c)
                else:
                    md = dve.do(lambda e, hh=hh, h=h: e.tensor_scalar(kblk(hh)[0:RK, :], sg[0:RK, 0:n].bitcast(F32),
                                                                      mk[:, h:h + 1], None, ALU.mult), m, k_marks, ready_c)
            stg.free(i, ma, md)
            yield
            return [ma, md]

        def queries(a, g, par, hT, qs):
            b, marks = banks.take()
            m = pe.do(mm(PS[0:96, b, :], a.wq[:, g, :], HT[:, 512 * par:512 * par + 512]), marks, hT, a.ready)
            yield
            m2 = yield from split(a, b, 512, qs(g), 32, a.bq(g), [m], qfree[par])
            return m2, m

        def row_maxima(par, reduced, qs, groups, q_marks):
            nonlocal mtfree
            b, marks = banks.take()
            M = MX[:, 4 * RK * par:4 * RK * par + 4 * RK].rearrange("p (t c) -> p t c", t=4).bitcast(F32)
            for t in range(4):
                f = (lambda e, t=t: e.transpose(PS[0:RK, b, 128 * t:128 * t + 128], M[:, t, :], ident[:, :]))
                if t < 3:
                    pe.quiet(f, marks, reduced)
                else:
                    m = pe.do(f)
            yield
            m = dve.do(lambda e: e.tensor_copy(MT[RM:RK, :], PS[RM:RK, b, :]), m, mtfree)
            banks.free(b, m)
            for g in groups:
                mq[par].start(sp, qs(g)[RM:RK, :].bitcast(F32), MT[RM:RK, :].bitcast(F32), m, q_marks)
            mtfree = [mq[par].all()]
            yield
            return mq[par].all()

        ot_free = [[loads["zero"].all()] for _ in range(4)]
        oc_free = []
        on = Slots([ON[:, 0:256], ON[:, 256:512]])

        def finish(a, par, ot_marks, dst, dst_marks, extra=None):
            nonlocal oc_free
            vd = a.vd
            nc2 = NH * vd // 128
            cb = []
            for c in range(nc2):
                i, o, om = acc_bank.take()
                cb.append((o, om, i))
            for j in range(4):
                b, marks = banks.take()
                for hg in range(4):
                    f = (lambda e, hg=hg, b=b, j=j: e.transpose(PS[:, b, 128 * hg:128 * hg + 128],
                                                                OT[:, 512 * hg + 128 * j:512 * hg + 128 * j + 128], ident[:, :]))
                    if hg < 3:
                        pe.quiet(f, marks, ot_marks)
                    else:
                        m = pe.do(f)
                yield
                O = PS[:, b, :].rearrange("p (h c) -> p h c", c=32)
                R = den[:, 64 * par + 16 * j:64 * par + 16 * j + 16]
                if extra is None:
                    m = dve.do(lambda e, R=R, O=O: e.reciprocal(R, O[:, :, vd]), m)
                else:
                    m = dve.do(lambda e, R=R, O=O, j=j: e.tensor_tensor(R, O[:, :, vd], extra[0](j), ALU.add), m, extra[1])
                    m = dve.do(lambda e, R=R: e.reciprocal(R, R), m)
                i, N, nm = on.take()
                m = dve.do(lambda e, N=N, O=O, R=R: e.tensor_tensor(
                    N[:, 0:NH * vd].rearrange("p (h c) -> p h c", c=vd), O[:, :, 0:vd],
                    R.rearrange("p (h o) -> p h o", o=1).broadcast_to((128, NH, vd)), ALU.mult), m, nm)
                banks.free(b, m)
                yield
                for c in range(nc2):
                    m2 = pe.do(lambda e, c=c, j=j, N=N: e.transpose(PS[:, cb[c][0], 128 * j:128 * j + 128],
                                                                    N[:, 128 * c:128 * c + 128], ident[:, :]), m, cb[c][1])
                on.free(i, m2)
                yield
            for hg in range(4):
                ot_free[hg] = [m2]
            done = []
            for c in range(nc2):
                m = act.do(lambda e, c=c: e.activation(OC[:, 512 * c:512 * c + 512], PS[:, cb[c][0], :], ACT.Copy), m2, oc_free)
                acc_bank.free(cb[c][2], m)
            yield
            b, marks = banks.take()
            for j in range(4):
                for c in range(nc2):
                    f = mm(PS[:, b, 128 * j:128 * j + 128], OC[:, 512 * c + 128 * j:512 * c + 128 * j + 128], a.wo[:, c, :],
                           c == 0, c == nc2 - 1)
                    if j < 3 or c < nc2 - 1:
                        pe.quiet(f, m, marks, a.ready)
                    else:
                        m2 = pe.do(f, m, marks)
            oc_free = [m2]
            yield
            m = dve.do(lambda e, b=b: e.tensor_tensor(dst, dst, PS[:, b, :], ALU.add), m2, dst_marks)
            banks.free(b, m)
            return m

        kall = KB[:, 0:NH * CK].rearrange("p (h k) -> p h k", h=NH)
        vall = VB[:, :].rearrange("p (b h c) -> p b h c", b=4, h=16)

        def prepare(a, wv, bvrow, bv_sign=None):
            nonlocal kfree, vfree
            kf, vf = kfree, vfree
            kfree, vfree = None, None
            a.kd = []
            for g in range(a.ng):
                m = yield from keys(a, g, CK, CT[:, :], loads["ctx"].all(), lambda hh, g=g: kall[:, g * a.hpg + hh, :], kf)
                a.kd.append(m)
            vd = a.vd
            vz = VB[0:NK, :].rearrange("p (g c) -> p g c", c=32)
            m0 = dve.do(lambda e: e.memset(vz[:, :, vd + 1:32], 0.0), vf)
            m0 = dve.do(lambda e: e.memset(vz[:, :, vd:vd + 1], 1.0), vf)
            n = NH * vd
            a.vd_marks = [m0]
            for b in range(NB):
                k, marks = banks.take()
                m = pe.do(mm(PS[0:NK, k, 0:n], CT[:, NKP * b:NKP * b + NK], wv), marks, loads["ctx"].all(), a.ready)
                yield
                src = PS[0:NK, k, 0:n].rearrange("p (h c) -> p h c", c=vd)
                dst = vall[0:NK, b, :, 0:vd]
                if a.expo:
                    i, E, em = pt.take()
                    m = dve.do(lambda e, E=E, k=k: e.tensor_tensor(E[0:NK, 0:n], PS[0:NK, k, 0:n], bvrow, ALU.add), m, em)
                    banks.free(k, m)
                    m = act.do(lambda e, E=E, dst=dst: e.activation(dst, E[0:NK, 0:n].rearrange("p (h c) -> p h c", c=vd), ACT.Exp),
                               m, vf)
                    pt.free(i, m)
                elif bvrow is None:
                    m = dve.do(lambda e, dst=dst, src=src: e.tensor_copy(dst, src), m, vf)
                    banks.free(k, m)
                else:
                    m = dve.do(lambda e, dst=dst, src=src: e.tensor_tensor(dst, src, bvrow.rearrange("p (h c) -> p h c", c=vd), ALU.add),
                               m, vf, loads["rb"].all())
                    banks.free(k, m)
                a.vd_marks.append(m)
                yield

        def cross_front(a, b, par, qbuf):
            h, hT = yield from ln_front(b, par)
            add_row(b, a.row, h)
            qs = lambda g: qbuf[par][:, 512 * g:512 * g + 512]
            qm = []
            for g in range(a.ng):
                m, read = yield from queries(a, g, par, hT, qs)
                qm.append(m)
            htfree[par] = [read]
            M = MX[:, 4 * RK * par:4 * RK * par + 4 * RK].rearrange("p (t c) -> p t c", t=4)
            per = 1 if a.hpg == 4 else 3
            nr = a.hpg * NKP
            for t in range(4):
                for g0 in range(0, a.ng, per):
                    gs = range(g0, min(g0 + per, a.ng))
                    k, marks = banks.take()
                    for g in gs:
                        o = PS[:, k, nr * (g - g0):nr * (g - g0) + nr]
                        l = qs(g)[0:RM, 128 * t:128 * t + 128]
                        r = kall[0:RM, g * a.hpg:(g + 1) * a.hpg, NKP * b:NKP * b + NKP]
                        if a.mask:
                            pe.quiet(mm(o, l, r, True, False), marks, qm[g], a.kd[g])
                            m = pe.do(mm(o.rearrange("p (h k) -> p h k", k=NKP)[:, :, 0:NK], mkb[0:NK, 512 * b + 128 * t:512 * b + 128 * t + 128],
                                         negI[0:NK, 0:4 * NK], False, True), a.mask_ready)
                        else:
                            m = pe.do(mm(o, l, r), marks, qm[g], a.kd[g])
                    yield
                    nh_ = len(gs) * a.hpg
                    src = PS[:, k, 0:nh_ * NKP].rearrange("p (h k) -> p h k", k=NKP)[:, :, 0:NK]
                    dst = M[:, t, RM + g0 * a.hpg:RM + g0 * a.hpg + nh_]
                    m = dve.do(lambda e, dst=dst, src=src: e.tensor_reduce(dst, src, AX, ALU.max), m, mxfree[par])
                    banks.free(k, m)
            extra = None
            if a.mask:
                m = dve.do(lambda e: e.tensor_scalar(M[:, :, RM:RK], M[:, :, RM:RK].bitcast(F32), 0.0, None, ALU.max), m)
                X1 = rt[:, 512 * par:512 * par + 64].rearrange("p (t h) -> p t h", t=4)
                me = act.do(lambda e: e.activation(X1, M[:, :, RM:RK].bitcast(F32), ACT.Exp, bias=0.0, scale=-a.scale), m, rtfree[par])
                rtfree[par] = None
                extra = (lambda j: X1[:, j, :], me)
            mt = yield from row_maxima(par, m, qs, range(a.ng), qfree[par])
            mxfree[par] = [(pe.sem, pe.n)] + ([extra[1]] if extra else [])
            qfree[par] = None
            return qs, qm, mt, extra

        def cross_back(a, b, par, state):
            nonlocal kfree, vfree
            qs, qm, mt, extra = state
            ot = []
            wait_exp = []

            def scores(hg):
                res = []
                for i in range(4):
                    h = 4 * hg + i
                    g = h // a.hpg
                    k, marks = banks.take()
                    l = kall[0:RK, h, NKP * b:NKP * b + NK]
                    if a.mask:
                        pe.quiet(mm(PS[0:NK, k, :], l, qs(g)[0:RK, :], True, False), marks, mt, qm[g], a.kd[g])
                        m = pe.do(mm(PS[0:NK, k, :], negI[0:NK, 0:NK], mkb[0:NK, 512 * b:512 * b + 512], False, True), a.mask_ready)
                    else:
                        m = pe.do(mm(PS[0:NK, k, :], l, qs(g)[0:RK, :]), marks, mt, qm[g], a.kd[g])
                    s, P, pm = pt.take()
                    m = act.do(lambda e, P=P, k=k: e.activation(P[0:NK, :], PS[0:NK, k, :], ACT.Exp, bias=0.0, scale=a.scale), m, pm)
                    banks.free(k, m)
                    res.append((h, s, P, m))
                    yield
                return res

            def values(hg, res):
                i6, o, om = acc_bank.take()
                for i, (h, s, P, m) in enumerate(res):
                    f = mm(PS[32 * i:32 * i + 32, o, :], vall[0:NK, b, h, :], P[0:NK, :])
                    if i < 3:
                        pe.quiet(f, [r[3] for r in res], om, a.vd_marks)
                    else:
                        m = pe.do(f)
                yield
                for (h, s, P, _) in res:
                    pt.free(s, m)
                m = dve.do(lambda e, o=o: e.tensor_copy(OT[:, 512 * hg:512 * hg + 512], PS[:, o, :]), m, ot_free[hg])
                acc_bank.free(i6, m)
                ot.append(m)

            last = yield from scores(0)
            for hg in range(4):
                nxt = (yield from scores(hg + 1)) if hg < 3 else None
                yield from values(hg, last)
                last = nxt
            qfree[par] = [(pe.sem, pe.n)]
            kfree = [(pe.sem, pe.n)]
            vfree = [(pe.sem, pe.n)]
            m = yield from finish(a, par, ot, Xb[b], xw[b], extra)
            if extra:
                rtfree[par] = [m]
            xw[b] = [m]

        def route_common(L, par, k0, lm):
            R = rt[:, 512 * par + k0:512 * par + k0 + 128]
            v = R[:, 0:4]
            r = R[:, 8:40].rearrange("p (t e) -> p t e", t=4)
            mx = R[:, 4:8]
            oh = R[:, 40:72].rearrange("p (t e) -> p t e", t=4)
            m = dve.do(lambda e: e.tensor_reduce(v, L, AX, ALU.max), lm)
            yield
            vb = v.rearrange("p (t o) -> p t o", o=1).broadcast_to((128, 4, 8))
            m = dve.do(lambda e: e.tensor_tensor(r, L, vb, ALU.is_equal), m)
            yield
            m = dve.do(lambda e: e.tensor_tensor(r, r, rev[:, :].rearrange("p (t e) -> p t e", t=4), ALU.mult), m, loads["c2"].all())
            yield
            m = dve.do(lambda e: e.tensor_reduce(mx, r, AX, ALU.max), m)
            yield
            m = dve.do(lambda e: e.tensor_tensor(oh, r, mx.rearrange("p (t o) -> p t o", o=1).broadcast_to((128, 4, 8)), ALU.is_equal), m)
            yield
            return v, oh, m

        def moe_front(kind, b, par, li, scale=None, shift=None, src=None):
            if src is None:
                h, hT = yield from ln_front(b, par)
            else:
                h, hT = src
            G = gates[:, 8 * li:8 * li + 8]
            hv = HT[:, 512 * par:512 * par + 512]
            k, marks = banks.take()
            for t in range(4):
                f = mm(PS[:, k, 8 * t:8 * t + 8], hv[:, 128 * t:128 * t + 128], G)
                if t < 3:
                    pe.quiet(f, marks, hT, loads["c2"].all())
                else:
                    m = pe.do(f)
            yield
            Rt = rt[:, 512 * par:512 * par + 448]
            L = Rt[:, 0:32].rearrange("p (t e) -> p t e", t=4)
            W = Rt[:, 32:68].rearrange("p (t e) -> p t e", t=4)
            psl = PS[:, k, 0:32].rearrange("p (t e) -> p t e", t=4)
            if kind == 0:
                m = dve.do(lambda e: e.tensor_copy(L, psl), m, rtfree[par])
                yield
            else:
                gb = rt[:, 960 + 8 * (kind - 1):968 + 8 * (kind - 1)].rearrange("p (o e) -> p o e", o=1).broadcast_to((128, 4, 8))
                m = dve.do(lambda e: e.tensor_tensor(L, psl, gb, ALU.add), m, rtfree[par], loads["rb"].all())
                yield
            banks.free(k, m)
            v1, oh1, m = yield from route_common(L, par, 80, m)
            W8 = W[:, :, 0:8]
            bc = lambda ap: ap.rearrange("p (t o) -> p t o", o=1).broadcast_to((128, 4, 8))
            wT = None
            if kind == 0:
                L2 = Rt[:, 352:384].rearrange("p (t e) -> p t e", t=4)
                m = dve.do(lambda e: e.scalar_tensor_tensor(L2, oh1, -BIG, L, ALU.mult, ALU.add), m)
                yield
                v2, oh2, m = yield from route_common(L2, par, 208, m)
                gv = Rt[:, 384:392]
                T = Rt[:, 392:404]
                m = dve.do(lambda e: e.tensor_copy(gv[:, 0:4], v1), m)
                yield
                m = dve.do(lambda e: e.tensor_copy(gv[:, 4:8], v2), m)
                yield
                m = act.do(lambda e: e.activation(gv, gv, ACT.Exp, bias=0.0, scale=-1.0), m)
                yield
                m = dve.do(lambda e: e.tensor_scalar(gv, gv, 1.0, None, ALU.add), m)
                yield
                m = dve.do(lambda e: e.reciprocal(gv, gv), m)
                yield
                m = dve.do(lambda e: e.tensor_tensor(T[:, 0:4], gv[:, 0:4], gv[:, 4:8], ALU.add), m)
                yield
                m = dve.do(lambda e: e.tensor_scalar(T[:, 0:4], T[:, 0:4], 3.0, None, ALU.mult), m)
                yield
                m = dve.do(lambda e: e.reciprocal(T[:, 4:8], T[:, 0:4]), m)
                yield
                m = dve.do(lambda e: e.tensor_tensor(gv.rearrange("p (a t) -> p a t", a=2), gv.rearrange("p (a t) -> p a t", a=2),
                                                     T[:, 4:8].rearrange("p (o t) -> p o t", o=1).broadcast_to((128, 2, 4)), ALU.mult), m)
                m = dve.do(lambda e: e.tensor_tensor(W8, oh1, bc(gv[:, 0:4]), ALU.mult), m)
                yield
                m = dve.do(lambda e: e.tensor_tensor(L2, oh2, bc(gv[:, 4:8]), ALU.mult), m)
                yield
                m = dve.do(lambda e: e.tensor_tensor(W8, W8, L2, ALU.add), m)
                yield
                m = dve.do(lambda e: e.memset(W[:, :, 8:9], 1.0 / 3.0), m)
                yield
            elif kind == 1:
                E = Rt[:, 352:384].rearrange("p (t e) -> p t e", t=4)
                P1 = Rt[:, 384:392]
                me = dve.do(lambda e: e.tensor_tensor(E, L, bc(v1), ALU.subtract), m)
                yield
                me = act.do(lambda e: e.activation(E, E, ACT.Exp), me)
                yield
                me = dve.do(lambda e: e.tensor_reduce(P1[:, 0:4], E, AX, ALU.add), me)
                yield
                me = dve.do(lambda e: e.reciprocal(P1[:, 4:8], P1[:, 0:4]), me)
                yield
                pv = prev[:, 32 * b:32 * b + 40]
                mp = m
                for t in range(4):
                    mp = dve.do(lambda e, t=t: e.tensor_tensor(pv[:, 8 * t + 8:8 * t + 16], pv[:, 8 * t:8 * t + 8], oh1[:, t, :], ALU.add), mp, k_prev)
                k, marks = banks.take()
                ohf = Rt[:, 120:152]
                pe.quiet(mm(PS[:, k, 0:32], tri[:, :], ohf, True, False), marks, m, loads["c2"].all())
                m = pe.do(mm(PS[:, k, 0:32], ones[:, :], pv[:, 0:32], False, True), mp, k_ones)
                psl2 = PS[:, k, 0:32].rearrange("p (t e) -> p t e", t=4)
                C = Rt[:, 400:432].rearrange("p (t e) -> p t e", t=4)
                C2 = Rt[:, 208:240].rearrange("p (t e) -> p t e", t=4)
                off = off1[:, :].rearrange("p (t e) -> p t e", t=4)
                mc = dve.do(lambda e: e.tensor_tensor(C, psl2, off, ALU.add), m, loads["c2"].all())
                mc = dve.do(lambda e: e.tensor_scalar(C2, psl2, CAP + 0.5, 10000.0, ALU.is_gt, ALU.mult), mc)
                mc = dve.do(lambda e: e.tensor_tensor(C, C, C2, ALU.add), mc)
                mc = dve.do(lambda e: e.tensor_tensor(C, C, oh1, ALU.mult), mc)
                yield
                mc = dve.do(lambda e: e.tensor_reduce(Rt[:, 440:444], C, AX, ALU.add), mc)
                mi = dve.do(lambda e: e.tensor_copy(ints[:, 4 * b:4 * b + 4], Rt[:, 440:444]), mc)
                mi = dve.do(lambda e: e.tensor_scalar(Rt[:, 444:448], Rt[:, 440:444], 8.0 * CAP - 1.0, None, ALU.min), mi)
                mi = dve.do(lambda e: e.tensor_copy(ints[:, 16 + 4 * b:20 + 4 * b], Rt[:, 444:448]), mi)
                yield
                for t in range(4):
                    sc1[b].scatter(pool, dbuf, ints[:, 4 * b + t:4 * b + t + 1], Ht[:, 512 * par + 128 * t:512 * par + 128 * t + 128],
                                8 * CAP - 1, mi, h, loads["zero"].all())
                hfree[par] = hfree[par] + [sc1[b].all()]
                m = dve.do(lambda e: e.scalar_tensor_tensor(W8, psl2, CAP + 0.5, oh1, ALU.is_le, ALU.mult), m)
                yield
                banks.free(k, m)
                m = dve.do(lambda e: e.tensor_reduce(keep[:, 4 * b:4 * b + 4], W8, AX, ALU.add), m)
                m = dve.do(lambda e: e.tensor_tensor(keep[:, 4 * b:4 * b + 4], keep[:, 4 * b:4 * b + 4], P1[:, 4:8], ALU.mult), m, me)
                k1["slot", b], k1["w", b] = mi, m
                rtfree[par] = [m, mi]
                htfree[par] = [(pe.sem, pe.n)]
                return None
                yield
            else:
                m = dve.do(lambda e: e.tensor_copy(W8, oh1), m)
                yield
            if kind:
                k, marks = banks.take()
                for t in range(4):
                    f = (lambda e, t=t, k=k: e.transpose(PS[0:8, k, 128 * t:128 * t + 128], W8[:, t, :], ident[:, :]))
                    if t < 3:
                        pe.quiet(f, marks, m)
                    else:
                        mw = pe.do(f)
                wT = Ht[0:8, 512 * par:512 * par + 512]
                mw = act.do(lambda e, k=k: e.activation(wT, PS[0:8, k, :], ACT.Copy), mw, hfree[par])
                banks.free(k, mw)
                hfree[par] = None
                rtfree[par] = None
                return hT, W, m, wT, mw
            rtfree[par] = None
            return hT, W, m, None, None

        sc1 = [Loads(sem(f"sc1{b}")) for b in range(NB)]
        ex = [Loads(sem("exa")), Loads(sem("exb"))]
        eo = [Loads(sem("eoa")), Loads(sem("eob"))]
        gq = [Loads(sem("gqa")), Loads(sem("gqb"))]
        k1 = {}
        gfree = [[], []]

        def capacity_experts():
            nonlocal oc_free
            raws, outs = Slots([OT[:, 0:512], OT[:, 512:1024]]), Slots([OT[:, 1024:1536], OT[:, 1536:2048]])
            for i in range(2):
                raws.free(i, ot_free[i])
                outs.free(i, ot_free[2 + i])
            xts = Slots([OC[:, 0:512], OC[:, 512:1024]])
            xts.free(0, oc_free)
            xts.free(1, oc_free)
            rdy = loads["l1f"].all()
            P3 = [(0, 128), (128, 128), (256, 64)]

            def fetch(x):
                i, raw, rm = raws.take()
                q = ex[x % 2]
                q.start(sp, raw[:, 0:256].rearrange("p (t d) -> p t d", t=2),
                        dbuf[CAP * x:CAP * x + 256, :].rearrange("(t p) d -> p t d", p=128), [s.all() for s in sc1], rm)
                q.start(sp, raw[0:64, 256:384], dbuf[CAP * x + 256:CAP * x + CAP, :])
                return i, raw, q.all()

            def turn(i, raw, rm):
                k, m1 = banks.take()
                for n, (a, w) in enumerate(P3):
                    f = (lambda e, a=a, w=w, n=n: e.transpose(PS[:, k, a:a + w], raw[0:w, 128 * n:128 * n + 128], ident[0:w, 0:w]))
                    if n < 2:
                        pe.quiet(f, m1, rm)
                    else:
                        m = pe.do(f)
                raws.free(i, m)
                j, xt, xm = xts.take()
                m = dve.do(lambda e: e.tensor_copy(xt[:, 0:CAP], PS[:, k, 0:CAP]), m, xm)
                banks.free(k, m)
                yield
                return j, xt, m

            def up(x, j, xt, xm):
                res = []
                for c in range(4):
                    k, m1 = banks.take()
                    m = pe.do(mm(PS[:, k, 0:CAP], w1e[:, x, 128 * c:128 * c + 128], xt[:, 0:CAP]), m1, xm, rdy)
                    s, P, pm = pt.take()
                    bb = b1t[:, 4 * x + c:4 * x + c + 1]
                    if c % 2:
                        m2 = dve.do(lambda e, P=P, k=k, bb=bb: e.tensor_scalar(P[:, 0:CAP], PS[:, k, 0:CAP], bb, 0.0, ALU.add, ALU.max),
                                    m, pm, loads["l2"].all())
                    else:
                        m2 = act.do(lambda e, P=P, k=k, bb=bb: e.activation(P[:, 0:CAP], PS[:, k, 0:CAP], ACT.Relu, bias=bb, scale=1.0),
                                    m, pm, loads["l2"].all())
                    banks.free(k, m2)
                    res.append((s, P, m2))
                    yield
                xts.free(j, m)
                return res

            def down(x, res):
                k, m1 = banks.take()
                for n, (a, w) in enumerate(P3):
                    for c in range(4):
                        f = mm(PS[0:w, k, 128 * n:128 * n + 128], res[c][1][:, a:a + w], w2e[:, x, c, :], c == 0, c == 3)
                        if n == 2 and c == 3:
                            m = pe.do(f)
                        else:
                            pe.quiet(f, m1, [r[2] for r in res])
                for r in res:
                    pt.free(r[0], m)
                yield
                i, o, om = outs.take()
                bb = b2r[:, 128 * x:128 * x + 128]
                b3 = bb.rearrange("p (o d) -> p o d", o=1).broadcast_to((128, 2, 128))
                m2 = dve.do(lambda e: e.tensor_tensor(o[:, 0:256].rearrange("p (t d) -> p t d", t=2),
                                                      PS[:, k, 0:256].rearrange("p (t d) -> p t d", t=2), b3, ALU.add), m, om, loads["l1b"].all())
                m3 = dve.do(lambda e: e.tensor_tensor(o[0:64, 256:384], PS[0:64, k, 256:384], bb[0:64, :], ALU.add), m)
                banks.free(k, m3)
                eo[i].start(sp, dout[CAP * x:CAP * x + 256, :].rearrange("(t p) d -> p t d", p=128),
                         o[:, 0:256].rearrange("p (t d) -> p t d", t=2), m3)
                eo[i].start(sp, dout[CAP * x + 256:CAP * x + CAP, :], o[0:64, 256:384])
                outs.free(i, eo[i].all())

            raw = fetch(0)
            t = yield from turn(*raw)
            raw = fetch(1)
            last = yield from up(0, *t)
            for x in range(8):
                nxt = None
                if x < 7:
                    t = yield from turn(*raw)
                    if x < 6:
                        raw = fetch(x + 2)
                    nxt = yield from up(x + 1, *t)
                yield from down(x, last)
                last = nxt
            for i in range(4):
                ot_free[i] = [eo[0].all(), eo[1].all(), (pe.sem, pe.n)]
            oc_free = [(pe.sem, pe.n)]

        def capacity_combine(b, par):
            G = Ht[:, 512 * par:512 * par + 512]
            for t in range(4):
                gq[par].gather(pool, G[:, 128 * t:128 * t + 128], dout, ints[:, 16 + 4 * b + t:17 + 4 * b + t], 8 * CAP - 1,
                               k1["slot", b], eo[0].all(), eo[1].all(), hfree[par])
            gm = gq[par].all()
            yield
            ms = []
            for t in range(4):
                x = Xb[b][:, 128 * t:128 * t + 128]
                m = dve.do(lambda e, t=t, x=x: e.scalar_tensor_tensor(x, G[:, 128 * t:128 * t + 128], keep[:, 4 * b + t:4 * b + t + 1],
                                                                      x, ALU.mult, ALU.add), gm, k1["w", b], xw[b])
            hfree[par] = [m]
            xw[b] = [m]
            yield

        def combine(b, W, wm, e_, k, m):
            ms = []
            for t in range(4):
                x = Xb[b][:, 128 * t:128 * t + 128]
                ms.append(dve.do(lambda e, t=t, x=x: e.scalar_tensor_tensor(x, PS[:, k, 128 * t:128 * t + 128], W[:, t, e_:e_ + 1],
                                                                            x, ALU.mult, ALU.add), m, wm, xw[b]))
            banks.free(k, ms[-1])
            xw[b] = [ms[-1]]

        def gated_back(b, par, state):
            hT, W, wm, _, _ = state
            hv = HT[:, 512 * par:512 * par + 512]
            rdy = loads["l0f"].all()

            def up(x):
                res = []
                for c in range(2):
                    kg, m1 = banks.take()
                    mg = pe.do(mm(PS[:, kg, :], W13[:, x, 128 * c:128 * c + 128], hv), m1, hT, rdy)
                    ku, m1 = banks.take()
                    mu = pe.do(mm(PS[:, ku, :], W13[:, x, 256 + 128 * c:384 + 128 * c], hv), m1)
                    s, P, pm = pt.take()
                    m = act.do(lambda e, P=P, kg=kg: e.activation(P, PS[:, kg, :], ACT.Silu), mg, pm)
                    banks.free(kg, m)
                    m = dve.do(lambda e, P=P, ku=ku: e.tensor_tensor(P, P, PS[:, ku, :], ALU.mult), m, mu)
                    banks.free(ku, m)
                    res.append((s, P, m))
                    yield
                return res

            def down(x, res):
                k, m1 = banks.take()
                for t in range(4):
                    for c in range(2):
                        f = mm(PS[:, k, 128 * t:128 * t + 128], res[c][1][:, 128 * t:128 * t + 128], W2m[:, x, c, :], c == 0, c == 1)
                        if t == 3 and c == 1:
                            m = pe.do(f)
                        else:
                            pe.quiet(f, m1, [r[2] for r in res])
                for r in res:
                    pt.free(r[0], m)
                yield
                combine(b, W, wm, x, k, m)

            last = yield from up(0)
            for x in range(9):
                nxt = (yield from up(x + 1)) if x < 8 else None
                yield from down(x, last)
                last = nxt
            htfree[par] = [(pe.sem, pe.n)]
            rtfree[par] = list(xw[b])

        def relu_back(b, par, state, w1, w2, b1, b2, rdy):
            hT, W, wm, wT, mw = state
            hv = HT[:, 512 * par:512 * par + 512]

            def up(x):
                res = []
                for c in range(4):
                    k, m1 = banks.take()
                    m = pe.do(mm(PS[:, k, :], w1[:, x, 128 * c:128 * c + 128], hv), m1, hT, rdy)
                    s, P, pm = pt.take()
                    bb = b1[:, 4 * x + c:4 * x + c + 1]
                    if c == 3:
                        m = dve.do(lambda e, P=P, k=k, bb=bb: e.tensor_scalar(P, PS[:, k, :], bb, 0.0, ALU.add, ALU.max), m, pm, loads["l2"].all())
                    else:
                        m = act.do(lambda e, P=P, k=k, bb=bb: e.activation(P, PS[:, k, :], ACT.Relu, bias=bb, scale=1.0), m, pm, loads["l2"].all())
                    banks.free(k, m)
                    res.append((s, P, m))
                    yield
                return res

            def down(x, res):
                k, m1 = banks.take()
                for t in range(4):
                    for c in range(4):
                        f = mm(PS[:, k, 128 * t:128 * t + 128], res[c][1][:, 128 * t:128 * t + 128], w2[:, x, c, :], c == 0, c == 3)
                        if t == 3 and c == 3:
                            m = pe.do(f)
                        else:
                            pe.quiet(f, m1, [r[2] for r in res])
                for r in res:
                    pt.free(r[0], m)
                yield
                combine(b, W, wm, x, k, m)

            last = yield from up(0)
            for x in range(8):
                nxt = (yield from up(x + 1)) if x < 7 else None
                yield from down(x, last)
                last = nxt
            htfree[par] = [(pe.sem, pe.n)]
            k, m1 = banks.take()
            for t in range(4):
                f = mm(PS[:, k, 128 * t:128 * t + 128], wT[:, 128 * t:128 * t + 128], b2)
                if t < 3:
                    pe.quiet(f, m1, mw, loads["l2"].all())
                else:
                    m = pe.do(f)
            hfree[par] = [m]
            m = dve.do(lambda e: e.tensor_tensor(Xb[b], Xb[b], PS[:, k, :], ALU.add), m, xw[b])
            banks.free(k, m)
            xw[b] = [m]
            rtfree[par] = [m]

        W0 = S0[:, 0:512]
        WR0 = S2[:, 0:768]
        wr0 = WR0.rearrange("p (g q c) -> p g q c", g=8, q=3)
        wv0 = S0[:, 768:1024]
        l0r = loads["l0"].all()
        F8 = S0[:, 512:520].rearrange("p (o e) -> p o e", o=1).broadcast_to((128, 32, 8))
        blk = S0[:, 768:1024].rearrange("p (a e) -> p a e", e=8)
        m = dve.do(lambda e: e.tensor_tensor(blk, blk, F8, ALU.mult), l0r)
        for q in range(3):
            mw0 = dve.do(lambda e, q=q: e.tensor_copy(wr0[:, :, q, :], wv0.rearrange("p (g c) -> p g c", g=8)), m)
        m = dve.do(lambda e: e.tensor_tensor(cols[0:96, 0:1], cols[0:96, 0:1], cols[0:96, 1:2], ALU.mult), l0r)
        bv0 = OC[0:NK, 0:256]
        mw0 = dve.do(lambda e: e.tensor_tensor(bv0, bv0, OC[0:NK, 256:512], ALU.mult), l0r)

        wrap = WR0.rearrange("p (g c) -> p g c", g=8)
        a0 = Att(0, 2, 16, 1.0 / float(np.sqrt(np.float32(128))), wrap, wrap, lambda g: cols[0:96, 0:1], lambda g: cols[0:96, 0:1],
                 S0[:, 1024:1280].rearrange("p (c n) -> p c n", c=2), [l0r, mw0], 0, expo=True)
        alone_(prepare(a0, wv0, bv0))
        oc_free = [(dve.sem, dve.n)]

        units = []
        for b in range(NB):
            units.append((lambda par, b=b: cross_front(a0, b, par, Q0), lambda par, s, b=b: cross_back(a0, b, par, s), f"l0x{b}"))

        for b in range(NB):
            units.append((lambda par, b=b: moe_front(0, b, par, 0), lambda par, s, b=b: gated_back(b, par, s), f"l0f{b}"))

        w1v = S1[:, :]
        a1 = Att(1, 4, 8, 1.0 / float(np.sqrt(np.float32(8))),
                 w1v[:, 0:384].rearrange("p (g c) -> p g c", g=4), w1v[:, 384:768].rearrange("p (g c) -> p g c", g=4),
                 lambda g: cols[0:96, 2 + g:3 + g], lambda g: cols[0:96, 6 + g:7 + g],
                 w1v[:, 896:1024].rearrange("p (c n) -> p c n", c=1), [loads["l1"].all(), loads["cb"].all()], 1)
        QQ = [QB[:, 0:2048], QB[:, 2048:4096]]
        for b in range(NB):
            units.append((lambda par, b=b: cross_front(a1, b, par, QQ), lambda par, s, b=b: cross_back(a1, b, par, s), f"l1x{b}"))
        w1e = RB[:, 0:4096].rearrange("p (e n) -> p e n", e=8)
        w2e = RB[:, 4096:8192].rearrange("p (e c n) -> p e c n", e=8, c=4)

        def nothing(par, s):
            return iter(())

        for b in range(NB):
            units.append((lambda par, b=b: moe_front(1, b, par, 1), nothing, f"l1f{b}"))
        units.append((lambda par: capacity_experts(), nothing, "l1e"))
        for b in range(NB):
            units.append((lambda par, b=b: capacity_combine(b, par), nothing, f"l1c{b}"))

        KP = RB[:, 0:CK]
        VP = RB[:, 512:1024]
        QP = RB[:, 1024:2048]
        S2v = S2[:, :]
        l2 = {}

        def l2_prepare():
            end1 = [(pe.sem, pe.n)]
            l2["free"] = end1
            load("l2m", mkf[0:NK, :], A["mfT"], end1)
            for i in range(2):
                ltfree[i], w12free[i] = end1, end1
            k, marks = banks.take()
            m = pe.do(mm(PS[:, k, 0:CK], S2v[:, 128:256], CT[:, :]), marks, loads["l2w"].all())
            m = act.do(lambda e, k=k: e.activation(KP, PS[:, k, 0:CK], ACT.Relu, bias=cols[:, 11:12], scale=1.0), m, end1)
            banks.free(k, m)
            l2["k"] = m
            k, marks = banks.take()
            for b in range(NB):
                f = mm(PS[0:NK, k, 128 * b:128 * b + 128], CT[:, NKP * b:NKP * b + NK], S2v[:, 256:384])
                if b < 3:
                    pe.quiet(f, marks)
                else:
                    m = pe.do(f)
            vb = bias[0:NK, 128 * 6:128 * 7].rearrange("p (o d) -> p o d", o=1).broadcast_to((NK, 4, 128))
            vv = VP[0:NK, 0:512].rearrange("p (b d) -> p b d", b=4)
            m = dve.do(lambda e: e.tensor_tensor(vv, PS[0:NK, k, :].rearrange("p (b d) -> p b d", b=4), vb, ALU.add), m, end1)
            banks.free(k, m)
            l2["v"] = dve.do(lambda e: e.tensor_scalar(VP[0:NK, 0:512], VP[0:NK, 0:512], 0.0, None, ALU.max), m)
            yield

        qpfree = [None, None]

        def l2x_front(b, par):
            h, hT = yield from ln_front(b, par)
            k, marks = banks.take()
            m = pe.do(mm(PS[:, k, :], S2v[:, 0:128], HT[:, 512 * par:512 * par + 512]), marks, hT, loads["l2w"].all())
            htfree[par] = [m]
            yield
            qp = QP[:, 512 * par:512 * par + 512]
            qpfree[par] = qpfree[par] or l2["free"]
            m = act.do(lambda e: e.activation(qp, PS[:, k, :], ACT.Relu, bias=cols[:, 10:11], scale=1.0), m, qpfree[par])
            banks.free(k, m)
            return qp, m

        def l2x_back(b, par, state):
            qp, m = state
            k, marks = banks.take()
            m = pe.do(mm(PS[0:NK, k, :], KP[:, NKP * b:NKP * b + NK], qp), m, marks, l2["k"])
            qpfree[par] = [m]
            yield
            s, P, pm = pt.take()
            m = act.do(lambda e: e.activation(P[0:NK, :], PS[0:NK, k, :], ACT.Relu, bias=0.0, scale=1.0 / float(np.sqrt(np.float32(128)))), m, pm)
            banks.free(k, m)
            m = dve.do(lambda e: e.tensor_tensor(P[0:NK, :], P[0:NK, :], mkf[0:NK, :], ALU.add), m, loads["l2m"].all())
            yield
            k2, marks = banks.take()
            for t in range(4):
                f = mm(PS[:, k2, 128 * t:128 * t + 128], P[0:NK, 128 * t:128 * t + 128], VP[0:NK, 128 * b:128 * b + 128])
                if t < 3:
                    pe.quiet(f, m, marks, l2["v"])
                else:
                    m = pe.do(f)
            pt.free(s, m)
            yield
            m = dve.do(lambda e: e.scalar_tensor_tensor(Xb[b], PS[:, k2, :], 0.0, Xb[b], ALU.max, ALU.add), m, xw[b])
            banks.free(k2, m)
            xw[b] = [m]

        for b in range(NB):
            units.append((lambda par, b=b: l2x_front(b, par), lambda par, s, b=b: l2x_back(b, par, s), f"l2x{b}"))

        LT = RB[:, 2048:6144]
        W1x = RB[:, 6144:7168]
        W2x = RB[:, 7168:8192]
        lq = [Loads(sem("lq0")), Loads(sem("lq1"))]
        ltfree = [[], []]
        w12free = [[], []]

        def l2f_front(b, par):
            H = Ht[:, 512 * par:512 * par + 512]
            h, hT = yield from ln_front(b, par)
            add_row(b, 2, h)
            lt = LT[64 * par:64 * par + 1, 0:2048]
            lq[par].start(sp, lt.rearrange("o (t d) -> o t d", t=16), H[1:17, 0:128], h, ltfree[par])
            lm = lq[par].all()
            hfree[par] = hfree[par] + [lm]
            yield
            yield
            row = lambda t: lt[:, 128 * t:128 * t + 128]
            w1 = W1x[:, 512 * par:512 * par + 512]
            w2 = W2x[:, 512 * par:512 * par + 512]
            k, marks = banks.take()
            for i in range(4):
                f = mm(PS[:, k, 128 * i:128 * i + 128], row(2 * i + 1), row(2 * i))
                if i < 3:
                    pe.quiet(f, marks, lm)
                else:
                    m = pe.do(f)
            yield
            m1 = dve.do(lambda e, k=k: e.scalar_tensor_tensor(w1, PS[:, k, :], cols[:, 12:13], S2v[:, 384:896], ALU.mult, ALU.add),
                        m, w12free[par], loads["cb"].all(), loads["l2w"].all())
            banks.free(k, m1)
            k, marks = banks.take()
            o = PS[:, k, :].rearrange("p (r o) -> p r o", r=4)
            for i in range(4):
                f = mm(o[:, :, 32 * i:32 * i + 32], row(2 * (4 + i) + 1),
                       row(2 * (4 + i)).rearrange("p (o r) -> p r o", r=4))
                if i < 3:
                    pe.quiet(f, marks)
                else:
                    m = pe.do(f)
            ltfree[par] = [m]
            yield
            m2 = dve.do(lambda e, k=k: e.scalar_tensor_tensor(w2, PS[:, k, :], cols[:, 12:13], S2v[:, 896:1408], ALU.mult, ALU.add), m)
            banks.free(k, m2)
            return hT, w1, w2, m1, m2

        def l2f_back(b, par, state):
            hT, w1, w2, m1, m2 = state
            res = []
            for c in range(4):
                k, marks = banks.take()
                m = pe.do(mm(PS[:, k, :], w1[:, 128 * c:128 * c + 128], HT[:, 512 * par:512 * par + 512]), marks, hT, m1)
                s, P, pm = pt.take()
                m = act.do(lambda e, P=P, k=k, c=c: e.activation(P, PS[:, k, :], ACT.Gelu, bias=cols[:, 13 + c:14 + c], scale=1.0), m, pm)
                banks.free(k, m)
                res.append((s, P, m))
                yield
            htfree[par] = [(pe.sem, pe.n)]
            k, marks = banks.take()
            for t in range(4):
                for c in range(4):
                    f = mm(PS[:, k, 128 * t:128 * t + 128], res[c][1][:, 128 * t:128 * t + 128], w2[:, 128 * c:128 * c + 128], c == 0, c == 3)
                    if t == 3 and c == 3:
                        m = pe.do(f)
                    else:
                        pe.quiet(f, marks, m2, [r[2] for r in res])
            for r in res:
                pt.free(r[0], m)
            w12free[par] = [m]
            yield
            m = dve.do(lambda e: e.tensor_tensor(Xb[b], Xb[b], PS[:, k, :], ALU.add), m, xw[b])
            banks.free(k, m)
            xw[b] = [m]

        for b in range(NB):
            units.append((lambda par, b=b: l2f_front(b, par), lambda par, s, b=b: l2f_back(b, par, s), f"l2f{b}"))

        w3 = S0[:, 0:1024]
        a3 = Att(3, 4, 8, float(8 ** -0.5),
                 w3[:, 0:384].rearrange("p (g c) -> p g c", g=4), w3[:, 384:768].rearrange("p (g c) -> p g c", g=4),
                 lambda g: None, lambda g: None,
                 w3[:, 896:1024].rearrange("p (c n) -> p c n", c=1), None, 3, mask=True)

        def l3x_masks():
            m = dve.do(lambda e: e.tensor_copy(mkb[0:NK, :], mk8[0:NK, :]), loads["l2"].all())
            i3 = ident[0:NK, 0:NK].rearrange("p (o k) -> p o k", o=1).broadcast_to((NK, 4, NK))
            a3.mask_ready = dve.do(lambda e: e.tensor_scalar(negI[0:NK, 0:4 * NK].rearrange("p (h k) -> p h k", h=4), i3, -BIG, None, ALU.mult), ready_c)

        for b in range(NB):
            units.append((lambda par, b=b: cross_front(a3, b, par, QQ), lambda par, s, b=b: cross_back(a3, b, par, s), f"l3x{b}"))

        w4 = S1[:, :]
        a4 = Att(4, 4, 8, 1.0 / float(np.sqrt(np.float32(8))),
                 w4[:, 0:384].rearrange("p (g c) -> p g c", g=4), w4[:, 384:768].rearrange("p (g c) -> p g c", g=4),
                 lambda g: cols[0:96, 17 + g:18 + g], lambda g: cols[0:96, 21 + g:22 + g],
                 w4[:, 896:1024].rearrange("p (c n) -> p c n", c=1), None, 4)
        Y = RB[:, 0:2048]
        Yb = [Y[:, 512 * b:512 * b + 512] for b in range(NB)]
        V4 = [RB[:, 2048:4096], RB[:, 4096:6144]]
        v4free = [[], []]
        kslots = Slots([KB[:, 2048 * i:2048 * i + 2048] for i in range(3)])
        k4 = {}
        q4free = [[], []]

        def l3_self_open(marks):
            for i in range(2):
                vz = V4[i].rearrange("p (g c) -> p g c", c=32)
                m = dve.do(lambda e, vz=vz: e.memset(vz[:, :, 9:32], 0.0), marks)
                m = dve.do(lambda e, vz=vz: e.memset(vz[:, :, 8:9], 1.0), marks)
                v4free[i] = [m]

        def self_norms(b, par):
            h0 = yield from layernorm(Xb[b], Yb[b], par, xw[b], k4["rb_free"])
            H = Ht[:, 512 * par:512 * par + 512]
            h = yield from layernorm(Yb[b], H, par, h0, hfree[par])
            hT, turned = yield from transposed(H, par, h, cols[:, 25:26], cols[:, 26:27])
            hfree[par] = [turned]
            r = bias[:, 128 * 4:128 * 5].rearrange("p (o d) -> p o d", o=1).broadcast_to((128, 4, 128))
            y = Yb[b].rearrange("p (t d) -> p t d", t=4)
            yw[b] = [pool.do(lambda e: e.tensor_tensor(y, y, r, ALU.add), h)]
            k, marks = banks.take()
            hv = HT[:, 512 * par:512 * par + 512]
            for c in range(4):
                f = mm(PS[:, k, 128 * c:128 * c + 128], hv[:, 128 * c:128 * c + 128], w4[:, 768:896])
                if c < 3:
                    pe.quiet(f, marks, hT, a4.ready)
                else:
                    m = pe.do(f)
            yield
            bv = bias[:, 128 * 7:128 * 8].rearrange("p (h c) -> p h c", c=8)
            vv = V4[par].rearrange("p (c h k) -> p c h k", c=4, h=16)
            for c in range(4):
                src = PS[:, k, 128 * c:128 * c + 128].rearrange("p (h c) -> p h c", c=8)
                mv_ = dve.do(lambda e, c=c, src=src: e.tensor_tensor(vv[:, c, :, 0:8], src, bv, ALU.add), m, v4free[par])
            banks.free(k, mv_)
            v4free[par] = None
            return hT, vv, mv_

        def self_open(b, g, par, st):
            hT, vv, vm = st
            qs = lambda g: QQ[par][:, 512 * g:512 * g + 512]
            qm, read = yield from queries(a4, g, par, hT, qs)
            s, K, km = kslots.take()
            kv = K.rearrange("p (h k) -> p h k", h=4)
            kd = yield from keys(a4, g, 512, HT[:, 512 * par:512 * par + 512], hT, lambda hh: kv[:, hh, :], km)
            return s, kv, kd, qm

        def self_front(b, g, par, s, kv, kd, qm):
            qs = lambda g: QQ[par][:, 512 * g:512 * g + 512]
            M = MX[:, 4 * RK * par:4 * RK * par + 4 * RK].rearrange("p (t c) -> p t c", t=4)
            for t in range(4):
                for p2 in range(2):
                    k, marks = banks.take_pair()
                    for i in range(2):
                        f = mm(PS[:, k + i, :], qs(g)[0:RM, 128 * t:128 * t + 128], kv[0:RM, 2 * p2 + i, :])
                        if i:
                            m = pe.do(f)
                        else:
                            pe.quiet(f, marks, qm, kd)
                    yield
                    dst = M[:, t, RM + 4 * g + 2 * p2:RM + 4 * g + 2 * p2 + 2]
                    m = dve.do(lambda e, dst=dst, k=k: e.tensor_reduce(dst, PS[:, k:k + 2, :], AX, ALU.max), m, mxfree[par])
                    banks.free(k, m)
                    banks.free(k + 1, m)
            mt = yield from row_maxima(par, m, qs, [g], q4free[par])
            mxfree[par] = [(pe.sem, pe.n)]
            return s, kv, kd, qm, mt

        def self_back(b, g, par, st, fr):
            hT, vv, vm = st
            s, kv, kd, qm, mt = fr
            qs = QQ[par][:, 512 * g:512 * g + 512]
            i6, o, om = acc_bank.take()

            def scores(c):
                res = []
                for i in range(4):
                    k, marks = banks.take()
                    m = pe.do(mm(PS[:, k, :], kv[0:RK, i, 128 * c:128 * c + 128], qs[0:RK, :]), marks, mt, qm, kd)
                    sl, P, pm = pt.take()
                    m = act.do(lambda e, P=P, k=k: e.activation(P, PS[:, k, :], ACT.Exp, bias=0.0, scale=a4.scale), m, pm)
                    banks.free(k, m)
                    res.append((sl, P, m))
                    yield
                return res

            def values(c, res):
                for i, (sl, P, m) in enumerate(res):
                    f = mm(PS[32 * i:32 * i + 32, o, :], vv[:, c, 4 * g + i, :], P, c == 0, c == 3)
                    if i < 3:
                        pe.quiet(f, [r[2] for r in res], om, vm)
                    else:
                        m = pe.do(f)
                for r in res:
                    pt.free(r[0], m)
                yield
                return m

            last = yield from scores(0)
            for c in range(4):
                nxt = (yield from scores(c + 1)) if c < 3 else None
                m = yield from values(c, last)
                last = nxt
            kslots.free(s, m)
            m = dve.do(lambda e: e.tensor_copy(OT[:, 512 * g:512 * g + 512], PS[:, o, :]), m, ot_free[g])
            acc_bank.free(i6, m)
            return m

        def self_attention():
            st = [None]
            ots = []

            def first(b, g, par):
                if g == 0:
                    st[0] = yield from self_norms(b, par)
                    qfree[par] = q4free[par]
                op = yield from self_open(b, g, par, st[0])
                if g == 3:
                    htfree[par] = [(pe.sem, pe.n)]
                    qfree[par] = None
                return (b, g, par, st[0], op)

            def second(b, g, par, s, op):
                fr = yield from self_front(b, g, par, *op)
                return (b, g, par, s, fr)

            def third(b, g, par, s, fr):
                m = yield from self_back(b, g, par, s, fr)
                ots.append(m)
                if g == 3:
                    q4free[par] = [(pe.sem, pe.n)]
                    v4free[par] = [(pe.sem, pe.n)]
                    m = yield from finish(a4, par, list(ots), Yb[b], yw[b])
                    yw[b] = [m]
                    ots.clear()
                    xx = pool.do(lambda e: e.tensor_tensor(Xb[b], Xb[b], Yb[b], ALU.add), m, xw[b])
                    xw[b] = [xx]

            q4free[0], q4free[1] = qfree[0], qfree[1]
            steps = [(b, g, b % 2) for b in range(NB) for g in range(4)]
            one, two = None, None
            for i in range(len(steps) + 2):
                g = steps[i][1] if i < len(steps) else 1
                streams = [(first(*steps[i]) if i < len(steps) else iter(()), 8 if g else 22),
                           (second(*one) if one else iter(()), 11),
                           (third(*two) if two else iter(()), 25 if i > 1 and steps[i - 2][1] < 3 else 40)]
                one, two, _ = together(*streams)

        def l3m_front(b, par):
            H = Ht[:, 512 * par:512 * par + 512]
            h = yield from layernorm(Yb[b], H, par, yw[b], hfree[par])
            hT, turned = yield from transposed(H, par, h, cols[:, 27:28], cols[:, 28:29])
            hfree[par] = [turned]
            st_ = yield from moe_front(2, b, par, 2, src=(h, hT))
            return st_

        w1g = RA[:, 0:4096].rearrange("p (e n) -> p e n", e=8)
        w2g = RA[:, 4096:8192].rearrange("p (e c n) -> p e c n", e=8, c=4)

        def play_units(us, between, alone):
            pend = None
            for i, (front, back, name) in enumerate(us):
                par = i % 2
                if name in alone:
                    alone_(pend)
                    pend = None
                    alone_(alone[name]())
                f = front(par)
                if name in beside:
                    f = chain(f, beside[name]())
                if pend:
                    size = FRONT[name[:3]] + (24 if name in beside else 0)
                    state, _ = together((f, size), (pend, BACK[us[i - 1][2][:3]]))
                else:
                    state = alone_(f)
                if name in between:
                    between[name]()
                pend = back(par, state)
            alone_(pend)

        def chain(f, g):
            state = yield from f
            yield from g
            return state

        FRONT = {"l0x": 44, "l0f": 31, "l1x": 36, "l1f": 19, "l1e": 60, "l1c": 2, "l2x": 7, "l2f": 10, "l3x": 36, "l3m": 14}
        BACK = {"l0x": 34, "l0f": 27, "l1x": 34, "l1f": 40, "l1e": 1, "l1c": 1, "l2x": 3, "l2f": 5, "l3x": 34, "l3m": 40}
        beside = {}

        def after_l0x():
            m = (pe.sem, pe.n)
            load("l1f", w1e, A["l1_w1"].rearrange("e p n -> p e n"), m)
            load("l1f", w2e, A["l1_w2"].rearrange("e (c p) n -> p e c n", p=128), m)
            load("l3x", w3, A["l3x_w"], m)
            load("l2w", S2[:, :], A["l2_w"], m)

        def mid_l0f():
            yield from prepare(a1, w1v[:, 768:896], bias[0:NK, 128 * 5:128 * 6])

        def after_l0f():
            m = (pe.sem, pe.n)
            load("l3f", w1g, A["l3_w1"].rearrange("e p n -> p e n"), m)
            load("l3f", w2g, A["l3_w2"].rearrange("e (c p) n -> p e c n", p=128), m)

        def after_l1x():
            load("l1b", b2r, A["l1_b2r"], (pe.sem, pe.n))
            load("l3s", w4, A["l3s_w"], (pe.sem, pe.n))

        def before_l3x():
            l3x_masks()
            a3.ready = [loads["l3x"].all()]
            yield from prepare(a3, w3[:, 768:896], None)

        beside["l0f2"], beside["l2f2"] = mid_l0f, before_l3x
        play_units(units, {"l0f0": after_l0x, "l1x0": after_l0f, "l1f0": after_l1x}, {"l2x0": l2_prepare})
        a4.ready = [loads["l3s"].all()]
        end3 = [(pe.sem, pe.n)]
        k4["rb_free"] = end3
        for i in range(3):
            kslots.free(i, end3)
        l3_self_open(end3)
        self_attention()
        um = [(lambda par, b=b: l3m_front(b, par),
               lambda par, s, b=b: relu_back(b, par, s, w1g, w2g, b1t[:, 32:64], b2t[0:8, 128:256], loads["l3f"].all()), f"l3m{b}")
              for b in range(NB)]
        fin = Loads(sem("fin"))

        def emit_out(b):
            fin.start(sp, out[b].rearrange("(t p) d -> p t d", p=128), Xb[b].rearrange("p (t d) -> p t d", t=4), xw[b])

        def with_out(bk, b):
            def back(par, s):
                yield from bk(par, s)
                emit_out(b)
            return back

        um = [(f, with_out(bk, b), n) for b, (f, bk, n) in enumerate(um)]
        play_units(um, {}, {})
        sp.wait(fin.all())

        block = ctx.enter_context(nc.Block())
        block.sync(sp.play)
        block.gpsimd(pool.play)
        block.scalar(act.play)
        block.vector(dve.play)
        block.tensor(pe.play)


def kernel(**inputs):
    import numpy as _np
    import concourse.bacc as _bacc
    from concourse import mybir as _mybir
    from concourse.bass_utils import run_bass_kernel_spmd as _run

    I = {k: _np.asarray(v) for k, v in inputs.items()}

    def rep(w):
        return _np.tile(w.reshape(128, 4, 1, 32), (1, 1, 3, 1)).reshape(128, 384)

    def repb(b):
        return _np.tile(b.reshape(4, 32).T, (4, 1))

    rows = lambda v: _np.broadcast_to(v.reshape(1, -1), (128, v.size))
    r = _np.arange(RK)[:, None]
    h = _np.arange(NH)[None, :]

    def mask(hd, hpg):
        return _np.where(r < RM, (r % 32) // hd == h % hpg, r - RM == h).astype(_np.float32)

    msk = _np.zeros((128, 32), _np.float32)
    msk[:RK, 0:16], msk[:RK, 16:32] = mask(8, 4), mask(16, 2)
    block = _np.zeros((16, 8, 16, 2, 8), _np.float32)
    for i in range(16):
        block[i, :, i, 0, :], block[i, :, i, 1, :] = 1.0, -1.0
    sign = _np.repeat(_np.tile(_np.array([1.0, -1.0], _np.float32), 128), 8)
    C = {
        "x": I["x"], "ctxT": _np.pad(I["ctx_1024"].transpose(2, 0, 1), ((0, 0), (0, 0), (0, 1))).reshape(128, CK),
        "c_ident": _np.eye(128, dtype=_np.float32), "c_mask": msk,
        "c_block": block.reshape(128, 256), "c_sign": sign[:96].reshape(96, 1), "c_signr": _np.tile(sign[:256], (NK, 1)),
        "c_tri": _np.triu(_np.ones((128, 128), _np.float32)),
        "c_off": _np.tile(_np.arange(8).astype(_np.float32) * CAP - 1.0, (128, 4)),
        "l1_b2r": rows(I["L1_ffn_b2"]),
        "c_rev": _np.tile(_np.arange(8, 0, -1).astype(_np.float32), (128, 4)),
        "fm_w": _np.tile(I["L0_xattn_fm_w"].T, (16, 1)), "fm_b": _np.tile(I["L0_xattn_fm_b"], 12).reshape(96, 1),
        "fm_br": _np.tile(I["L0_xattn_fm_b"], (NK, 32)), "fc_w": I["L0_xattn_fc_w"].T,
        "gates": _np.stack([I["L0_ffn_Wg"], I["L1_ffn_gate_w"].T, I["L3_ffn_gate_w"]]),
        "gateb": _np.concatenate([rows(I["L1_ffn_gate_b"]), rows(I["L3_ffn_gate_b"])], 1),
        "rows": _np.stack([rows(I[n]) for n in ("L0_xattn_fc_b", "L1_xattn_bo", "L2_ffn_b2", "L3_xattn_bproj", "L3_ffn_bo",
                                                "L1_xattn_bv", "L2_xattn_bias_v", "L3_ffn_bv")]),
        "colb": _np.concatenate([
            repb(I["L1_xattn_bq"]), repb(I["L1_xattn_bk"]), I["L2_xattn_bias_q"][:, None], I["L2_xattn_bias_k"][:, None],
            rows(I["L2_ffn_scale"].reshape(1)), I["L2_ffn_b1"].reshape(4, 128).T, repb(I["L3_ffn_bq"]), repb(I["L3_ffn_bk"]),
            I["L3_ffn_ln1_g"][:, None], I["L3_ffn_ln1_b"][:, None], I["L3_ffn_ln2_g"][:, None], I["L3_ffn_ln2_b"][:, None],
            _np.zeros((128, 11), _np.float32)], 1),
        "l0_w13": _np.concatenate([_np.concatenate([I["L0_ffn_We1"], I["L0_ffn_Ws1"][None]]),
                                   _np.concatenate([I["L0_ffn_We3"], I["L0_ffn_Ws3"][None]])], 2),
        "l0_w2": _np.concatenate([I["L0_ffn_We2"], I["L0_ffn_Ws2"][None]]),
        "l1_w": _np.concatenate([rep(I["L1_xattn_Wq"].T), rep(I["L1_xattn_Wk"].T), I["L1_xattn_Wv"].T, I["L1_xattn_Wo"].T], 1),
        "l1_w1": I["L1_ffn_w1"], "l1_w2": I["L1_ffn_w2"],
        "b1": _np.concatenate([I["L1_ffn_b1"].reshape(32, 128).T, I["L3_ffn_b1"].reshape(32, 128).T], 1),
        "b2": _np.concatenate([I["L1_ffn_b2"], I["L3_ffn_b2"]], 1),
        "l2_w": _np.concatenate([I["L2_xattn_kernel_q"][0, 0], I["L2_xattn_kernel_k"][0, 0], I["L2_xattn_kernel_v"][0, 0],
                                 I["L2_ffn_W1"].T, I["L2_ffn_W2"].T.reshape(4, 128, 128).transpose(1, 0, 2).reshape(128, 512)], 1),
        "mfT": I["mask_1xSxS2_ff0"][0].T, "mbT": I["mask_BxSxS2_bk0"].transpose(2, 0, 1).reshape(NK, 2048),
        "l3x_w": _np.concatenate([rep(I["L3_xattn_Wq"]), rep(I["L3_xattn_Wkv"][:, 0:128]), I["L3_xattn_Wkv"][:, 128:256],
                                  I["L3_xattn_Wproj"]], 1),
        "l3s_w": _np.concatenate([rep(I["L3_ffn_wq"]), rep(I["L3_ffn_wk"]), I["L3_ffn_wv"], I["L3_ffn_wo"]], 1),
        "l3_w1": I["L3_ffn_w1"], "l3_w2": I["L3_ffn_w2"],
    }
    nc = _bacc.Bacc("TRN2", target_bir_lowering=False, num_devices=1)
    arrays, aps = {}, {}
    for name, a in C.items():
        a = _np.ascontiguousarray(a)
        arrays["in_" + name] = a
        aps[name] = nc.dram_tensor("in_" + name, a.shape, _mybir.dt.from_np(a.dtype), kind="ExternalInput").ap()
    o = nc.dram_tensor("out_0", (4, 512, 128), _mybir.dt.float32, kind="ExternalOutput").ap()
    program(nc, aps, o)
    res = _run(nc, [arrays], core_ids=[0])
    return res.results[0]["out_0"]
```

```python
from contextlib import ExitStack

import numpy as np

import concourse.bass as bass
from concourse import mybir

F32 = mybir.dt.float32
F32R = mybir.dt.float32r
BF16 = mybir.dt.bfloat16
U8 = mybir.dt.uint8
I32 = mybir.dt.int32
ALU = mybir.AluOpType
ACT = mybir.ActivationFunctionType
AX = mybir.AxisListType.X

NB, S, D, NK, NH = 4, 512, 128, 77, 16
NKP = NK + 1
CK = NB * NKP
EPS = 1e-5
BIG = 1e30
CAP = 320
NT = 15
RM = 96
RK = 112


class Engine:

    def __init__(self, sem):
        self.sem, self.n, self.queue, self.past = sem, 0, [], {}

    def wait(self, *marks):
        for m in marks:
            if m is None:
                continue
            if isinstance(m, list):
                self.wait(*m)
                continue
            sem, value = m
            if self.past.get(sem.name, 0) < value:
                self.past[sem.name] = value
                self.queue.append(lambda e, s=sem, v=value: e.wait_ge(s, v))

    def do(self, make, *marks):
        self.wait(*marks)
        self.n += 1
        self.queue.append(lambda e, s=self.sem: make(e).then_inc(s, 1))
        return (self.sem, self.n)

    def quiet(self, make, *marks):
        self.wait(*marks)
        self.queue.append(make)

    def play(self, e):
        for make in self.queue:
            make(e)


class Loads:

    def __init__(self, sem):
        self.sem, self.n = sem, 0

    def start(self, engine, out, in_, *marks):
        engine.wait(*marks)
        self.n += 16
        engine.queue.append(lambda e, s=self.sem: e.dma_start(out, in_).then_inc(s, 16))

    def scatter(self, pool, out, idx, in_, limit, *marks):
        pool.wait(*marks)
        self.n += 16
        pool.queue.append(lambda e, s=self.sem: e.indirect_dma_start(
            out, bass.IndirectOffsetOnAxis(ap=idx, axis=0), in_, None, bounds_check=limit, oob_is_err=False).then_inc(s, 16))

    def gather(self, pool, out, in_, idx, limit, *marks):
        pool.wait(*marks)
        self.n += 16
        pool.queue.append(lambda e, s=self.sem: e.indirect_dma_start(
            out, None, in_, bass.IndirectOffsetOnAxis(ap=idx, axis=0), bounds_check=limit, oob_is_err=False).then_inc(s, 16))

    def all(self):
        return (self.sem, self.n)


class Turns:

    def __init__(self, places):
        self.places, self.read, self.order = places, [[] for _ in places], list(range(len(places)))

    def take(self):
        i = next(i for i in self.order if self.read[i] is not None)
        self.order.remove(i)
        self.order.append(i)
        marks, self.read[i] = self.read[i], None
        return i, marks

    def free(self, i, *marks):
        self.order.remove(i)
        self.order.append(i)
        self.read[i] = list(marks)


    def get(self):
        while all(r is None for r in self.read):
            yield
        return self.take()

    def give(self, keep):
        marks = [self.read[i] for i in self.order if i not in keep]
        for i in list(self.order):
            if i not in keep:
                self.order.remove(i)
                self.read[i] = None
        return marks


class Slots(Turns):
    def take(self):
        i, marks = super().take()
        return i, self.places[i], marks


def together(*streams):
    out, at, live = [None] * len(streams), [0] * len(streams), set(range(len(streams)))
    while live:
        k = min(live, key=lambda i: (at[i] / streams[i][1] + (streams[i][2] if len(streams[i]) > 2 else 0), i))
        try:
            next(streams[k][0])
            at[k] += 1
        except StopIteration as stop:
            out[k] = stop.value
            live.remove(k)
    return out


def alone_(stream):
    return together((stream, 1))[0]


def by_turns(*streams):
    out, live = [None] * len(streams), list(range(len(streams)))
    while live:
        for i in list(live):
            try:
                next(streams[i])
                yield
            except StopIteration as stop:
                out[i] = stop.value
                live.remove(i)
    return out


def program(nc, A, out):
    with ExitStack() as ctx:
        def sb(name, cols, dt=F32):
            return ctx.enter_context(nc.sbuf_tensor(name, [128, cols], dt))

        def sem(name):
            return ctx.enter_context(nc.semaphore(name))

        PS = ctx.enter_context(nc.psum_tensor("PS", [128, 8, 512], F32))
        banks = Turns(list(range(6)))
        acc_bank = Slots([6, 7])

        pe, act, dve, pool, sp = (Engine(sem(n)) for n in ("pe", "act", "dve", "pool", "sp"))
        loads = {}

        def load(name, dst, src, *marks, by=None):
            if name not in loads:
                loads[name] = Loads(sem("ld_" + name))
            loads[name].start(by or sp, dst, src, *marks)

        X = sb("X", NB * 512)
        Xb = [X[:, 512 * b:512 * b + 512] for b in range(NB)]
        RA = sb("RA", 8192)
        with nc.sbuf_tensor("Q0", [128, 8192], F32R) as Q0t:
            Q0 = [Q0t[:, 0:4096], Q0t[:, 4096:8192]]
        RB = sb("RB", 8192)
        S0 = sb("S0", 1280)
        S1 = sb("S1", 1024)
        S2 = sb("S2", 1408)
        QB = ctx.enter_context(nc.sbuf_tensor("QB", [128, 2 * 2048], F32R))
        KB = ctx.enter_context(nc.sbuf_tensor("KB", [128, 3 * 2048], F32R))
        STG = ctx.enter_context(nc.sbuf_tensor("STG", [128, 2 * 512], F32R))
        MX = ctx.enter_context(nc.sbuf_tensor("MX", [128, 2 * 4 * RK], F32R))
        MT = ctx.enter_context(nc.sbuf_tensor("MT", [128, 512], F32R))
        VB = sb("VB", 2048)
        Ht = sb("Ht", 2 * 512)
        HT = sb("HT", 2 * 512)
        PT = sb("PT", 10 * 512)
        OT = sb("OT", 2048)
        ON = sb("ON", 2 * 256)
        OC = sb("OC", 1024)
        CT = sb("CT", CK)
        ident = sb("ident", 128)
        tri = sb("tri", 128)
        ones = sb("ones", 128)
        msk = sb("msk", 2 * NH)
        rev = sb("rev", 32)
        bias = sb("bias", 8 * 128)
        b1t = sb("b1t", 64)
        b2t = sb("b2t", 256)
        cols = sb("cols", 40)
        st = sb("st", 3 * 24)
        mv = sb("mv", 3 * 8)
        ve = sb("ve", 3 * 8)
        nh = sb("nh", 4)
        rt = sb("rt", 2 * 512)
        den = sb("den", 2 * 64)
        negI = ctx.enter_context(nc.sbuf_tensor("negI", [128, 4 * NK + 4], BF16))
        mkb = ctx.enter_context(nc.sbuf_tensor("mkb", [128, 4 * 512], BF16))
        mk8 = ctx.enter_context(nc.sbuf_tensor("mk8", [128, 4 * 512], U8))
        mkf = RB[:, 4096:4608]
        gates = sb("gates", 24)
        prev = sb("prev", 8 * 17)
        off1 = sb("off1", 32)
        ints = ctx.enter_context(nc.sbuf_tensor("ints", [128, 32], I32))
        keep = sb("keep", 16)
        ints3 = ctx.enter_context(nc.sbuf_tensor("ints3", [128, 48], I32))
        d3 = [nc.dram_tensor(f"d3{g}", (128 * NT, 128), F32, kind="Internal").ap() for g in range(2)]
        o3 = [nc.dram_tensor(f"o3{g}", (128 * NT, 128), F32, kind="Internal").ap() for g in range(2)]
        dbuf = nc.dram_tensor("dbuf", (8 * CAP, 128), F32, kind="Internal").ap()
        dout = nc.dram_tensor("dout", (8 * CAP, 128), F32, kind="Internal").ap()
        b2r = S1[:, :]

        pt = Slots([PT[:, 512 * i:512 * i + 512] for i in range(10)])
        stg = Slots([STG[:, 512 * i:512 * i + 512] for i in range(2)])

        load("l0", S0[:, 760:1280], A["l0_pack"])
        load("l0b", cols[0:96, 0:2], A["fm_b"])
        load("ctx", CT[:, :], A["ctxT"])
        load("c", msk[:, :], A["c_mask"])
        load("x0", X[:, 0:512].rearrange("p (t d) -> p t d", t=4), A["x"][0].rearrange("(t p) d -> p t d", p=128))
        load("c", ident[:, :], A["c_ident"])
        load("l0b", OC[0:NK, 0:512], A["fm_br"])
        for b in range(1, NB):
            load(f"x{b}", Xb[b].rearrange("p (t d) -> p t d", t=4), A["x"][b].rearrange("(t p) d -> p t d", p=128))
        load("c2", tri[:, :], A["c_tri"])
        load("c2", rev[:, :], A["c_rev"])
        load("c2", gates[:, :].rearrange("p (l e) -> p l e", l=3), A["gates"].rearrange("l p e -> p l e"))
        load("rb", bias[:, 0:1024].rearrange("p (r d) -> p r d", r=8), A["rows"].rearrange("r p d -> p r d"))
        load("cb", cols[:, 2:40], A["colb"])
        load("rb", rt[:, 960:976], A["gateb"])

        W13 = RA[:, 0:9 * 512].rearrange("p (e n) -> p e n", e=9)
        W2m = RA[:, 9 * 512:9 * 512 + 9 * 256].rearrange("p (e c n) -> p e c n", e=9, c=2)
        load("l0f", W13, A["l0_w13"].rearrange("e p n -> p e n"))
        load("l0f", W2m, A["l0_w2"].rearrange("e (c p) n -> p e c n", p=128))
        load("l1", S1[:, :], A["l1_w"])
        load("l2", mk8[0:NK, :], A["mbT"])
        load("l2", b1t[:, :], A["b1"])
        load("l2", b2t[0:8, :], A["b2"])
        load("c2", off1[:, :], A["c_off"])

        ready_c = loads["c"].all()
        k_zero = dve.do(lambda e: e.memset(OT[:, :], 0.0))
        for i in range(2):
            load("zero", dbuf[1280 * i:1280 * i + 1280, :].rearrange("(p t) d -> p (t d)", p=128), OT[:, 0:1280], k_zero)

        for i in range(2):
            load("zero3", d3[i].rearrange("(p t) d -> p (t d)", p=128), OT[:, 0:128 * NT])

        k = pool.do(lambda e: e.memset(nh[:, :], -0.5))
        k_nh = k
        k_ones = pool.do(lambda e: e.memset(ones[:, :], 1.0))
        k_mx = dve.do(lambda e: e.memset(MX[:, :].bitcast(F32), 0.0))
        k_stg = dve.do(lambda e: e.memset(STG[:, :].bitcast(F32), -1.0))
        k_prev = pool.do(lambda e: e.memset(prev[:, 0:8], 0.0))
        for i in range(2):
            stg.free(i, k_stg)

        xw = [[loads[f"x{b}"].all()] for b in range(NB)]
        yw = [[] for _ in range(NB)]
        hfree = [[], []]
        htfree = [[], []]
        qfree = [[], []]
        mxfree = [[k_mx], [k_mx]]
        rtfree = [[], []]
        mtfree = []
        kfree = []
        vfree = []
        mq = [Loads(sem("mq0")), Loads(sem("mq1"))]

        def mm(o, l, r, first=True, last=True):
            return lambda e: e.matmul(o, l, r, start=first, stop=last, skip_group_check=True)

        def layernorm(src, dst, par, src_marks, dst_marks):
            s6 = st[:, 24 * par:24 * par + 24]
            s2 = mv[:, 8 * par:8 * par + 8].rearrange("p (t c) -> p t c", t=4)
            v4 = ve[:, 8 * par:8 * par + 4]
            r4 = ve[:, 8 * par + 4:8 * par + 8]
            for t in range(4):
                m = dve.do(lambda e, t=t: e.bn_stats(s6[:, 6 * t:6 * t + 6], src[:, 128 * t:128 * t + 128]), src_marks)
            yield
            for t in range(4):
                m = dve.do(lambda e, t=t: e.bn_aggr(s2[:, t, :], s6[:, 6 * t:6 * t + 6]), m)
            m = dve.do(lambda e: e.tensor_scalar(v4, s2[:, :, 1], EPS, None, ALU.add), m)
            m = pool.do(lambda e: e.tensor_tensor(r4, v4, nh[:, :], ALU.pow), m, k_nh)
            yield
            yield
            for t in range(4):
                m2 = dve.do(lambda e, t=t: e.tensor_scalar(dst[:, 128 * t:128 * t + 128], src[:, 128 * t:128 * t + 128],
                                                           s2[:, t, 0:1], r4[:, t:t + 1], ALU.subtract, ALU.mult),
                            m, dst_marks)
            yield
            return m2

        def transposed(src, par, ready, scale=None, shift=None):
            b, marks = yield from banks.get()
            for t in range(4):
                f = (lambda e, t=t: e.transpose(PS[:, b, 128 * t:128 * t + 128], src[:, 128 * t:128 * t + 128], ident[:, :]))
                if t < 3:
                    pe.quiet(f, ready, ready_c, marks)
                else:
                    turned = pe.do(f)
            yield
            dst = HT[:, 512 * par:512 * par + 512]
            if scale is None:
                m = act.do(lambda e: e.activation(dst, PS[:, b, :], ACT.Copy), turned, htfree[par])
            else:
                m = act.do(lambda e: e.activation(dst, PS[:, b, :], ACT.Identity, bias=shift, scale=scale),
                           turned, htfree[par], loads["cb"].all())
            htfree[par] = None
            banks.free(b, m)
            yield
            return m, turned

        def norm(b, par, row=None, src=None, scale=None, shift=None):
            H = Ht[:, 512 * par:512 * par + 512]
            a, am = src or (Xb[b], xw[b])
            h = yield from layernorm(a, H, par, am, hfree[par])
            hfree[par] = None
            if row is not None:
                add_row(b, row, h)
            if htfree[par] is None:
                return h, None
            return h, (yield from turn_norm(par, (h, None), scale, shift))

        def turn_norm(par, hs, scale=None, shift=None):
            h, hT = hs
            if hT is None:
                hT, turned = yield from transposed(Ht[:, 512 * par:512 * par + 512], par, h, scale, shift)
                hfree[par] = [turned]
            return hT

        def add_row(b, row, h):
            r = bias[:, 128 * row:128 + 128 * row].rearrange("p (o d) -> p o d", o=1).broadcast_to((128, 4, 128))
            x = Xb[b].rearrange("p (t d) -> p t d", t=4)
            m = pool.do(lambda e: e.tensor_tensor(x, x, r, ALU.add), h, xw[b], loads["rb"].all())
            xw[b] = [m]

        class Att:
            def __init__(self, n, hpg, vd, scale, wq, wk, bq, bk, wo, ready, row, expo=False, mask=False, bqm=None):
                self.n, self.hpg, self.vd, self.scale = n, hpg, vd, scale
                self.wq, self.wk, self.bq, self.bk, self.wo = wq, wk, bq, bk, wo
                self.ready, self.row, self.expo, self.mask = ready, row, expo, mask
                self.ng = NH // hpg

        def split(a, src_bank, n, out, part, bq, marks_ps, marks_out):
            P = PS[:, src_bank, 0:n]
            if a.expo:
                i, E, em = pt.take()
                m = act.do(lambda e: e.activation(E[0:96, 0:n], P[0:96, :], ACT.Exp, bias=bq, scale=1.0), marks_ps, em, a.ready)
                banks.free(src_bank, m)
                yield
                m1 = dve.do(lambda e: e.tensor_copy(out[0:96, :], E[0:96, 0:n]), m, marks_out)
                m2 = dve.do(lambda e: e.tensor_tensor(out[part:part + 32, :], E[part:part + 32, 0:n],
                                                      out[part:part + 32, :].bitcast(F32), ALU.subtract), m1)
                pt.free(i, m2)
                yield
                return m2
            if bq is None:
                m1 = act.do(lambda e: e.activation(out[0:96, :], P[0:96, :], ACT.Copy), marks_ps, marks_out)
                yield
                m2 = dve.do(lambda e: e.tensor_tensor(out[part:part + 32, :], P[part:part + 32, :],
                                                      out[part:part + 32, :].bitcast(F32), ALU.subtract), m1)
            else:
                m1 = act.do(lambda e: e.activation(out[0:96, :], P[0:96, :], ACT.Identity, bias=bq, scale=1.0),
                            marks_ps, marks_out, loads["cb"].all())
                yield
                m2 = dve.do(lambda e: e.scalar_tensor_tensor(out[part:part + 32, :], P[part:part + 32, :],
                                                             bq[part:part + 32, :],
                                                             out[part:part + 32, :].bitcast(F32),
                                                             ALU.add, ALU.subtract), m1)
            banks.free(src_bank, m2)
            yield
            return m2

        def keys(a, g, n, rhs, rhs_marks, kblk, k_marks):
            b, marks = yield from banks.get()
            m = pe.do(mm(PS[0:96, b, 0:n], a.wk[:, g, :], rhs), marks, rhs_marks, a.ready)
            yield
            i, sg, sm = stg.take()
            m = yield from split(a, b, n, sg[:, 0:n], 64, a.bk(g), [m], sm)
            mk = msk[0:RK, 0:16] if a.hpg == 4 else msk[0:RK, 16:32]
            for hh in range(a.hpg):
                h = g * a.hpg + hh
                if hh % 2:
                    ma = act.do(lambda e, hh=hh, h=h: e.activation(kblk(hh)[0:RK, :], sg[0:RK, 0:n].bitcast(F32), ACT.Copy,
                                                                   scale=mk[:, h:h + 1]), m, k_marks, ready_c)
                else:
                    md = dve.do(lambda e, hh=hh, h=h: e.tensor_scalar(kblk(hh)[0:RK, :], sg[0:RK, 0:n].bitcast(F32),
                                                                      mk[:, h:h + 1], None, ALU.mult), m, k_marks, ready_c)
            stg.free(i, ma, md)
            yield
            return [ma, md]

        def queries(a, g, par, hT, qs):
            b, marks = yield from banks.get()
            m = pe.do(mm(PS[0:96, b, :], a.wq[:, g, :], HT[:, 512 * par:512 * par + 512]), marks, hT, a.ready)
            yield
            m2 = yield from split(a, b, 512, qs(g), 32, a.bq(g), [m], qfree[par])
            return m2, m

        def row_maxima(par, reduced, qs, groups, q_marks):
            nonlocal mtfree
            b, marks = yield from banks.get()
            M = MX[:, 4 * RK * par:4 * RK * par + 4 * RK].rearrange("p (t c) -> p t c", t=4).bitcast(F32)
            for t in range(4):
                f = (lambda e, t=t: e.transpose(PS[0:RK, b, 128 * t:128 * t + 128], M[:, t, :], ident[:, :]))
                if t < 3:
                    pe.quiet(f, marks, reduced)
                else:
                    m = pe.do(f)
            yield
            m = dve.do(lambda e: e.tensor_copy(MT[RM:RK, :], PS[RM:RK, b, :]), m, mtfree)
            banks.free(b, m)
            for g in groups:
                mq[par].start(sp, qs(g)[RM:RK, :].bitcast(F32), MT[RM:RK, :].bitcast(F32), m, q_marks)
            mtfree = [mq[par].all()]
            yield
            return mq[par].all()

        ot_free = [[loads["zero"].all(), loads["zero3"].all()] for _ in range(4)]
        oc_free = []
        on = Slots([ON[:, 0:256], ON[:, 256:512]])

        def finish(a, par, ot_marks, dst, dst_marks, extra=None):
            nonlocal oc_free
            vd = a.vd
            nc2 = NH * vd // 128
            cb = []
            for c in range(nc2):
                i, o, om = yield from acc_bank.get()
                cb.append((o, om, i))
            for j in range(4):
                b, marks = yield from banks.get()
                for hg in range(4):
                    f = (lambda e, hg=hg, b=b, j=j: e.transpose(PS[:, b, 128 * hg:128 * hg + 128],
                                                                OT[:, 512 * hg + 128 * j:512 * hg + 128 * j + 128], ident[:, :]))
                    if hg < 3:
                        pe.quiet(f, marks, ot_marks)
                    else:
                        m = pe.do(f)
                yield
                O = PS[:, b, :].rearrange("p (h c) -> p h c", c=32)
                R = den[:, 64 * par + 16 * j:64 * par + 16 * j + 16]
                if extra is None:
                    m = dve.do(lambda e, R=R, O=O: e.reciprocal(R, O[:, :, vd]), m)
                else:
                    m = dve.do(lambda e, R=R, O=O, j=j: e.tensor_tensor(R, O[:, :, vd], extra[0](j), ALU.add), m, extra[1])
                    m = dve.do(lambda e, R=R: e.reciprocal(R, R), m)
                i, N, nm = on.take()
                m = dve.do(lambda e, N=N, O=O, R=R: e.tensor_tensor(
                    N[:, 0:NH * vd].rearrange("p (h c) -> p h c", c=vd), O[:, :, 0:vd],
                    R.rearrange("p (h o) -> p h o", o=1).broadcast_to((128, NH, vd)), ALU.mult), m, nm)
                banks.free(b, m)
                yield
                for c in range(nc2):
                    m2 = pe.do(lambda e, c=c, j=j, N=N: e.transpose(PS[:, cb[c][0], 128 * j:128 * j + 128],
                                                                    N[:, 128 * c:128 * c + 128], ident[:, :]), m, cb[c][1])
                on.free(i, m2)
                yield
            for hg in range(4):
                ot_free[hg] = [m2]
            done = []
            for c in range(nc2):
                m = act.do(lambda e, c=c: e.activation(OC[:, 512 * c:512 * c + 512], PS[:, cb[c][0], :], ACT.Copy), m2, oc_free)
                acc_bank.free(cb[c][2], m)
            yield
            b, marks = yield from banks.get()
            for j in range(4):
                for c in range(nc2):
                    f = mm(PS[:, b, 128 * j:128 * j + 128], OC[:, 512 * c + 128 * j:512 * c + 128 * j + 128], a.wo[:, c, :],
                           c == 0, c == nc2 - 1)
                    if j < 3 or c < nc2 - 1:
                        pe.quiet(f, m, marks, a.ready)
                    else:
                        m2 = pe.do(f, m, marks)
            oc_free = [m2]
            yield
            m = dve.do(lambda e, b=b: e.tensor_tensor(dst, dst, PS[:, b, :], ALU.add), m2, dst_marks)
            banks.free(b, m)
            return m

        kall = KB[:, 0:NH * CK].rearrange("p (h k) -> p h k", h=NH)
        vall = VB[:, :].rearrange("p (b h c) -> p b h c", b=4, h=16)

        def prepare(a, wv, bvrow, bv_sign=None):
            nonlocal kfree, vfree
            kf, vf = kfree, vfree
            kfree, vfree = None, None
            a.kd = []
            for g0 in range(0, a.ng, 2):
                a.kd += yield from by_turns(*(keys(a, g, CK, CT[:, :], loads["ctx"].all(),
                                                   lambda hh, g=g: kall[:, g * a.hpg + hh, :], kf) for g in (g0, g0 + 1)))
            vd = a.vd
            vz = VB[0:NK, :].rearrange("p (g c) -> p g c", c=32)
            m0 = dve.do(lambda e: e.memset(vz[:, :, vd + 1:32], 0.0), vf)
            m0 = dve.do(lambda e: e.memset(vz[:, :, vd:vd + 1], 1.0), vf)
            n = NH * vd
            a.vd_marks = [m0]
            for b in range(NB):
                k, marks = yield from banks.get()
                m = pe.do(mm(PS[0:NK, k, 0:n], CT[:, NKP * b:NKP * b + NK], wv), marks, loads["ctx"].all(), a.ready)
                yield
                src = PS[0:NK, k, 0:n].rearrange("p (h c) -> p h c", c=vd)
                dst = vall[0:NK, b, :, 0:vd]
                if a.expo:
                    i, E, em = pt.take()
                    m = dve.do(lambda e, E=E, k=k: e.tensor_tensor(E[0:NK, 0:n], PS[0:NK, k, 0:n], bvrow, ALU.add), m, em)
                    banks.free(k, m)
                    m = act.do(lambda e, E=E, dst=dst: e.activation(dst, E[0:NK, 0:n].rearrange("p (h c) -> p h c", c=vd), ACT.Exp),
                               m, vf)
                    pt.free(i, m)
                elif bvrow is None:
                    m = dve.do(lambda e, dst=dst, src=src: e.tensor_copy(dst, src), m, vf)
                    banks.free(k, m)
                else:
                    m = dve.do(lambda e, dst=dst, src=src: e.tensor_tensor(dst, src, bvrow.rearrange("p (h c) -> p h c", c=vd), ALU.add),
                               m, vf, loads["rb"].all())
                    banks.free(k, m)
                a.vd_marks.append(m)
                yield

        def cross_front(a, b, par, qbuf, h):
            hT = yield from turn_norm(par, h)
            qs = lambda g: qbuf[par][:, 512 * g:512 * g + 512]
            qm = []
            for g in range(0, a.ng, 2):
                for m, read in (yield from by_turns(queries(a, g, par, hT, qs), queries(a, g + 1, par, hT, qs))):
                    qm.append(m)
            htfree[par] = [(pe.sem, pe.n)]
            M = MX[:, 4 * RK * par:4 * RK * par + 4 * RK].rearrange("p (t c) -> p t c", t=4)
            per = 1 if a.hpg == 4 else 3
            nr = a.hpg * NKP
            for t in range(4):
                for g0 in range(0, a.ng, per):
                    gs = range(g0, min(g0 + per, a.ng))
                    k, marks = yield from banks.get()
                    for g in gs:
                        o = PS[:, k, nr * (g - g0):nr * (g - g0) + nr]
                        l = qs(g)[0:RM, 128 * t:128 * t + 128]
                        r = kall[0:RM, g * a.hpg:(g + 1) * a.hpg, NKP * b:NKP * b + NKP]
                        if a.mask:
                            pe.quiet(mm(o, l, r, True, False), marks, qm[g], a.kd[g])
                            m = pe.do(mm(o.rearrange("p (h k) -> p h k", k=NKP)[:, :, 0:NK], mkb[0:NK, 512 * b + 128 * t:512 * b + 128 * t + 128],
                                         negI[0:NK, 0:4 * NK], False, True), a.mask_ready)
                        else:
                            m = pe.do(mm(o, l, r), marks, qm[g], a.kd[g])
                    yield
                    nh_ = len(gs) * a.hpg
                    src = PS[:, k, 0:nh_ * NKP].rearrange("p (h k) -> p h k", k=NKP)[:, :, 0:NK]
                    dst = M[:, t, RM + g0 * a.hpg:RM + g0 * a.hpg + nh_]
                    m = dve.do(lambda e, dst=dst, src=src: e.tensor_reduce(dst, src, AX, ALU.max), m, mxfree[par])
                    banks.free(k, m)
            extra = None
            if a.mask:
                m = dve.do(lambda e: e.tensor_scalar(M[:, :, RM:RK], M[:, :, RM:RK].bitcast(F32), 0.0, None, ALU.max), m)
                X1 = rt[:, 512 * par:512 * par + 64].rearrange("p (t h) -> p t h", t=4)
                me = act.do(lambda e: e.activation(X1, M[:, :, RM:RK].bitcast(F32), ACT.Exp, bias=0.0, scale=-a.scale), m, rtfree[par])
                rtfree[par] = None
                extra = (lambda j: X1[:, j, :], me)
            mt = yield from row_maxima(par, m, qs, range(a.ng), qfree[par])
            mxfree[par] = [(pe.sem, pe.n)] + ([extra[1]] if extra else [])
            qfree[par] = None
            return qs, qm, mt, extra

        def cross_back(a, b, par, state):
            nonlocal kfree, vfree
            qs, qm, mt, extra = state
            ot = []

            def scores(hg):
                res = []
                for i in range(4):
                    h = 4 * hg + i
                    g = h // a.hpg
                    k, marks = yield from banks.get()
                    l = kall[0:RK, h, NKP * b:NKP * b + NK]
                    if a.mask:
                        pe.quiet(mm(PS[0:NK, k, :], l, qs(g)[0:RK, :], True, False), marks, mt, qm[g], a.kd[g])
                        m = pe.do(mm(PS[0:NK, k, :], negI[0:NK, 0:NK], mkb[0:NK, 512 * b:512 * b + 512], False, True), a.mask_ready)
                    else:
                        m = pe.do(mm(PS[0:NK, k, :], l, qs(g)[0:RK, :]), marks, mt, qm[g], a.kd[g])
                    s, P, pm = pt.take()
                    m = act.do(lambda e, P=P, k=k: e.activation(P[0:NK, :], PS[0:NK, k, :], ACT.Exp, bias=0.0, scale=a.scale), m, pm)
                    banks.free(k, m)
                    res.append((h, s, P, m))
                    yield
                return res

            def values(hg, res):
                i6, o, om = yield from acc_bank.get()
                for i, (h, s, P, m) in enumerate(res):
                    f = mm(PS[32 * i:32 * i + 32, o, :], vall[0:NK, b, h, :], P[0:NK, :])
                    if i < 3:
                        pe.quiet(f, [r[3] for r in res], om, a.vd_marks)
                    else:
                        m = pe.do(f)
                yield
                for (h, s, P, _) in res:
                    pt.free(s, m)
                m = dve.do(lambda e, o=o: e.tensor_copy(OT[:, 512 * hg:512 * hg + 512], PS[:, o, :]), m, ot_free[hg])
                acc_bank.free(i6, m)
                ot.append(m)

            last = yield from scores(0)
            for hg in range(4):
                nxt = (yield from scores(hg + 1)) if hg < 3 else None
                yield from values(hg, last)
                last = nxt
            qfree[par] = [(pe.sem, pe.n)]
            kfree = [(pe.sem, pe.n)]
            vfree = [(pe.sem, pe.n)]

            def tail():
                m = yield from finish(a, par, ot, Xb[b], xw[b], extra)
                if extra:
                    rtfree[par] = [m]
                xw[b] = [m]

            return tail()

        def route_common(L, par, k0, lm):
            R = rt[:, 512 * par + k0:512 * par + k0 + 128]
            v = R[:, 0:4]
            r = R[:, 8:40].rearrange("p (t e) -> p t e", t=4)
            mx = R[:, 4:8]
            oh = R[:, 40:72].rearrange("p (t e) -> p t e", t=4)
            m = dve.do(lambda e: e.tensor_reduce(v, L, AX, ALU.max), lm)
            yield
            vb = v.rearrange("p (t o) -> p t o", o=1).broadcast_to((128, 4, 8))
            m = dve.do(lambda e: e.tensor_tensor(r, L, vb, ALU.is_equal), m)
            yield
            m = dve.do(lambda e: e.tensor_tensor(r, r, rev[:, :].rearrange("p (t e) -> p t e", t=4), ALU.mult), m, loads["c2"].all())
            yield
            m = dve.do(lambda e: e.tensor_reduce(mx, r, AX, ALU.max), m)
            yield
            m = dve.do(lambda e: e.tensor_tensor(oh, r, mx.rearrange("p (t o) -> p t o", o=1).broadcast_to((128, 4, 8)), ALU.is_equal), m)
            yield
            return v, oh, m

        def moe_front(kind, b, par, li, h, hT, H=None, hv=None):
            G = gates[:, 8 * li:8 * li + 8]
            hv = HT[:, 512 * par:512 * par + 512] if hv is None else hv
            k, marks = yield from banks.get()
            for t in range(4):
                f = mm(PS[:, k, 8 * t:8 * t + 8], hv[:, 128 * t:128 * t + 128], G)
                if t < 3:
                    pe.quiet(f, marks, hT, loads["c2"].all())
                else:
                    m = pe.do(f)
            yield
            Rt = rt[:, 512 * par:512 * par + 448]
            L = Rt[:, 0:32].rearrange("p (t e) -> p t e", t=4)
            W = Rt[:, 32:68].rearrange("p (t e) -> p t e", t=4)
            psl = PS[:, k, 0:32].rearrange("p (t e) -> p t e", t=4)
            if kind == 0:
                m = dve.do(lambda e: e.tensor_copy(L, psl), m, rtfree[par])
                yield
            else:
                gb = rt[:, 960:968].rearrange("p (o e) -> p o e", o=1).broadcast_to((128, 4, 8))
                m = dve.do(lambda e: e.tensor_tensor(L, psl, gb, ALU.add), m, rtfree[par], loads["rb"].all())
                yield
            banks.free(k, m)
            v1, oh1, m = yield from route_common(L, par, 80, m)
            W8 = W[:, :, 0:8]
            bc = lambda ap: ap.rearrange("p (t o) -> p t o", o=1).broadcast_to((128, 4, 8))
            if kind == 0:
                L2 = Rt[:, 352:384].rearrange("p (t e) -> p t e", t=4)
                m = dve.do(lambda e: e.scalar_tensor_tensor(L2, oh1, -BIG, L, ALU.mult, ALU.add), m)
                yield
                v2, oh2, m = yield from route_common(L2, par, 208, m)
                gv = Rt[:, 384:392]
                T = Rt[:, 392:404]
                m = dve.do(lambda e: e.tensor_copy(gv[:, 0:4], v1), m)
                yield
                m = dve.do(lambda e: e.tensor_copy(gv[:, 4:8], v2), m)
                yield
                m = act.do(lambda e: e.activation(gv, gv, ACT.Exp, bias=0.0, scale=-1.0), m)
                yield
                m = dve.do(lambda e: e.tensor_scalar(gv, gv, 1.0, None, ALU.add), m)
                yield
                m = dve.do(lambda e: e.reciprocal(gv, gv), m)
                yield
                m = dve.do(lambda e: e.tensor_tensor(T[:, 0:4], gv[:, 0:4], gv[:, 4:8], ALU.add), m)
                yield
                m = dve.do(lambda e: e.tensor_scalar(T[:, 0:4], T[:, 0:4], 3.0, None, ALU.mult), m)
                yield
                m = dve.do(lambda e: e.reciprocal(T[:, 4:8], T[:, 0:4]), m)
                yield
                m = dve.do(lambda e: e.tensor_tensor(gv.rearrange("p (a t) -> p a t", a=2), gv.rearrange("p (a t) -> p a t", a=2),
                                                     T[:, 4:8].rearrange("p (o t) -> p o t", o=1).broadcast_to((128, 2, 4)), ALU.mult), m)
                m = dve.do(lambda e: e.tensor_tensor(W8, oh1, bc(gv[:, 0:4]), ALU.mult), m)
                yield
                m = dve.do(lambda e: e.tensor_tensor(L2, oh2, bc(gv[:, 4:8]), ALU.mult), m)
                yield
                m = dve.do(lambda e: e.tensor_tensor(W8, W8, L2, ALU.add), m)
                yield
                m = dve.do(lambda e: e.memset(W[:, :, 8:9], 1.0 / 3.0), m)
                yield
            else:
                E = Rt[:, 352:384].rearrange("p (t e) -> p t e", t=4)
                P1 = Rt[:, 384:392]
                me = dve.do(lambda e: e.tensor_tensor(E, L, bc(v1), ALU.subtract), m)
                yield
                me = act.do(lambda e: e.activation(E, E, ACT.Exp), me)
                yield
                me = dve.do(lambda e: e.tensor_reduce(P1[:, 0:4], E, AX, ALU.add), me)
                yield
                me = dve.do(lambda e: e.reciprocal(P1[:, 4:8], P1[:, 0:4]), me)
                yield
                pv = prev[:, 32 * b:32 * b + 40]
                mp = m
                for t in range(4):
                    mp = dve.do(lambda e, t=t: e.tensor_tensor(pv[:, 8 * t + 8:8 * t + 16], pv[:, 8 * t:8 * t + 8], oh1[:, t, :], ALU.add), mp, k_prev)
                k, marks = yield from banks.get()
                ohf = Rt[:, 120:152]
                pe.quiet(mm(PS[:, k, 0:32], tri[:, :], ohf, True, False), marks, m, loads["c2"].all())
                m = pe.do(mm(PS[:, k, 0:32], ones[:, :], pv[:, 0:32], False, True), mp, k_ones)
                psl2 = PS[:, k, 0:32].rearrange("p (t e) -> p t e", t=4)
                C = Rt[:, 400:432].rearrange("p (t e) -> p t e", t=4)
                C2 = Rt[:, 208:240].rearrange("p (t e) -> p t e", t=4)
                off = off1[:, :].rearrange("p (t e) -> p t e", t=4)
                mc = dve.do(lambda e: e.tensor_tensor(C, psl2, off, ALU.add), m, loads["c2"].all())
                mc = dve.do(lambda e: e.tensor_scalar(C2, psl2, CAP + 0.5, 10000.0, ALU.is_gt, ALU.mult), mc)
                mc = dve.do(lambda e: e.tensor_tensor(C, C, C2, ALU.add), mc)
                mc = dve.do(lambda e: e.tensor_tensor(C, C, oh1, ALU.mult), mc)
                yield
                mc = dve.do(lambda e: e.tensor_reduce(Rt[:, 440:444], C, AX, ALU.add), mc)
                mi = dve.do(lambda e: e.tensor_copy(ints[:, 4 * b:4 * b + 4], Rt[:, 440:444]), mc)
                mi = dve.do(lambda e: e.tensor_scalar(Rt[:, 444:448], Rt[:, 440:444], 8.0 * CAP - 1.0, None, ALU.min), mi)
                mi = dve.do(lambda e: e.tensor_copy(ints[:, 16 + 4 * b:20 + 4 * b], Rt[:, 444:448]), mi)
                yield
                for t in range(4):
                    sc1[b].scatter(pool, dbuf, ints[:, 4 * b + t:4 * b + t + 1], H[:, 128 * t:128 * t + 128],
                                   8 * CAP - 1, mi, h, loads["zero"].all())
                m = dve.do(lambda e: e.scalar_tensor_tensor(W8, psl2, CAP + 0.5, oh1, ALU.is_le, ALU.mult), m)
                yield
                banks.free(k, m)
                m = dve.do(lambda e: e.tensor_reduce(keep[:, 4 * b:4 * b + 4], W8, AX, ALU.add), m)
                m = dve.do(lambda e: e.tensor_tensor(keep[:, 4 * b:4 * b + 4], keep[:, 4 * b:4 * b + 4], P1[:, 4:8], ALU.mult), m, me)
                k1["slot", b], k1["w", b] = mi, m
                rtfree[par] = [m, mi]
                return None
            rtfree[par] = None
            return hT, W, m

        sc1 = [Loads(sem(f"sc1{b}")) for b in range(NB)]
        ex = [Loads(sem("exa")), Loads(sem("exb"))]
        eo = [Loads(sem("eoa")), Loads(sem("eob"))]
        gq = [Loads(sem(f"gq{b}")) for b in range(NB)]
        k1 = {}

        def capacity_experts():
            nonlocal oc_free
            raws, outs = Slots([OT[:, 0:512], OT[:, 512:1024]]), Slots([OT[:, 1024:1536], OT[:, 1536:2048]])
            for i in range(2):
                raws.free(i, ot_free[i])
                outs.free(i, ot_free[2 + i])
            xts = Slots([OC[:, 0:512], OC[:, 512:1024]])
            xts.free(0, oc_free)
            xts.free(1, oc_free)
            rdy = loads["l1f"].all()
            P3 = [(0, 128), (128, 128), (256, 64)]

            def fetch(x):
                i, raw, rm = raws.take()
                q = ex[x % 2]
                q.start(sp, raw[:, 0:256].rearrange("p (t d) -> p t d", t=2),
                        dbuf[CAP * x:CAP * x + 256, :].rearrange("(t p) d -> p t d", p=128), [s.all() for s in sc1], rm)
                q.start(sp, raw[0:64, 256:384], dbuf[CAP * x + 256:CAP * x + CAP, :])
                return i, raw, q.all()

            def turn(i, raw, rm):
                k, m1 = yield from banks.get()
                for n, (a, w) in enumerate(P3):
                    f = (lambda e, a=a, w=w, n=n: e.transpose(PS[:, k, a:a + w], raw[0:w, 128 * n:128 * n + 128], ident[0:w, 0:w]))
                    if n < 2:
                        pe.quiet(f, m1, rm)
                    else:
                        m = pe.do(f)
                raws.free(i, m)
                j, xt, xm = xts.take()
                m = dve.do(lambda e: e.tensor_copy(xt[:, 0:CAP], PS[:, k, 0:CAP]), m, xm)
                banks.free(k, m)
                yield
                return j, xt, m

            def up(x, j, xt, xm):
                res = []
                for c in range(4):
                    k, m1 = yield from banks.get()
                    m = pe.do(mm(PS[:, k, 0:CAP], w1e[:, x, 128 * c:128 * c + 128], xt[:, 0:CAP]), m1, xm, rdy)
                    s, P, pm = pt.take()
                    bb = b1t[:, 4 * x + c:4 * x + c + 1]
                    if c % 2:
                        m2 = dve.do(lambda e, P=P, k=k, bb=bb: e.tensor_scalar(P[:, 0:CAP], PS[:, k, 0:CAP], bb, 0.0, ALU.add, ALU.max),
                                    m, pm, loads["l2"].all())
                    else:
                        m2 = act.do(lambda e, P=P, k=k, bb=bb: e.activation(P[:, 0:CAP], PS[:, k, 0:CAP], ACT.Relu, bias=bb, scale=1.0),
                                    m, pm, loads["l2"].all())
                    banks.free(k, m2)
                    res.append((s, P, m2))
                    yield
                xts.free(j, m)
                return res

            def down(x, res):
                k, m1 = yield from banks.get()
                for n, (a, w) in enumerate(P3):
                    for c in range(4):
                        f = mm(PS[0:w, k, 128 * n:128 * n + 128], res[c][1][:, a:a + w], w2e[:, x, c, :], c == 0, c == 3)
                        if n == 2 and c == 3:
                            m = pe.do(f)
                        else:
                            pe.quiet(f, m1, [r[2] for r in res])
                for r in res:
                    pt.free(r[0], m)
                yield
                i, o, om = outs.take()
                bb = b2r[:, 128 * x:128 * x + 128]
                b3 = bb.rearrange("p (o d) -> p o d", o=1).broadcast_to((128, 2, 128))
                m2 = dve.do(lambda e: e.tensor_tensor(o[:, 0:256].rearrange("p (t d) -> p t d", t=2),
                                                      PS[:, k, 0:256].rearrange("p (t d) -> p t d", t=2), b3, ALU.add), m, om, loads["l1b"].all())
                m3 = dve.do(lambda e: e.tensor_tensor(o[0:64, 256:384], PS[0:64, k, 256:384], bb[0:64, :], ALU.add), m)
                banks.free(k, m3)
                eo[i].start(sp, dout[CAP * x:CAP * x + 256, :].rearrange("(t p) d -> p t d", p=128),
                         o[:, 0:256].rearrange("p (t d) -> p t d", t=2), m3)
                eo[i].start(sp, dout[CAP * x + 256:CAP * x + CAP, :], o[0:64, 256:384])
                outs.free(i, eo[i].all())

            raw = fetch(0)
            t = yield from turn(*raw)
            raw = fetch(1)
            last = yield from up(0, *t)
            for x in range(8):
                nxt = None
                if x < 7:
                    t = yield from turn(*raw)
                    if x < 6:
                        raw = fetch(x + 2)
                    nxt = yield from up(x + 1, *t)
                yield from down(x, last)
                last = nxt
            for i in range(4):
                ot_free[i] = [eo[0].all(), eo[1].all(), (pe.sem, pe.n)]
            oc_free = [(pe.sem, pe.n)]

        def route(b):
            par = b % 2
            i, H, im = pt.take()
            h = yield from layernorm(Xb[b], H, 2, xw[b], im)
            j, T, jm = pt.take()
            k, marks = yield from banks.get()
            for t in range(4):
                f = (lambda e, t=t: e.transpose(PS[:, k, 128 * t:128 * t + 128], H[:, 128 * t:128 * t + 128], ident[:, :]))
                if t < 3:
                    pe.quiet(f, h, ready_c, marks)
                else:
                    turned = pe.do(f)
            yield
            hT = act.do(lambda e: e.activation(T, PS[:, k, :], ACT.Copy), turned, jm)
            banks.free(k, hT)
            yield
            yield from moe_front(1, b, par, 1, h, hT, H, T)
            pt.free(i, turned, sc1[b].all())
            pt.free(j, (pe.sem, pe.n))

        def gather(b):
            for t in range(4):
                c = 512 * b + 128 * t
                gq[b].gather(pool, OT[:, c:c + 128], dout, ints[:, 16 + 4 * b + t:17 + 4 * b + t], 8 * CAP - 1,
                             k1["slot", b], ot_free[b])

        def combine_norm(b, par):
            G = OT[:, 512 * b:512 * b + 512]
            gm = gq[b].all()
            for t in range(4):
                x = Xb[b][:, 128 * t:128 * t + 128]
                m = dve.do(lambda e, t=t, x=x: e.scalar_tensor_tensor(x, G[:, 128 * t:128 * t + 128], keep[:, 4 * b + t:4 * b + t + 1],
                                                                      x, ALU.mult, ALU.add), gm, k1["w", b], xw[b])
            xw[b] = [m]
            ot_free[b] = [m]
            yield
            h = yield from norm(b, par)
            if b < 2:
                gather(b + 2)
            return h

        def combine(b, W, wm, e_, k, m):
            ms = []
            for t in range(4):
                x = Xb[b][:, 128 * t:128 * t + 128]
                ms.append(dve.do(lambda e, t=t, x=x: e.scalar_tensor_tensor(x, PS[:, k, 128 * t:128 * t + 128], W[:, t, e_:e_ + 1],
                                                                            x, ALU.mult, ALU.add), m, wm, xw[b]))
            banks.free(k, ms[-1])
            xw[b] = [ms[-1]]

        def gated_back(b, par, state):
            hT, W, wm = state
            hv = HT[:, 512 * par:512 * par + 512]
            rdy = loads["l0f"].all()

            def up(x):
                res = []
                for c in range(2):
                    kg, m1 = yield from banks.get()
                    mg = pe.do(mm(PS[:, kg, :], W13[:, x, 128 * c:128 * c + 128], hv), m1, hT, rdy)
                    ku, m1 = yield from banks.get()
                    mu = pe.do(mm(PS[:, ku, :], W13[:, x, 256 + 128 * c:384 + 128 * c], hv), m1)
                    s, P, pm = pt.take()
                    m = act.do(lambda e, P=P, kg=kg: e.activation(P, PS[:, kg, :], ACT.Silu), mg, pm)
                    banks.free(kg, m)
                    m = dve.do(lambda e, P=P, ku=ku: e.tensor_tensor(P, P, PS[:, ku, :], ALU.mult), m, mu)
                    banks.free(ku, m)
                    res.append((s, P, m))
                    yield
                return res

            def down(x, res):
                k, m1 = yield from banks.get()
                for t in range(4):
                    for c in range(2):
                        f = mm(PS[:, k, 128 * t:128 * t + 128], res[c][1][:, 128 * t:128 * t + 128], W2m[:, x, c, :], c == 0, c == 1)
                        if t == 3 and c == 1:
                            m = pe.do(f)
                        else:
                            pe.quiet(f, m1, [r[2] for r in res])
                for r in res:
                    pt.free(r[0], m)
                yield
                combine(b, W, wm, x, k, m)

            last = yield from up(0)
            for x in range(9):
                nxt = (yield from up(x + 1)) if x < 8 else None
                yield from down(x, last)
                last = nxt
            htfree[par] = [(pe.sem, pe.n)]
            rtfree[par] = list(xw[b])

        def gated_front(b, par, h):
            hT = yield from turn_norm(par, h)
            return (yield from moe_front(0, b, par, 0, h[0], hT))

        WR0 = S2[:, 0:768]
        wr0 = WR0.rearrange("p (g q c) -> p g q c", g=8, q=3)
        wv0 = S0[:, 768:1024]
        l0r = loads["l0"].all()
        F8 = S0[:, 760:768].rearrange("p (o e) -> p o e", o=1).broadcast_to((128, 32, 8))
        blk = S0[:, 768:1024].rearrange("p (a e) -> p a e", e=8)
        m = dve.do(lambda e: e.tensor_tensor(blk, blk, F8, ALU.mult), l0r)
        for q in range(3):
            mw0 = dve.do(lambda e, q=q: e.tensor_copy(wr0[:, :, q, :], wv0.rearrange("p (g c) -> p g c", g=8)), m)
        m = dve.do(lambda e: e.tensor_tensor(cols[0:96, 0:1], cols[0:96, 0:1], cols[0:96, 1:2], ALU.mult), loads["l0b"].all())
        bv0 = OC[0:NK, 0:256]
        mw0 = dve.do(lambda e: e.tensor_tensor(bv0, bv0, OC[0:NK, 256:512], ALU.mult), loads["l0b"].all())

        wrap = WR0.rearrange("p (g c) -> p g c", g=8)
        a0 = Att(0, 2, 16, 1.0 / float(np.sqrt(np.float32(128))), wrap, wrap, lambda g: cols[0:96, 0:1], lambda g: cols[0:96, 0:1],
                 S0[:, 1024:1280].rearrange("p (c n) -> p c n", c=2), [l0r, mw0], 0, expo=True)

        units = []
        for b in range(NB):
            units.append((lambda par, b=b: norm(b, par, 0), lambda par, h, b=b: cross_front(a0, b, par, Q0, h), lambda par, s, b=b: cross_back(a0, b, par, s), f"l0x{b}"))

        for b in range(NB):
            units.append((lambda par, b=b: norm(b, par), lambda par, h, b=b: gated_front(b, par, h), lambda par, s, b=b: gated_back(b, par, s), f"l0f{b}"))

        w1v = S1[:, :]
        a1 = Att(1, 4, 8, 1.0 / float(np.sqrt(np.float32(8))),
                 w1v[:, 0:384].rearrange("p (g c) -> p g c", g=4), w1v[:, 384:768].rearrange("p (g c) -> p g c", g=4),
                 lambda g: cols[0:96, 2 + g:3 + g], lambda g: cols[0:96, 6 + g:7 + g],
                 w1v[:, 896:1024].rearrange("p (c n) -> p c n", c=1), [loads["l1"].all(), loads["cb"].all()], 1)
        QQ = [QB[:, 0:2048], QB[:, 2048:4096]]
        for b in range(NB):
            units.append((lambda par, b=b: norm(b, par, 1), lambda par, h, b=b: cross_front(a1, b, par, QQ, h), lambda par, s, b=b: cross_back(a1, b, par, s), f"l1x{b}"))
        w1e = RB[:, 0:4096].rearrange("p (e n) -> p e n", e=8)
        w2e = RB[:, 4096:8192].rearrange("p (e c n) -> p e c n", e=8, c=4)

        units2 = []

        KP = RB[:, 0:CK]
        VP = RB[:, 512:1024]
        QP = RB[:, 1024:2048]
        S2v = S2[:, :]
        l2 = {}

        def l2_prepare():
            end1 = [(pe.sem, pe.n)]
            l2["free"] = end1
            load("l2m", mkf[0:NK, :], A["mfT"], end1)
            for i in range(2):
                ltfree[i], w12free[i] = end1, end1
            k, marks = yield from banks.get()
            m = pe.do(mm(PS[:, k, 0:CK], S2v[:, 128:256], CT[:, :]), marks, loads["l2w"].all())
            m = act.do(lambda e, k=k: e.activation(KP, PS[:, k, 0:CK], ACT.Relu, bias=cols[:, 11:12], scale=1.0), m, end1)
            banks.free(k, m)
            l2["k"] = m
            k, marks = yield from banks.get()
            for b in range(NB):
                f = mm(PS[0:NK, k, 128 * b:128 * b + 128], CT[:, NKP * b:NKP * b + NK], S2v[:, 256:384])
                if b < 3:
                    pe.quiet(f, marks)
                else:
                    m = pe.do(f)
            vb = bias[0:NK, 128 * 6:128 * 7].rearrange("p (o d) -> p o d", o=1).broadcast_to((NK, 4, 128))
            vv = VP[0:NK, 0:512].rearrange("p (b d) -> p b d", b=4)
            m = dve.do(lambda e: e.tensor_tensor(vv, PS[0:NK, k, :].rearrange("p (b d) -> p b d", b=4), vb, ALU.add), m, end1)
            banks.free(k, m)
            l2["v"] = dve.do(lambda e: e.tensor_scalar(VP[0:NK, 0:512], VP[0:NK, 0:512], 0.0, None, ALU.max), m)
            yield

        qpfree = [None, None]

        def l2x_front(b, par, h):
            hT = yield from turn_norm(par, h)
            k, marks = yield from banks.get()
            m = pe.do(mm(PS[:, k, :], S2v[:, 0:128], HT[:, 512 * par:512 * par + 512]), marks, hT, loads["l2w"].all())
            htfree[par] = [m]
            yield
            qp = QP[:, 512 * par:512 * par + 512]
            qpfree[par] = qpfree[par] or l2["free"]
            m = act.do(lambda e: e.activation(qp, PS[:, k, :], ACT.Relu, bias=cols[:, 10:11], scale=1.0), m, qpfree[par])
            banks.free(k, m)
            return qp, m

        def l2x_back(b, par, state):
            qp, m = state
            k, marks = yield from banks.get()
            m = pe.do(mm(PS[0:NK, k, :], KP[:, NKP * b:NKP * b + NK], qp), m, marks, l2["k"])
            qpfree[par] = [m]
            yield
            s, P, pm = pt.take()
            m = act.do(lambda e: e.activation(P[0:NK, :], PS[0:NK, k, :], ACT.Relu, bias=0.0, scale=1.0 / float(np.sqrt(np.float32(128)))), m, pm)
            banks.free(k, m)
            m = dve.do(lambda e: e.tensor_tensor(P[0:NK, :], P[0:NK, :], mkf[0:NK, :], ALU.add), m, loads["l2m"].all())
            yield
            k2, marks = yield from banks.get()
            for t in range(4):
                f = mm(PS[:, k2, 128 * t:128 * t + 128], P[0:NK, 128 * t:128 * t + 128], VP[0:NK, 128 * b:128 * b + 128])
                if t < 3:
                    pe.quiet(f, m, marks, l2["v"])
                else:
                    m = pe.do(f)
            pt.free(s, m)
            yield
            m = dve.do(lambda e: e.scalar_tensor_tensor(Xb[b], PS[:, k2, :], 0.0, Xb[b], ALU.max, ALU.add), m, xw[b])
            banks.free(k2, m)
            xw[b] = [m]

        for b in range(NB):
            units2.append((lambda par, b=b: combine_norm(b, par), lambda par, h, b=b: l2x_front(b, par, h), lambda par, s, b=b: l2x_back(b, par, s), f"l2x{b}"))

        LT = RB[:, 2048:6144]
        W1x = RB[:, 6144:7168]
        W2x = RB[:, 7168:8192]
        lq = [Loads(sem("lq0")), Loads(sem("lq1"))]
        ltfree = [[], []]
        w12free = [[], []]

        def l2f_front(b, par, h):
            H = Ht[:, 512 * par:512 * par + 512]
            hT = yield from turn_norm(par, h)
            lt = LT[64 * par:64 * par + 1, 0:2048]
            lq[par].start(sp, lt.rearrange("o (t d) -> o t d", t=16), H[1:17, 0:128], h[0], ltfree[par])
            lm = lq[par].all()
            hfree[par] = hfree[par] + [lm]
            yield
            yield
            row = lambda t: lt[:, 128 * t:128 * t + 128]
            w1 = W1x[:, 512 * par:512 * par + 512]
            w2 = W2x[:, 512 * par:512 * par + 512]
            k, marks = yield from banks.get()
            for i in range(4):
                f = mm(PS[:, k, 128 * i:128 * i + 128], row(2 * i + 1), row(2 * i))
                if i < 3:
                    pe.quiet(f, marks, lm)
                else:
                    m = pe.do(f)
            yield
            m1 = dve.do(lambda e, k=k: e.scalar_tensor_tensor(w1, PS[:, k, :], cols[:, 12:13], S2v[:, 384:896], ALU.mult, ALU.add),
                        m, w12free[par], loads["cb"].all(), loads["l2w"].all())
            banks.free(k, m1)
            k, marks = yield from banks.get()
            o = PS[:, k, :].rearrange("p (r o) -> p r o", r=4)
            for i in range(4):
                f = mm(o[:, :, 32 * i:32 * i + 32], row(2 * (4 + i) + 1),
                       row(2 * (4 + i)).rearrange("p (o r) -> p r o", r=4))
                if i < 3:
                    pe.quiet(f, marks)
                else:
                    m = pe.do(f)
            ltfree[par] = [m]
            yield
            m2 = dve.do(lambda e, k=k: e.scalar_tensor_tensor(w2, PS[:, k, :], cols[:, 12:13], S2v[:, 896:1408], ALU.mult, ALU.add), m)
            banks.free(k, m2)
            return hT, w1, w2, m1, m2

        def l2f_back(b, par, state):
            hT, w1, w2, m1, m2 = state
            res = []
            for c in range(4):
                k, marks = yield from banks.get()
                m = pe.do(mm(PS[:, k, :], w1[:, 128 * c:128 * c + 128], HT[:, 512 * par:512 * par + 512]), marks, hT, m1)
                s, P, pm = pt.take()
                m = act.do(lambda e, P=P, k=k, c=c: e.activation(P, PS[:, k, :], ACT.Gelu, bias=cols[:, 13 + c:14 + c], scale=1.0), m, pm)
                banks.free(k, m)
                res.append((s, P, m))
                yield
            htfree[par] = [(pe.sem, pe.n)]
            k, marks = yield from banks.get()
            for t in range(4):
                for c in range(4):
                    f = mm(PS[:, k, 128 * t:128 * t + 128], res[c][1][:, 128 * t:128 * t + 128], w2[:, 128 * c:128 * c + 128], c == 0, c == 3)
                    if t == 3 and c == 3:
                        m = pe.do(f)
                    else:
                        pe.quiet(f, marks, m2, [r[2] for r in res])
            for r in res:
                pt.free(r[0], m)
            w12free[par] = [m]
            yield
            m = dve.do(lambda e: e.tensor_tensor(Xb[b], Xb[b], PS[:, k, :], ALU.add), m, xw[b])
            banks.free(k, m)
            xw[b] = [m]

        for b in range(NB):
            units2.append((lambda par, b=b: norm(b, par, 2), lambda par, h, b=b: l2f_front(b, par, h), lambda par, s, b=b: l2f_back(b, par, s), f"l2f{b}"))

        w3 = S0[:, 0:1024]
        a3 = Att(3, 4, 8, float(8 ** -0.5),
                 w3[:, 0:384].rearrange("p (g c) -> p g c", g=4), w3[:, 384:768].rearrange("p (g c) -> p g c", g=4),
                 lambda g: None, lambda g: None,
                 w3[:, 896:1024].rearrange("p (c n) -> p c n", c=1), None, 3, mask=True)

        def l3x_masks():
            m = dve.do(lambda e: e.tensor_copy(mkb[0:NK, :], mk8[0:NK, :]), loads["l2"].all())
            i3 = ident[0:NK, 0:NK].rearrange("p (o k) -> p o k", o=1).broadcast_to((NK, 4, NK))
            a3.mask_ready = dve.do(lambda e: e.tensor_scalar(negI[0:NK, 0:4 * NK].rearrange("p (h k) -> p h k", h=4), i3, -BIG, None, ALU.mult), ready_c)

        for b in range(NB):
            units2.append((lambda par, b=b: norm(b, par, 3), lambda par, h, b=b: cross_front(a3, b, par, QQ, h), lambda par, s, b=b: cross_back(a3, b, par, s), f"l3x{b}"))

        w4 = S1[:, :]
        a4 = Att(4, 4, 8, 1.0 / float(np.sqrt(np.float32(8))),
                 w4[:, 0:384].rearrange("p (g c) -> p g c", g=4), w4[:, 384:768].rearrange("p (g c) -> p g c", g=4),
                 lambda g: cols[0:96, 17 + g:18 + g], lambda g: cols[0:96, 21 + g:22 + g],
                 w4[:, 896:1024].rearrange("p (c n) -> p c n", c=1), None, 4)
        Y = RB[:, 0:2048]
        Yb = [Y[:, 512 * b:512 * b + 512] for b in range(NB)]
        V4 = [RB[:, 2048:4096], RB[:, 4096:6144]]
        v4free = [[], []]
        kslots = Slots([KB[:, 2048 * i:2048 * i + 2048] for i in range(3)])
        k4 = {}
        q4free = [[], []]

        def l3_self_open(marks):
            for i in range(2):
                vz = V4[i].rearrange("p (g c) -> p g c", c=32)
                m = dve.do(lambda e, vz=vz: e.memset(vz[:, :, 9:32], 0.0), marks)
                m = dve.do(lambda e, vz=vz: e.memset(vz[:, :, 8:9], 1.0), marks)
                v4free[i] = [m]

        def self_norms(b, par):
            h0 = yield from layernorm(Xb[b], Yb[b], par, xw[b], k4["rb_free"])
            H = Ht[:, 512 * par:512 * par + 512]
            h = yield from layernorm(Yb[b], H, par, h0, hfree[par])
            hT, turned = yield from transposed(H, par, h, cols[:, 25:26], cols[:, 26:27])
            hfree[par] = [turned]
            r = bias[:, 128 * 4:128 * 5].rearrange("p (o d) -> p o d", o=1).broadcast_to((128, 4, 128))
            y = Yb[b].rearrange("p (t d) -> p t d", t=4)
            yw[b] = [pool.do(lambda e: e.tensor_tensor(y, y, r, ALU.add), h)]
            k, marks = yield from banks.get()
            hv = HT[:, 512 * par:512 * par + 512]
            for c in range(4):
                f = mm(PS[:, k, 128 * c:128 * c + 128], hv[:, 128 * c:128 * c + 128], w4[:, 768:896])
                if c < 3:
                    pe.quiet(f, marks, hT, a4.ready)
                else:
                    m = pe.do(f)
            yield
            bv = bias[:, 128 * 7:128 * 8].rearrange("p (h c) -> p h c", c=8)
            vv = V4[par].rearrange("p (c h k) -> p c h k", c=4, h=16)
            for c in range(4):
                src = PS[:, k, 128 * c:128 * c + 128].rearrange("p (h c) -> p h c", c=8)
                mv_ = dve.do(lambda e, c=c, src=src: e.tensor_tensor(vv[:, c, :, 0:8], src, bv, ALU.add), m, v4free[par])
            banks.free(k, mv_)
            v4free[par] = None
            return hT, vv, mv_

        def self_open(b, g, par, st):
            hT, vv, vm = st
            qs = lambda g: QQ[par][:, 512 * g:512 * g + 512]
            qm, read = yield from queries(a4, g, par, hT, qs)
            s, K, km = kslots.take()
            kv = K.rearrange("p (h k) -> p h k", h=4)
            kd = yield from keys(a4, g, 512, HT[:, 512 * par:512 * par + 512], hT, lambda hh: kv[:, hh, :], km)
            return s, kv, kd, qm

        def self_front(b, g, par, s, kv, kd, qm):
            qs = lambda g: QQ[par][:, 512 * g:512 * g + 512]
            M = MX[:, 4 * RK * par:4 * RK * par + 4 * RK].rearrange("p (t c) -> p t c", t=4)
            for t in range(4):
                for p2 in range(2):
                    i2, k, marks = yield from pairs.get()
                    for i in range(2):
                        f = mm(PS[:, k + i, :], qs(g)[0:RM, 128 * t:128 * t + 128], kv[0:RM, 2 * p2 + i, :])
                        if i:
                            m = pe.do(f)
                        else:
                            pe.quiet(f, marks, qm, kd)
                    yield
                    dst = M[:, t, RM + 4 * g + 2 * p2:RM + 4 * g + 2 * p2 + 2]
                    m = dve.do(lambda e, dst=dst, k=k: e.tensor_reduce(dst, PS[:, k:k + 2, :], AX, ALU.max), m, mxfree[par])
                    pairs.free(i2, m)
            mt = yield from row_maxima(par, m, qs, [g], q4free[par])
            mxfree[par] = [(pe.sem, pe.n)]
            return s, kv, kd, qm, mt

        def self_back(b, g, par, st, fr):
            hT, vv, vm = st
            s, kv, kd, qm, mt = fr
            qs = QQ[par][:, 512 * g:512 * g + 512]
            def scores(c):
                res = []
                for i in range(4):
                    k, marks = yield from banks.get()
                    m = pe.do(mm(PS[:, k, :], kv[0:RK, i, 128 * c:128 * c + 128], qs[0:RK, :]), marks, mt, qm, kd)
                    sl, P, pm = pt.take()
                    m = act.do(lambda e, P=P, k=k: e.activation(P, PS[:, k, :], ACT.Exp, bias=0.0, scale=a4.scale), m, pm)
                    banks.free(k, m)
                    res.append((sl, P, m))
                    yield
                return res

            def values(c, res):
                for i, (sl, P, m) in enumerate(res):
                    f = mm(PS[32 * i:32 * i + 32, o, :], vv[:, c, 4 * g + i, :], P, c == 0, c == 3)
                    if i < 3:
                        pe.quiet(f, [r[2] for r in res], om, vm)
                    else:
                        m = pe.do(f)
                for r in res:
                    pt.free(r[0], m)
                yield
                return m

            last = yield from scores(0)
            for c in range(4):
                nxt = (yield from scores(c + 1)) if c < 3 else None
                if c == 0:
                    i6, o, om = yield from acc_bank.get()
                m = yield from values(c, last)
                last = nxt
            kslots.free(s, m)
            m = dve.do(lambda e: e.tensor_copy(OT[:, 512 * g:512 * g + 512], PS[:, o, :]), m, ot_free[g])
            acc_bank.free(i6, m)
            return m

        pairs = Slots([0, 2])

        def self_attention(first_norms, tail):
            marks = banks.give([4, 5])
            banks.places.append(6)
            banks.read.append(acc_bank.give([1])[0])
            banks.order.append(6)
            pairs.free(0, *marks)
            pairs.free(1, *marks)
            st = [first_norms] + [None] * 3
            ots = []

            def first(b, g, par):
                if g == 0:
                    qfree[par] = q4free[par]
                op = yield from self_open(b, g, par, st[b])
                if g == 3:
                    htfree[par] = [(pe.sem, pe.n)]
                    qfree[par] = None
                return (b, g, par, st[b], op)

            def second(b, g, par, s, op):
                fr = yield from self_front(b, g, par, *op)
                return (b, g, par, s, fr)

            def third(b, g, par, s, fr):
                m = yield from self_back(b, g, par, s, fr)
                ots.append(m)
                if g == 3:
                    q4free[par] = [(pe.sem, pe.n)]
                    v4free[par] = [(pe.sem, pe.n)]
                    done = list(ots)
                    ots.clear()

                    def tail():
                        m = yield from finish(a4, par, done, Yb[b], yw[b])
                        yw[b] = [m]
                        xx = pool.do(lambda e: e.tensor_tensor(Xb[b], Xb[b], Yb[b], ALU.add), m, xw[b])
                        xw[b] = [xx]

                    return tail()

            q4free[0], q4free[1] = qfree[0], qfree[1]
            steps = [(b, g, b % 2) for b in range(NB) for g in range(4)]
            one, two = None, None
            for i in range(len(steps) + 2):
                b, g = steps[i][0:2] if i < len(steps) else (3, 1)
                streams = [(first(*steps[i]) if i < len(steps) else iter(()), 12),
                           (second(*one) if one else iter(()), 11),
                           (third(*two) if two else iter(()), 24, 0.1), (tail or iter(()), 36)]
                if g == 2 and b < 3:
                    streams.append((self_norms(b + 1, (b + 1) % 2), 15))
                if i in (6, 10, 14):
                    streams.append((route3((i - 6) // 4), 22, 0.4))
                if i == 11:
                    streams.append((place3(0), 20))
                one, two, tail, _, *more = together(*streams)
                if g == 2 and b < 3:
                    st[b + 1] = more[0]
                if i == 13:
                    x3["free"] = [(pe.sem, pe.n)]
            for k in range(4):
                banks.order.append(k)
                banks.read[k] = pairs.read[k // 2]
            return tail

        G3 = [S2[:, 0:512], S2[:, 512:1024], S0[:, 0:512], S0[:, 512:1024]]
        C3 = S2[:, 1024:1408]
        M3 = S0[:, 1024:1280]
        x3 = {}
        q3in = [Loads(sem(f"s3{b}")) for b in range(NB)]
        q3x = [Loads(sem(f"f3{i}")) for i in range(2)]
        q3o = [[Loads(sem(f"o3{g}{i}")) for i in range(4)] for g in range(2)]
        q3g = [Loads(sem(f"g3{b}")) for b in range(NB)]

        def bc(ap, shape):
            return ap.broadcast_to(shape)

        def route3(b):
            par = b % 2
            H = VB[:, 512 * b:512 * b + 512]
            h = yield from layernorm(Yb[b], H, 2, yw[b], x3["open"])
            j, T, jm = pt.take()
            k, marks = yield from banks.get()
            for t in range(4):
                f = (lambda e, t=t, k=k: e.transpose(PS[:, k, 128 * t:128 * t + 128], H[:, 128 * t:128 * t + 128], ident[:, :]))
                if t < 3:
                    pe.quiet(f, h, marks)
                else:
                    turned = pe.do(f)
            yield
            hT = act.do(lambda e, k=k: e.activation(T, PS[:, k, :], ACT.Identity, bias=cols[:, 28:29], scale=cols[:, 27:28]), turned, jm)
            banks.free(k, hT)
            yield
            k, marks = yield from banks.get()
            for t in range(4):
                f = mm(PS[:, k, 8 * t:8 * t + 8], T[:, 128 * t:128 * t + 128], gates[:, 16:24])
                if t < 3:
                    pe.quiet(f, marks, hT)
                else:
                    m = pe.do(f)
            pt.free(j, m)
            yield
            Rt = rt[:, 512 * par:512 * par + 448]
            L = Rt[:, 0:32].rearrange("p (t e) -> p t e", t=4)
            gb = rt[:, 968:976].rearrange("p (o e) -> p o e", o=1).broadcast_to((128, 4, 8))
            m = dve.do(lambda e, k=k: e.tensor_tensor(L, PS[:, k, 0:32].rearrange("p (t e) -> p t e", t=4), gb, ALU.add), m, rtfree[par])
            banks.free(k, m)
            rtfree[par] = None
            yield
            v1, oh1, m = yield from route_common(L, par, 80, m)
            moh = m
            pv = P3[b // 2][:, 32 * par:32 * par + 40]
            mp = [m, x3["p"][b // 2]]
            for t in range(4):
                mp = dve.do(lambda e, t=t: e.tensor_tensor(pv[:, 8 * t + 8:8 * t + 16], pv[:, 8 * t:8 * t + 8], oh1[:, t, :], ALU.add), mp)
            k, marks = yield from banks.get()
            pe.quiet(mm(PS[:, k, 0:32], tri[:, :], Rt[:, 120:152], True, False), marks, m)
            m = pe.do(mm(PS[:, k, 0:32], ones[:, :], pv[:, 0:32], False, True), mp)
            yield
            m = dve.do(lambda e, k=k: e.tensor_copy(Rt[:, 400:432], PS[:, k, 0:32]), m)
            banks.free(k, m)
            x3["rank", b] = [m, mp]
            k, marks = yield from banks.get()
            for t in range(4):
                f = (lambda e, t=t, k=k: e.transpose(PS[0:8, k, 128 * t:128 * t + 128], oh1[:, t, :], ident[:, :]))
                if t < 3:
                    pe.quiet(f, marks, moh)
                else:
                    mw = pe.do(f)
            yield
            wT = G3[b][0:8, :]
            mw = act.do(lambda e, k=k: e.activation(wT, PS[0:8, k, :], ACT.Copy), mw, x3["open"])
            banks.free(k, mw)
            yield
            k, marks = yield from banks.get()
            for t in range(4):
                f = mm(PS[:, k, 128 * t:128 * t + 128], wT[:, 128 * t:128 * t + 128], b2t[0:8, 128:256])
                if t < 3:
                    pe.quiet(f, marks, mw, loads["l2"].all())
                else:
                    m = pe.do(f)
            x3["g", b] = [m]
            yield
            m = dve.do(lambda e: e.tensor_tensor(Xb[b], Xb[b], PS[:, k, :], ALU.add), m, xw[b])
            banks.free(k, m)
            xw[b] = [m]

        BS = [CT[:, 0:60], CT[:, 60:120]]
        P3 = [CT[:, 120:192], CT[:, 192:264]]

        def place3(g):
            k, marks = yield from banks.get()
            m = pe.do(mm(PS[:, k, 0:8], ones[:, :], P3[g][:, 64:72]), marks, x3["rank", 2 * g + 1])
            yield
            c_k, c_low = C3[:, 0:64], C3[:, 64:128]
            c_tile, c_e = C3[:, 128:128 + 8 * NT], C3[:, 248:248 + 8 * NT]
            v8 = lambda ap: ap.rearrange("p (a b) -> p a b", b=8)
            cmp_, nt, base, T = M3[:, 0:64], M3[:, 64:72], M3[:, 72:80], M3[:, 80:80 + 8 * NT]
            b128, te = M3[:, 200:208], M3[:, 208:208 + NT]
            m = dve.do(lambda e: e.tensor_tensor(v8(cmp_), PS[:, k, 0:8].rearrange("p (e o) -> p e o", o=1).broadcast_to((128, 8, 8)),
                                                 v8(c_k), ALU.is_gt), m, loads["c3"].all(), x3["open"])
            banks.free(k, m)
            yield
            m = dve.do(lambda e: e.tensor_reduce(nt, v8(cmp_), AX, ALU.add), m)
            m = dve.do(lambda e: e.tensor_tensor(v8(cmp_), nt.rearrange("p (o e) -> p o e", o=1).broadcast_to((128, 8, 8)), v8(c_low), ALU.mult), m)
            yield
            mb = dve.do(lambda e: e.tensor_reduce(base, v8(cmp_), AX, ALU.add), m)
            m = dve.do(lambda e: e.tensor_scalar(b128, base, 128.0, -1.0, ALU.mult, ALU.add), mb)
            yield
            for b in (2 * g, 2 * g + 1):
                Rt = rt[:, 512 * (b % 2):512 * (b % 2) + 448]
                C, oh = v8(Rt[:, 400:432]), v8(Rt[:, 120:152])
                mc = dve.do(lambda e, C=C: e.tensor_tensor(C, C, b128.rearrange("p (o e) -> p o e", o=1).broadcast_to((128, 4, 8)), ALU.add),
                            m, x3["rank", b])
                mc = dve.do(lambda e, C=C, oh=oh: e.tensor_tensor(C, C, oh, ALU.mult), mc)
                yield
                mc = dve.do(lambda e, C=C, Rt=Rt: e.tensor_reduce(Rt[:, 432:436], C, AX, ALU.add), mc)
                mi = dve.do(lambda e, Rt=Rt, b=b: e.tensor_copy(ints3[:, 32 + 4 * b:36 + 4 * b], Rt[:, 432:436]), mc)
                x3["slot", b] = mi
                rtfree[b % 2] = [mi]
                yield
                for t in range(4):
                    q3in[b].scatter(pool, d3[g], ints3[:, 32 + 4 * b + t:33 + 4 * b + t], VB[:, 512 * b + 128 * t:512 * b + 128 * t + 128],
                                    128 * NT - 1, mi, loads["zero3"].all())
                yield
            m = dve.do(lambda e: e.tensor_tensor(v8(T), base.rearrange("p (o e) -> p o e", o=1).broadcast_to((128, NT, 8)), v8(c_tile), ALU.is_le), mb)
            m = dve.do(lambda e: e.tensor_reduce(te, v8(T), AX, ALU.add), m)
            yield
            m = dve.do(lambda e: e.tensor_scalar(te, te, -1.0, None, ALU.add), m)
            x3["te", g] = dve.do(lambda e: e.tensor_copy(ints3[:, 16 * g:16 * g + NT], te), m)
            yield
            m = dve.do(lambda e: e.tensor_tensor(v8(T), te.rearrange("p (i o) -> p i o", o=1).broadcast_to((128, NT, 8)), v8(c_e), ALU.is_equal),
                       x3["te", g])
            j, Q, jm = pt.take()
            Q4 = Q[:, 0:32 * NT].rearrange("p (i c e) -> p i c e", c=4, e=8)
            m = dve.do(lambda e: e.tensor_tensor(
                Q4, T.rearrange("p (i o e) -> p i o e", o=1, e=8).broadcast_to((128, NT, 4, 8)),
                b1t[:, 32:64].rearrange("p (o e c) -> p o c e", o=1, c=4).broadcast_to((128, NT, 4, 8)), ALU.mult), m, jm)
            yield
            m = dve.do(lambda e: e.tensor_reduce(BS[g], Q[:, 0:32 * NT].rearrange("p (i e) -> p i e", e=8), AX, ALU.add), m)
            pt.free(j, m)
            x3["bias", g] = m
            x3["t"] = m
            yield

        def experts3(g):
            V = V4[0]
            raws = Slots([V[:, 0:512], V[:, 512:1024]])
            xts = Slots([V[:, 1024:1536], V[:, 1536:2048]])
            for i in range(2):
                raws.free(i, x3["free"])
                xts.free(i, x3["free"])
            rdy = [loads["l3f"].all(), x3["te", g]]
            quads = [(512 * q, min(4, NT - 4 * q)) for q in range((NT + 3) // 4)]
            outs = {}
            xt = {}
            reg = {}

            def fetch(q):
                a, n = quads[q]
                i, raw, rm = raws.take()
                q3x[i].start(sp, raw[:, 0:128 * n].rearrange("p (t d) -> p t d", t=n),
                             d3[g][a:a + 128 * n, :].rearrange("(t p) d -> p t d", p=128),
                             q3in[2 * g].all(), q3in[2 * g + 1].all(), rm)
                return i, raw, q3x[i].all()

            def turn(q, i, raw, rm):
                n = quads[q][1]
                k, m1 = yield from banks.get()
                for t in range(n):
                    f = (lambda e, t=t: e.transpose(PS[:, k, 128 * t:128 * t + 128], raw[:, 128 * t:128 * t + 128], ident[:, :]))
                    if t < n - 1:
                        pe.quiet(f, m1, rm)
                    else:
                        m = pe.do(f, m1, rm)
                raws.free(i, m)
                yield
                j, x, xm = xts.take()
                m = act.do(lambda e: e.activation(x[:, 0:128 * n], PS[:, k, 0:128 * n], ACT.Identity, bias=cols[:, 28:29],
                                                  scale=cols[:, 27:28]), m, xm)
                banks.free(k, m)
                xt[q] = (j, x, m)

            def up(i):
                q, t = i // 4, i % 4
                j, x, xm = xt[q]
                k, m1 = yield from banks.get()

                def go(e):
                    reg[i] = e.value_load(ints3[0:1, 16 * g + i:16 * g + i + 1], min_val=0, max_val=7)
                    return e.matmul(PS[:, k, :], x[:, 128 * t:128 * t + 128], RA[:, bass.ds(reg[i] * 512, 512)], start=True, stop=True,
                                    skip_group_check=True)

                m = pe.do(go, m1, xm, rdy)
                if t == quads[q][1] - 1:
                    xts.free(j, m)
                s, P, pm = pt.take()
                if i % 2:
                    m = dve.do(lambda e: e.tensor_copy(P, PS[:, k, :]), m, pm)
                else:
                    m = act.do(lambda e: e.activation(P, PS[:, k, :], ACT.Copy), m, pm)
                banks.free(k, m)
                yield
                return s, P, m

            def middle(i, s, P, pm):
                k, m1 = yield from banks.get()
                for c in range(4):
                    f = (lambda e, c=c, P=P: e.transpose(PS[:, k, 128 * c:128 * c + 128], P[:, 128 * c:128 * c + 128], ident[:, :]))
                    if c < 3:
                        pe.quiet(f, m1, pm)
                    else:
                        m = pe.do(f)
                pt.free(s, m)
                s, P, pm = pt.take()
                for c in range(4):
                    o, a, bb = P[:, 128 * c:128 * c + 128], PS[:, k, 128 * c:128 * c + 128], BS[g][:, 4 * i + c:4 * i + c + 1]
                    if i % 2:
                        m2 = act.do(lambda e, o=o, a=a, bb=bb: e.activation(o, a, ACT.Relu, bias=bb, scale=1.0), m, pm, x3["bias", g])
                    else:
                        m2 = dve.do(lambda e, o=o, a=a, bb=bb: e.tensor_scalar(o, a, bb, 0.0, ALU.add, ALU.max), m, pm, x3["bias", g])
                banks.free(k, m2)
                yield
                return s, P, m2

            def down(i, s, P, pm):
                q, t = i // 4, i % 4
                if t == 0:
                    outs[q] = yield from banks.get()
                k, m1 = outs[q]
                for c in range(4):
                    def f(e, c=c):
                        return e.matmul(PS[:, k, 128 * t:128 * t + 128], P[:, 128 * c:128 * c + 128],
                                        RA[:, bass.ds(reg[i] * 512 + (4096 + 128 * c), 128)], start=c == 0, stop=c == 3, skip_group_check=True)
                    if c < 3:
                        pe.quiet(f, m1, pm)
                    else:
                        m = pe.do(f)
                pt.free(s, m)
                yield
                a, n = quads[q]
                if t == n - 1:
                    s, O, om = pt.take()
                    if q % 2:
                        m = dve.do(lambda e: e.tensor_copy(O[:, 0:128 * n], PS[:, k, 0:128 * n]), m, om)
                    else:
                        m = act.do(lambda e: e.activation(O[:, 0:128 * n], PS[:, k, 0:128 * n], ACT.Copy), m, om)
                    banks.free(k, m)
                    qo = q3o[g][q]
                    qo.start(sp, o3[g][a:a + 128 * n, :].rearrange("(t p) d -> p t d", p=128),
                             O[:, 0:128 * n].rearrange("p (t d) -> p t d", t=n), m)
                    outs_pend.append((s, qo.all()))
                    if len(outs_pend) > 1:
                        pt.free(outs_pend[0][0], outs_pend[0][1])
                        outs_pend.pop(0)

            outs_pend = []
            raw = fetch(0)
            yield from turn(0, *raw)
            nxt = fetch(1)
            ups, mids = {}, {}
            for i in range(NT + 2):
                if i < NT:
                    ups[i] = yield from up(i)
                if i % 4 == 1 and i // 4 + 1 < len(quads):
                    yield from turn(i // 4 + 1, *nxt)
                    if i // 4 + 2 < len(quads):
                        nxt = fetch(i // 4 + 2)
                if 0 <= i - 1 < NT:
                    mids[i - 1] = yield from middle(i - 1, *ups.pop(i - 1))
                if 0 <= i - 2:
                    yield from down(i - 2, *mids.pop(i - 2))
            pt.free(outs_pend[0][0], outs_pend[0][1])
            x3["free"] = [(pe.sem, pe.n)]

        def gather3(b):
            for t in range(4):
                q3g[b].gather(pool, G3[b][:, 128 * t:128 * t + 128], o3[b // 2], ints3[:, 32 + 4 * b + t:33 + 4 * b + t], 128 * NT - 1,
                              x3["g", b], [q.all() for q in q3o[b // 2]], x3["slot", b])
            yield
            yield
            m = dve.do(lambda e: e.tensor_tensor(Xb[b], Xb[b], G3[b], ALU.add), q3g[b].all(), xw[b])
            xw[b] = [m]
            emit_out(b)
            yield

        w1g = RA[:, 0:4096].rearrange("p (e n) -> p e n", e=8)
        w2g = RA[:, 4096:8192].rearrange("p (e c n) -> p e c n", e=8, c=4)

        def play_units(us, between={}, beside={}, ahead=None, state=None, tail=None, end=()):
            done = state is not None
            if ahead is None:
                ahead = alone_(us[0][0](0))
            pend = us[0][2](0, state) if done else None
            for i, (_, front, back, name) in list(enumerate(us))[done:]:
                par = i % 2
                f = (front(par, ahead), FRONT[name[:3]])
                n = (us[i + 1][0](1 - par), 6) if i + 1 < len(us) else (iter(()), 1)
                p = (pend, BACK[us[i - 1][3][:3]], 0.2) if pend else (iter(()), 1)
                t = (tail, 36) if tail else (iter(()), 1)
                state, tail, ahead, *_ = together(f, p, n, t, *(beside[name]() if name in beside else ()))
                if name in between:
                    between[name]()
                pend = back(par, state)
            t = (tail, 36) if tail else (iter(()), 1)
            tail, _, *more = together((pend, BACK[us[-1][3][:3]], 0.2), t, *(f() for f in end))
            return tail, more

        FRONT = {"l0x": 40, "l0f": 27, "l1x": 32, "l2x": 3, "l2f": 6, "l3x": 32}
        BACK = {"l0x": 34, "l0f": 27, "l1x": 34, "l2x": 3, "l2f": 5, "l3x": 34}

        def after_l0x():
            m = (pe.sem, pe.n)
            load("l1f", w1e, A["l1_w1"].rearrange("e p n -> p e n"), m)
            load("l1f", w2e, A["l1_w2"].rearrange("e (c p) n -> p e c n", p=128), m)
            load("l2w", S2[:, :], A["l2_w"], m)

        def after_l0y():
            load("l3x", w3, A["l3x_w"], (pe.sem, pe.n))

        def mid_l0f():
            yield from prepare(a1, w1v[:, 768:896], bias[0:NK, 128 * 5:128 * 6])

        def after_l0f():
            m = (pe.sem, pe.n)
            load("l3f", w1g, A["l3_w1"].rearrange("e p n -> p e n"), m)
            load("l3f", w2g, A["l3_w2"].rearrange("e (c p) n -> p e c n", p=128), m)

        def after_l1x():
            load("l1b", b2r, A["l1_b2r"], (pe.sem, pe.n))

        def before_l3x():
            l3x_masks()
            a3.ready = [loads["l3x"].all()]
            yield from prepare(a3, w3[:, 768:896], None)

        _, ahead = together((prepare(a0, wv0, bv0), 36), (units[0][0](0), 5))
        oc_free = [(dve.sem, dve.n)]
        tail, _ = play_units(units, {"l0f0": after_l0x, "l0f1": after_l0y, "l1x0": after_l0f},
                             {"l0f2": lambda: [(mid_l0f(), 24)], "l1x2": lambda: [(route(0), 20, 0.4)],
                              "l1x3": lambda: [(route(1), 20, 0.4)]}, ahead, end=[lambda: (route(2), 20, 0.4)])
        alone_(tail)
        after_l1x()
        alone_(route(3))
        alone_(capacity_experts())
        load("l3s", w4, A["l3s_w"], (dve.sem, dve.n))
        gather(0)
        gather(1)
        ahead, _, _ = together((units2[0][0](0), 6), (l2_prepare(), 6), (before_l3x(), 12))
        a4.ready = [loads["l3s"].all()]

        def after_l2():
            k4["rb_free"] = [(pe.sem, pe.n)]
            load("c3", C3[:, 0:368], A["c_3"], k4["rb_free"])
            l3_self_open(k4["rb_free"])

        tail, (norms,) = play_units(units2, {"l3x1": after_l2}, ahead=ahead, end=[lambda: (self_norms(0, 0), 20)])
        for i in range(3):
            kslots.free(i, [(pe.sem, pe.n)])
        x3["open"] = [(pe.sem, pe.n), (dve.sem, dve.n)]
        fin = Loads(sem("fin"))

        def emit_out(b):
            fin.start(sp, out[b].rearrange("(t p) d -> p t d", p=128), Xb[b].rearrange("p (t d) -> p t d", t=4), xw[b])

        m = dve.do(lambda e: e.memset(P3[0][:, 0:8], 0.0), x3["open"])
        m2 = dve.do(lambda e: e.memset(P3[1][:, 0:8], 0.0), x3["open"])
        x3["p"] = [m, m2]
        tail = self_attention(norms, tail)

        def last_route():
            yield from tail
            yield from route3(3)
            yield from place3(1)

        together((experts3(0), 60), (last_route(), 75))
        together((experts3(1), 60), (by_turns(gather3(0), gather3(1)), 12, 0.4))
        alone_(by_turns(gather3(2), gather3(3)))
        sp.wait(fin.all())

        block = ctx.enter_context(nc.Block())
        block.sync(sp.play)
        block.gpsimd(pool.play)
        block.scalar(act.play)
        block.vector(dve.play)
        block.tensor(pe.play)


def kernel(**inputs):
    import numpy as _np
    import concourse.bacc as _bacc
    from concourse import mybir as _mybir
    from concourse.bass_utils import run_bass_kernel_spmd as _run

    I = {k: _np.asarray(v) for k, v in inputs.items()}

    def rep(w):
        return _np.tile(w.reshape(128, 4, 1, 32), (1, 1, 3, 1)).reshape(128, 384)

    def repb(b):
        return _np.tile(b.reshape(4, 32).T, (4, 1))

    rows = lambda v: _np.broadcast_to(v.reshape(1, -1), (128, v.size))
    r = _np.arange(RK)[:, None]
    h = _np.arange(NH)[None, :]

    def mask(hd, hpg):
        return _np.where(r < RM, (r % 32) // hd == h % hpg, r - RM == h).astype(_np.float32)

    msk = _np.zeros((128, 32), _np.float32)
    msk[:RK, 0:16], msk[:RK, 16:32] = mask(8, 4), mask(16, 2)
    block = _np.zeros((16, 8, 16, 2, 8), _np.float32)
    for i in range(16):
        block[i, :, i, 0, :], block[i, :, i, 1, :] = 1.0, -1.0
    sign = _np.repeat(_np.tile(_np.array([1.0, -1.0], _np.float32), 128), 8)
    C = {
        "x": I["x"], "ctxT": _np.pad(I["ctx_1024"].transpose(2, 0, 1), ((0, 0), (0, 0), (0, 1))).reshape(128, CK),
        "c_ident": _np.eye(128, dtype=_np.float32), "c_mask": msk,
        "l0_pack": _np.concatenate([_np.tile(I["L0_xattn_fm_w"].T, (16, 1)), block.reshape(128, 256),
                                    I["L0_xattn_fc_w"].T.reshape(2, 128, 128).transpose(1, 0, 2).reshape(128, 256)], 1),
        "c_tri": _np.triu(_np.ones((128, 128), _np.float32)),
        "c_off": _np.tile(_np.arange(8).astype(_np.float32) * CAP - 1.0, (128, 4)),
        "c_3": _np.tile(_np.concatenate([_np.tile(_np.arange(8) * 128, 8), _np.tril(_np.ones((8, 8)), -1).ravel(),
                                         _np.repeat(_np.arange(NT), 8), _np.tile(_np.arange(8), NT)]).astype(_np.float32), (128, 1)),
        "l1_b2r": rows(I["L1_ffn_b2"]),
        "c_rev": _np.tile(_np.arange(8, 0, -1).astype(_np.float32), (128, 4)),
        "fm_b": _np.stack([_np.tile(I["L0_xattn_fm_b"], 12), sign[:96]], 1),
        "fm_br": _np.concatenate([_np.tile(I["L0_xattn_fm_b"], (NK, 32)), _np.tile(sign[:256], (NK, 1))], 1),
        "gates": _np.stack([I["L0_ffn_Wg"], I["L1_ffn_gate_w"].T, I["L3_ffn_gate_w"]]),
        "gateb": _np.concatenate([rows(I["L1_ffn_gate_b"]), rows(I["L3_ffn_gate_b"])], 1),
        "rows": _np.stack([rows(I[n]) for n in ("L0_xattn_fc_b", "L1_xattn_bo", "L2_ffn_b2", "L3_xattn_bproj", "L3_ffn_bo",
                                                "L1_xattn_bv", "L2_xattn_bias_v", "L3_ffn_bv")]),
        "colb": _np.concatenate([
            repb(I["L1_xattn_bq"]), repb(I["L1_xattn_bk"]), I["L2_xattn_bias_q"][:, None], I["L2_xattn_bias_k"][:, None],
            rows(I["L2_ffn_scale"].reshape(1)), I["L2_ffn_b1"].reshape(4, 128).T, repb(I["L3_ffn_bq"]), repb(I["L3_ffn_bk"]),
            I["L3_ffn_ln1_g"][:, None], I["L3_ffn_ln1_b"][:, None], I["L3_ffn_ln2_g"][:, None], I["L3_ffn_ln2_b"][:, None],
            _np.zeros((128, 11), _np.float32)], 1),
        "l0_w13": _np.concatenate([_np.concatenate([I["L0_ffn_We1"], I["L0_ffn_Ws1"][None]]),
                                   _np.concatenate([I["L0_ffn_We3"], I["L0_ffn_Ws3"][None]])], 2),
        "l0_w2": _np.concatenate([I["L0_ffn_We2"], I["L0_ffn_Ws2"][None]]),
        "l1_w": _np.concatenate([rep(I["L1_xattn_Wq"].T), rep(I["L1_xattn_Wk"].T), I["L1_xattn_Wv"].T, I["L1_xattn_Wo"].T], 1),
        "l1_w1": I["L1_ffn_w1"], "l1_w2": I["L1_ffn_w2"],
        "b1": _np.concatenate([I["L1_ffn_b1"].reshape(32, 128).T, I["L3_ffn_b1"].reshape(32, 128).T], 1),
        "b2": _np.concatenate([I["L1_ffn_b2"], I["L3_ffn_b2"]], 1),
        "l2_w": _np.concatenate([I["L2_xattn_kernel_q"][0, 0], I["L2_xattn_kernel_k"][0, 0], I["L2_xattn_kernel_v"][0, 0],
                                 I["L2_ffn_W1"].T, I["L2_ffn_W2"].T.reshape(4, 128, 128).transpose(1, 0, 2).reshape(128, 512)], 1),
        "mfT": I["mask_1xSxS2_ff0"][0].T, "mbT": I["mask_BxSxS2_bk0"].transpose(2, 0, 1).reshape(NK, 2048),
        "l3x_w": _np.concatenate([rep(I["L3_xattn_Wq"]), rep(I["L3_xattn_Wkv"][:, 0:128]), I["L3_xattn_Wkv"][:, 128:256],
                                  I["L3_xattn_Wproj"]], 1),
        "l3s_w": _np.concatenate([rep(I["L3_ffn_wq"]), rep(I["L3_ffn_wk"]), I["L3_ffn_wv"], I["L3_ffn_wo"]], 1),
        "l3_w1": I["L3_ffn_w1"], "l3_w2": I["L3_ffn_w2"],
    }
    nc = _bacc.Bacc("TRN2", target_bir_lowering=False, num_devices=1)
    arrays, aps = {}, {}
    for name, a in C.items():
        a = _np.ascontiguousarray(a)
        arrays["in_" + name] = a
        aps[name] = nc.dram_tensor("in_" + name, a.shape, _mybir.dt.from_np(a.dtype), kind="ExternalInput").ap()
    o = nc.dram_tensor("out_0", (4, 512, 128), _mybir.dt.float32, kind="ExternalOutput").ap()
    program(nc, aps, o)
    res = _run(nc, [arrays], core_ids=[0])
    return res.results[0]["out_0"]
```
